# Optimizing a Trainium2 kernel written in Bass

```python
import numpy as np
import jax
import jax.numpy as jnp

def _softmax(x, axis=-1):
    return jax.nn.softmax(x, axis=axis)

def _gelu(x):
    return jax.nn.gelu(x, approximate=True)

def _silu(x):
    return jax.nn.silu(x)

def _sigmoid(x):
    return jax.nn.sigmoid(x)

def _layernorm(x, axis=-1, eps=1e-05):
    m = jnp.mean(x, axis=axis, keepdims=True)
    v = jnp.var(x, axis=axis, keepdims=True)
    return (x - m) / jnp.sqrt(v + eps)

def _scatter_add(tgt, idx, src, axis=0):
    return tgt.at[idx].add(src)

def _segment_sum(src, seg, n):
    return jax.ops.segment_sum(src, seg, n)
kernel_name = 'mk_decoder_preln_d2_seqx_r4_9f22e9'

def setup_inputs(seed: int=0):
    np.random.seed(seed)
    _w = jnp.asarray

    def _rec_inputs():
        import jax
        import jax.numpy as jnp
        _rk = jax.random.key(seed)
        x = 0.002226 + 0.9996 * jax.random.normal(jax.random.fold_in(_rk, 1), (16, 112, 256), jnp.float32)
        _lenS = 112 - jax.random.randint(jax.random.fold_in(_rk, 7), (16,), 0, max(1, 112 // 4) + 1, jnp.int32)
        _lenS2 = 375 - jax.random.randint(jax.random.fold_in(_rk, 8), (16,), 0, max(1, 375 // 4) + 1, jnp.int32)
        _ctx_1024P = jax.random.normal(jax.random.fold_in(_rk, 11), (16, 16, 256), jnp.float32)
        _ctx_1024c = jax.random.dirichlet(jax.random.fold_in(_rk, 511), 0.3 * jnp.ones((16,), jnp.float32), (16, 375))
        _ctx_1024t = jnp.einsum('bsk,bkd->bsd', _ctx_1024c, _ctx_1024P)
        _ctx_1024t = _ctx_1024t * jax.lax.rsqrt(jnp.mean(jnp.square(_ctx_1024t)) + 1e-12) * 0.953939
        ctx_1024 = -0.000125008 + 0.999885 * (_ctx_1024t + 0.3 * jax.random.normal(jax.random.fold_in(_rk, 611), (16, 375, 256), jnp.float32))
        _validS = jnp.arange(112)[None, :] < _lenS[:, None]
        _validS2 = jnp.arange(375)[None, :] < _lenS2[:, None]
        _causal = jnp.tril(jnp.ones((112, 112), dtype=bool))
        mask_BxS2_bk0 = jnp.logical_not(jnp.broadcast_to(_validS2[:, :], (16, 375)))
        mask_Bx1xSxS2_bf0 = jnp.logical_not(jnp.ones((16, 1, 112, 375), dtype=bool))
        return (x, ctx_1024, mask_BxS2_bk0, mask_Bx1xSxS2_bf0)
    x, ctx_1024, mask_BxS2_bk0, mask_Bx1xSxS2_bf0 = _rec_inputs()

    def _L0_attn_setup():
        import jax, jax.numpy as jnp
        import numpy as np
        B, T, E = (4, 512, 256)
        H, D = (8, 128)

        def sinusoidal_pe(length, dim, dtype=jnp.float32):
            pos = jnp.arange(length, dtype=jnp.float32)[:, None]
            inv_freq = jnp.exp(-jnp.log(jnp.float32(10000.0)) * (jnp.arange(0, dim, 2, dtype=jnp.float32) / dim))
            ang = pos * inv_freq[None, :]
            pe = jnp.zeros((length, dim), dtype=jnp.float32)
            pe = pe.at[:, 0::2].set(jnp.sin(ang)).at[:, 1::2].set(jnp.cos(ang))
            return pe.astype(dtype)
        key = jax.random.key(seed)
        kx, kq, kk, kv, ko = jax.random.split(key, 5)
        s = 0.02
        return {'x': jax.random.normal(kx, (B, T, E), dtype=jnp.float32), 'Wq': jax.random.normal(kq, (H * D, E), dtype=jnp.float32) * s, 'Wk': jax.random.normal(kk, (D, E), dtype=jnp.float32) * s, 'Wv': jax.random.normal(kv, (D, E), dtype=jnp.float32) * s, 'Wo': jax.random.normal(ko, (E, H * D), dtype=jnp.float32) * s}
    _L0_attn_all = _L0_attn_setup()
    _L0_attn_in = {k: v for k, v in _L0_attn_all.items() if k in ('Wq', 'Wk', 'Wv', 'Wo')}
    del _L0_attn_all

    def _L0_xattn_setup():
        import jax, jax.numpy as jnp
        import numpy as np
        EPS = 1e-05

        def layer_norm(x, g, b):
            mu = jnp.mean(x, axis=-1, keepdims=True)
            var = jnp.mean((x - mu) ** 2, axis=-1, keepdims=True)
            return (x - mu) * jax.lax.rsqrt(var + EPS) * g + b
        key = jax.random.key(seed)
        ks = jax.random.split(key, 8)
        b, n, l, D = (8, 1024, 64, 256)
        heads, dim_head = (16, 64)
        inner = heads * dim_head
        x = jax.random.normal(ks[0], (b, n, D), dtype=jnp.float32)
        latents = jax.random.normal(ks[1], (b, l, D), dtype=jnp.float32)
        mask = jax.random.randint(ks[2], (b, n), 0, 2) > 0
        Wq = jax.random.normal(ks[3], (D, inner), dtype=jnp.float32) * D ** (-0.5)
        Wkv = jax.random.normal(ks[4], (D, 2 * inner), dtype=jnp.float32) * D ** (-0.5)
        Wout = jax.random.normal(ks[5], (inner, D), dtype=jnp.float32) * inner ** (-0.5)
        g1 = jnp.ones((D,), jnp.float32)
        b1 = jnp.zeros((D,), jnp.float32)
        g2 = jnp.ones((D,), jnp.float32)
        b2 = jnp.zeros((D,), jnp.float32)
        return {'x': x, 'latents': latents, 'mask': mask, 'g1': g1, 'b1': b1, 'g2': g2, 'b2': b2, 'Wq': Wq, 'Wkv': Wkv, 'Wout': Wout}
    _L0_xattn_all = _L0_xattn_setup()
    _L0_xattn_in = {k: v for k, v in _L0_xattn_all.items() if k in ('g1', 'b1', 'g2', 'b2', 'Wq', 'Wkv', 'Wout')}
    del _L0_xattn_all

    def _L0_ffn_setup():
        import jax, jax.numpy as jnp
        import numpy as np
        LN_EPS = 1e-12
        key = jax.random.key(seed)
        ks = jax.random.split(key, 8)
        B, S, H, I, E = (4, 512, 256, 1024, 8)
        sH = 1.0 / np.sqrt(H)
        sI = 1.0 / np.sqrt(I)
        return {'hidden_states': jax.random.normal(ks[0], (B, S, H), dtype=jnp.float32), 'Wr': jax.random.uniform(ks[1], (E, H), jnp.float32, -sH, sH), 'W1': jax.random.uniform(ks[2], (E, H, I), jnp.float32, -sH, sH), 'b1': jax.random.uniform(ks[3], (E, I), jnp.float32, -sH, sH), 'Wo': jax.random.uniform(ks[4], (I, H), jnp.float32, -sI, sI), 'bo': jax.random.uniform(ks[5], (H,), jnp.float32, -sI, sI), 'gamma': jnp.ones((H,), jnp.float32), 'beta': jnp.zeros((H,), jnp.float32)}
    _L0_ffn_all = _L0_ffn_setup()
    _L0_ffn_in = {k: v for k, v in _L0_ffn_all.items() if k in ('Wr', 'W1', 'b1', 'Wo', 'bo', 'gamma', 'beta')}
    del _L0_ffn_all

    def _L1_attn_setup():
        import jax, jax.numpy as jnp
        import numpy as np
        HEADS = 16
        DIM_HEAD = 64
        SCALE = DIM_HEAD ** (-0.5)
        EPS = 1e-05

        def layer_norm(x, gamma):
            mu = jnp.mean(x, axis=-1, keepdims=True)
            var = jnp.var(x, axis=-1, keepdims=True)
            return (x - mu) * jax.lax.rsqrt(var + EPS) * gamma
        key = jax.random.key(seed)
        ks = jax.random.split(key, 5)
        B, S, D = (2, 512, 256)
        x = jax.random.normal(ks[0], (B, S, D), dtype=jnp.float32)
        gamma = jnp.ones((D,), dtype=jnp.float32)
        Wq = jax.random.normal(ks[1], (D, HEADS * DIM_HEAD), dtype=jnp.float32) * D ** (-0.5)
        Wkv = jax.random.normal(ks[2], (D, 2 * DIM_HEAD), dtype=jnp.float32) * D ** (-0.5)
        Wo = jax.random.normal(ks[3], (HEADS * DIM_HEAD, D), dtype=jnp.float32) * (HEADS * DIM_HEAD) ** (-0.5)
        return {'x': x, 'gamma': gamma, 'Wq': Wq, 'Wkv': Wkv, 'Wo': Wo}
    _L1_attn_all = _L1_attn_setup()
    _L1_attn_in = {k: v for k, v in _L1_attn_all.items() if k in ('gamma', 'Wq', 'Wkv', 'Wo')}
    del _L1_attn_all

    def _L1_xattn_setup():
        import jax, jax.numpy as jnp
        import numpy as np
        B, S, D, H = (2, 512, 256, 16)
        HD = D // H
        LN_EPS = 1e-05

        def _linear(x, w, b):
            return jnp.einsum('bsd,od->bso', x, w) + b

        def _split_heads(x):
            b, s, _ = x.shape
            return x.reshape(b, s, H, HD).transpose(0, 2, 1, 3)
        key = jax.random.key(seed)
        ks = jax.random.split(key, 14)
        w = 0.02
        return {'q': jax.random.normal(ks[0], (B, S, D), jnp.float32), 'k': jax.random.normal(ks[1], (B, S, D), jnp.float32), 'v': jax.random.normal(ks[2], (B, S, D), jnp.float32), 'mask': jnp.zeros((B, 1, S, S), dtype=bool), 'training': 0, 'wq_w': jax.random.normal(ks[3], (D, D), jnp.float32) * w, 'wq_b': jnp.zeros((D,), jnp.float32), 'wk_w': jax.random.normal(ks[4], (D, D), jnp.float32) * w, 'wk_b': jnp.zeros((D,), jnp.float32), 'wv_w': jax.random.normal(ks[5], (D, D), jnp.float32) * w, 'wv_b': jnp.zeros((D,), jnp.float32), 'wo_w': jax.random.normal(ks[6], (D, D), jnp.float32) * w, 'wo_b': jnp.zeros((D,), jnp.float32), 'ln_g': jnp.ones((D,), jnp.float32), 'ln_b': jnp.zeros((D,), jnp.float32)}
    _L1_xattn_all = _L1_xattn_setup()
    _L1_xattn_in = {k: v for k, v in _L1_xattn_all.items() if k in ('wq_w', 'wq_b', 'wk_w', 'wk_b', 'wv_w', 'wv_b', 'wo_w', 'wo_b', 'ln_g', 'ln_b')}
    del _L1_xattn_all

    def _L1_ffn_setup():
        import jax, jax.numpy as jnp
        import numpy as np
        TOP_K = 2
        key = jax.random.key(seed)
        ks = jax.random.split(key, 7)
        B_, S, D, F, E, R = (2, 512, 256, 1024, 4, 4)
        x = jax.random.normal(ks[0], (B_, S, D), dtype=jnp.float32)
        Wg = jax.random.normal(ks[1], (E, D), dtype=jnp.float32) * (1.0 / np.sqrt(D))
        bg = jnp.zeros((E,), dtype=jnp.float32)
        Wi = jax.random.normal(ks[2], (F, D), dtype=jnp.float32) * (1.0 / np.sqrt(D))
        Wo = jax.random.normal(ks[3], (D, F), dtype=jnp.float32) * (1.0 / np.sqrt(F))
        A = jax.random.normal(ks[4], (E, R, D), dtype=jnp.float32) * (1.0 / np.sqrt(D))
        Bm = jax.random.normal(ks[5], (E, F, R), dtype=jnp.float32) * 0.01
        return {'x': x, 'Wg': Wg, 'bg': bg, 'Wi': Wi, 'Wo': Wo, 'A': A, 'B': Bm}
    _L1_ffn_all = _L1_ffn_setup()
    _L1_ffn_in = {k: v for k, v in _L1_ffn_all.items() if k in ('Wg', 'bg', 'Wi', 'Wo', 'A', 'B')}
    del _L1_ffn_all
    return {'x': x, 'ctx_1024': ctx_1024, 'mask_BxS2_bk0': mask_BxS2_bk0, 'mask_Bx1xSxS2_bf0': mask_Bx1xSxS2_bf0, 'L0_attn_Wq': _L0_attn_in['Wq'], 'L0_attn_Wk': _L0_attn_in['Wk'], 'L0_attn_Wv': _L0_attn_in['Wv'], 'L0_attn_Wo': _L0_attn_in['Wo'], 'L0_xattn_g1': _L0_xattn_in['g1'], 'L0_xattn_b1': _L0_xattn_in['b1'], 'L0_xattn_g2': _L0_xattn_in['g2'], 'L0_xattn_b2': _L0_xattn_in['b2'], 'L0_xattn_Wq': _L0_xattn_in['Wq'], 'L0_xattn_Wkv': _L0_xattn_in['Wkv'], 'L0_xattn_Wout': _L0_xattn_in['Wout'], 'L0_ffn_Wr': _L0_ffn_in['Wr'], 'L0_ffn_W1': _L0_ffn_in['W1'], 'L0_ffn_b1': _L0_ffn_in['b1'], 'L0_ffn_Wo': _L0_ffn_in['Wo'], 'L0_ffn_bo': _L0_ffn_in['bo'], 'L0_ffn_gamma': _L0_ffn_in['gamma'], 'L0_ffn_beta': _L0_ffn_in['beta'], 'L1_attn_gamma': _L1_attn_in['gamma'], 'L1_attn_Wq': _L1_attn_in['Wq'], 'L1_attn_Wkv': _L1_attn_in['Wkv'], 'L1_attn_Wo': _L1_attn_in['Wo'], 'L1_xattn_wq_w': _L1_xattn_in['wq_w'], 'L1_xattn_wq_b': _L1_xattn_in['wq_b'], 'L1_xattn_wk_w': _L1_xattn_in['wk_w'], 'L1_xattn_wk_b': _L1_xattn_in['wk_b'], 'L1_xattn_wv_w': _L1_xattn_in['wv_w'], 'L1_xattn_wv_b': _L1_xattn_in['wv_b'], 'L1_xattn_wo_w': _L1_xattn_in['wo_w'], 'L1_xattn_wo_b': _L1_xattn_in['wo_b'], 'L1_xattn_ln_g': _L1_xattn_in['ln_g'], 'L1_xattn_ln_b': _L1_xattn_in['ln_b'], 'L1_ffn_Wg': _L1_ffn_in['Wg'], 'L1_ffn_bg': _L1_ffn_in['bg'], 'L1_ffn_Wi': _L1_ffn_in['Wi'], 'L1_ffn_Wo': _L1_ffn_in['Wo'], 'L1_ffn_A': _L1_ffn_in['A'], 'L1_ffn_B': _L1_ffn_in['B']}

def reference(x, ctx_1024, mask_BxS2_bk0, mask_Bx1xSxS2_bf0, L0_attn_Wq, L0_attn_Wk, L0_attn_Wv, L0_attn_Wo, L0_xattn_g1, L0_xattn_b1, L0_xattn_g2, L0_xattn_b2, L0_xattn_Wq, L0_xattn_Wkv, L0_xattn_Wout, L0_ffn_Wr, L0_ffn_W1, L0_ffn_b1, L0_ffn_Wo, L0_ffn_bo, L0_ffn_gamma, L0_ffn_beta, L1_attn_gamma, L1_attn_Wq, L1_attn_Wkv, L1_attn_Wo, L1_xattn_wq_w, L1_xattn_wq_b, L1_xattn_wk_w, L1_xattn_wk_b, L1_xattn_wv_w, L1_xattn_wv_b, L1_xattn_wo_w, L1_xattn_wo_b, L1_xattn_ln_g, L1_xattn_ln_b, L1_ffn_Wg, L1_ffn_bg, L1_ffn_Wi, L1_ffn_Wo, L1_ffn_A, L1_ffn_B):
    import jax
    import jax.numpy as jnp

    def _L0_attn_ref(x, Wq, Wk, Wv, Wo):
        import jax, jax.numpy as jnp
        import numpy as np
        B, T, E = (4, 512, 256)
        H, D = (8, 128)

        def sinusoidal_pe(length, dim, dtype=jnp.float32):
            pos = jnp.arange(length, dtype=jnp.float32)[:, None]
            inv_freq = jnp.exp(-jnp.log(jnp.float32(10000.0)) * (jnp.arange(0, dim, 2, dtype=jnp.float32) / dim))
            ang = pos * inv_freq[None, :]
            pe = jnp.zeros((length, dim), dtype=jnp.float32)
            pe = pe.at[:, 0::2].set(jnp.sin(ang)).at[:, 1::2].set(jnp.cos(ang))
            return pe.astype(dtype)
        Bv, Tv, Ev = x.shape
        scale = 1.0 / jnp.sqrt(jnp.float32(D)).astype(x.dtype)
        q = (x @ Wq.T).reshape(Bv, Tv, H, D)
        k = (x @ Wk.T).reshape(Bv, Tv, 1, D)
        v = (x @ Wv.T).reshape(Bv, Tv, 1, D)
        k = k + sinusoidal_pe(1, D, k.dtype)
        q = jnp.transpose(q, (0, 2, 1, 3))
        k1 = k[:, :, 0, :]
        v1 = v[:, :, 0, :]
        q = q + sinusoidal_pe(Tv, D, q.dtype)[None, None]
        scores = jnp.einsum('bhtd,bsd->bhts', q, k1) * scale
        causal = jnp.tril(jnp.ones((Tv, Tv), dtype=bool))
        scores = jnp.where(causal[None, None], scores, jnp.finfo(scores.dtype).min)
        probs = jax.nn.softmax(scores, axis=-1)
        attn = jnp.einsum('bhts,bsd->bhtd', probs, v1)
        out = jnp.transpose(attn, (0, 2, 1, 3)).reshape(Bv, Tv, H * D)
        return out @ Wo.T

    def _L0_xattn_ref(x, latents, mask, g1, b1, g2, b2, Wq, Wkv, Wout):
        import jax, jax.numpy as jnp
        import numpy as np
        EPS = 1e-05

        def layer_norm(x, g, b):
            mu = jnp.mean(x, axis=-1, keepdims=True)
            var = jnp.mean((x - mu) ** 2, axis=-1, keepdims=True)
            return (x - mu) * jax.lax.rsqrt(var + EPS) * g + b
        heads, dim_head = (16, 64)
        b, n, D = x.shape
        l = latents.shape[1]
        xn = layer_norm(x, g1, b1)
        ln_lat = layer_norm(latents, g2, b2)
        q = ln_lat @ Wq
        kv = jnp.concatenate([xn, ln_lat], axis=1) @ Wkv
        k, v = jnp.split(kv, 2, axis=-1)

        def to_heads(t):
            return t.reshape(t.shape[0], t.shape[1], heads, dim_head).transpose(0, 2, 1, 3)
        q, k, v = (to_heads(q), to_heads(k), to_heads(v))
        scale = 1.0 / np.sqrt(np.sqrt(dim_head)).astype(np.float32)
        weight = jnp.einsum('bhld,bhnd->bhln', q * scale, k * scale)
        full_mask = jnp.concatenate([mask, jnp.ones((b, l), dtype=bool)], axis=1)
        neg = -jnp.finfo(weight.dtype).max
        weight = jnp.where(full_mask[:, None, None, :], weight, neg)
        weight = jax.nn.softmax(weight.astype(jnp.float32), axis=-1).astype(q.dtype)
        out = jnp.einsum('bhln,bhnd->bhld', weight, v)
        out = out.transpose(0, 2, 1, 3).reshape(b, l, heads * dim_head)
        return out @ Wout

    def _L0_ffn_ref(hidden_states, Wr, W1, b1, Wo, bo, gamma, beta):
        import jax, jax.numpy as jnp
        import numpy as np
        LN_EPS = 1e-12
        B, S, H = hidden_states.shape
        E = Wr.shape[0]
        x = hidden_states.reshape(-1, H)
        router_logits = x @ Wr.T
        expert_idx = jnp.argmax(jax.nn.softmax(router_logits, axis=-1), axis=-1)
        inter = jnp.zeros((x.shape[0], W1.shape[2]), dtype=x.dtype)
        for e in range(E):
            mask = (expert_idx == e)[:, None].astype(x.dtype)
            inter = inter + mask * jax.nn.gelu(x @ W1[e] + b1[e], approximate=False)
        y = inter @ Wo + bo + x
        mu = jnp.mean(y, axis=-1, keepdims=True)
        var = jnp.mean(jnp.square(y - mu), axis=-1, keepdims=True)
        out = (y - mu) * jax.lax.rsqrt(var + LN_EPS) * gamma + beta
        return out.reshape(B, S, H)

    def _L1_attn_ref(x, gamma, Wq, Wkv, Wo):
        import jax, jax.numpy as jnp
        import numpy as np
        HEADS = 16
        DIM_HEAD = 64
        SCALE = DIM_HEAD ** (-0.5)
        EPS = 1e-05

        def layer_norm(x, gamma):
            mu = jnp.mean(x, axis=-1, keepdims=True)
            var = jnp.var(x, axis=-1, keepdims=True)
            return (x - mu) * jax.lax.rsqrt(var + EPS) * gamma
        B, S, D = x.shape
        kv_input = x
        xn = layer_norm(x, gamma)
        q = xn @ Wq
        kv = kv_input @ Wkv
        k, v = jnp.split(kv, 2, axis=-1)
        q = q.reshape(B, S, HEADS, DIM_HEAD).transpose(0, 2, 1, 3) * SCALE
        sim = jnp.einsum('bhid,bjd->bhij', q, k)
        i_idx = jnp.arange(S)[:, None]
        j_idx = jnp.arange(S)[None, :]
        neg = -jnp.finfo(sim.dtype).max
        sim = jnp.where(j_idx > i_idx, neg, sim)
        attn = jax.nn.softmax(sim, axis=-1)
        out = jnp.einsum('bhij,bjd->bhid', attn, v)
        out = out.transpose(0, 2, 1, 3).reshape(B, S, HEADS * DIM_HEAD)
        return out @ Wo

    def _L1_xattn_ref(q, k, v, mask, training, wq_w, wq_b, wk_w, wk_b, wv_w, wv_b, wo_w, wo_b, ln_g, ln_b):
        import jax, jax.numpy as jnp
        import numpy as np
        B, S, D, H = (2, 512, 256, 16)
        HD = D // H
        LN_EPS = 1e-05

        def _linear(x, w, b):
            return jnp.einsum('bsd,od->bso', x, w) + b

        def _split_heads(x):
            b, s, _ = x.shape
            return x.reshape(b, s, H, HD).transpose(0, 2, 1, 3)
        residual = q
        Q = _split_heads(_linear(q, wq_w, wq_b))
        K = _split_heads(_linear(k, wk_w, wk_b))
        V = _split_heads(_linear(v, wv_w, wv_b))
        dk = jnp.sqrt(jnp.asarray(HD, jnp.float16)).astype(jnp.float32) + 1e-08
        score = jnp.einsum('bhqd,bhkd->bhqk', Q, K) / dk
        attn = jnp.where(mask, -jnp.inf, score)
        ctx = jnp.einsum('bhqk,bhkd->bhqd', attn, V)
        b, _, s, _ = ctx.shape
        ctx = ctx.transpose(0, 2, 1, 3).reshape(b, s, D)
        o = _linear(ctx, wo_w, wo_b)
        x = residual + o
        mu = jnp.mean(x, axis=-1, keepdims=True)
        var = jnp.mean(jnp.square(x - mu), axis=-1, keepdims=True)
        return ln_g * (x - mu) * jax.lax.rsqrt(var + LN_EPS) + ln_b

    def _L1_ffn_ref(x, Wg, bg, Wi, Wo, A, B):
        import jax, jax.numpy as jnp
        import numpy as np
        TOP_K = 2
        E = Wg.shape[0]
        logits = jnp.einsum('bsd,ed->bse', x, Wg) + bg
        scores = jax.nn.softmax(logits, axis=-1)
        topv, topi = jax.lax.top_k(scores, TOP_K)
        w = jnp.sum(jax.nn.one_hot(topi, E, dtype=x.dtype) * topv[..., None], axis=-2)
        base = jnp.einsum('bsd,fd->bsf', x, Wi)
        lora_low = jnp.einsum('bsd,erd->bser', x, A)
        lora = jnp.einsum('bser,efr->bsef', lora_low, B)
        h = jax.nn.relu(base[:, :, None, :] + lora)
        expert_out = jnp.einsum('bsef,df->bsed', h, Wo)
        out = jnp.einsum('bse,bsed->bsd', w, expert_out)
        return out
    x = x + _L0_attn_ref(_layernorm(x, axis=-1), L0_attn_Wq, L0_attn_Wk, L0_attn_Wv, L0_attn_Wo)
    x = x + _L0_xattn_ref(ctx_1024, _layernorm(x, axis=-1), mask_BxS2_bk0, L0_xattn_g1, L0_xattn_b1, L0_xattn_g2, L0_xattn_b2, L0_xattn_Wq, L0_xattn_Wkv, L0_xattn_Wout)
    x = x + _L0_ffn_ref(_layernorm(x, axis=-1), L0_ffn_Wr, L0_ffn_W1, L0_ffn_b1, L0_ffn_Wo, L0_ffn_bo, L0_ffn_gamma, L0_ffn_beta)
    x = x + _L1_attn_ref(_layernorm(x, axis=-1), L1_attn_gamma, L1_attn_Wq, L1_attn_Wkv, L1_attn_Wo)
    x = x + _L1_xattn_ref(_layernorm(x, axis=-1), ctx_1024, ctx_1024, mask_Bx1xSxS2_bf0, 0, L1_xattn_wq_w, L1_xattn_wq_b, L1_xattn_wk_w, L1_xattn_wk_b, L1_xattn_wv_w, L1_xattn_wv_b, L1_xattn_wo_w, L1_xattn_wo_b, L1_xattn_ln_g, L1_xattn_ln_b)
    x = x + _L1_ffn_ref(_layernorm(x, axis=-1), L1_ffn_Wg, L1_ffn_bg, L1_ffn_Wi, L1_ffn_Wo, L1_ffn_A, L1_ffn_B)
    return x

_drawn_inputs = setup_inputs


def setup_inputs(seed=0):
    import zlib

    import numpy as np

    out = dict(_drawn_inputs(seed))
    spreads = {'L0_xattn_g1': (1.0, 0.2),
     'L0_xattn_b1': (0.0, 0.1),
     'L0_xattn_g2': (1.0, 0.2),
     'L0_xattn_b2': (0.0, 0.1),
     'L0_ffn_gamma': (1.0, 0.2),
     'L0_ffn_beta': (0.0, 0.1),
     'L1_attn_gamma': (1.0, 0.6),
     'L1_xattn_wq_b': (0.0, 0.1),
     'L1_xattn_wk_b': (0.0, 0.1),
     'L1_xattn_wv_b': (0.0, 0.1),
     'L1_xattn_wo_b': (0.0, 0.381),
     'L1_xattn_ln_g': (1.0, 0.2),
     'L1_xattn_ln_b': (0.0, 0.1),
     'L1_ffn_bg': (0.0, 0.8)}
    factors = {'L0_attn_Wq': 7.657,
     'L0_attn_Wk': 4.511,
     'L0_ffn_b1': 8.0,
     'L0_ffn_bo': 5.519,
     'L1_ffn_A': 8.0,
     'L1_ffn_B': 8.0}
    for name, (base, spread) in spreads.items():
        noise = np.random.default_rng([zlib.crc32(name.encode()), seed]).standard_normal(out[name].shape)
        drawn = base * np.exp(spread * noise) if base else spread * noise
        out[name] = jnp.asarray(drawn.astype(out[name].dtype))
    for name, factor in factors.items():
        out[name] = (out[name] * factor).astype(out[name].dtype)
    return out
```

```python
from contextlib import ExitStack

import numpy as np

import concourse.bass as bass
from concourse import mybir

F32 = mybir.dt.float32
F32R = mybir.dt.float32r
U8 = mybir.dt.uint8
U32 = mybir.dt.uint32
ALU = mybir.AluOpType
ACT = mybir.ActivationFunctionType
AX = mybir.AxisListType

B, S, D, N = 16, 112, 256, 375
KC = D // 128
MASK_WORDS = -(-N // 4)
PAIR = 2 * S
NEG = -3.0e38
LN_EPS = 1e-5


def since(eng, sem, value):
    if isinstance(value, int) and value <= 0:
        return
    eng.wait_ge(sem, value)


def over_steps(eng, body, count):
    body(0, first=True, last=False)
    if count > 2:
        with eng.Fori(1, count - 1) as i:
            body(i, first=False, last=False)
    body(count - 1, first=False, last=True)


class Phase:

    def __init__(self, nc, ctx, name):
        self.nc, self.ctx, self.name = nc, ctx, name

    def sb(self, name, shape, dt=F32):
        return self.ctx.enter_context(self.nc.sbuf_tensor(f"{self.name}_{name}", shape, dt))

    def banks(self, name, n):
        return self.ctx.enter_context(self.nc.psum_tensor(f"{self.name}_{name}_ps", [128, n, 512], F32))

    def sem(self, name):
        return self.ctx.enter_context(self.nc.semaphore(f"{self.name}_{name}"))


def wait_apart(eng, sem, value, passed):
    since(eng, sem, value)
    eng.sem_inc(passed, 1)


def update_x(nc, dve, x, stats, x_new, x_stats, y, b, x_step):
    nc.vector.tensor_tensor(x_new[:], x[:, b, :], y, ALU.add).then_inc(x_step, 1)
    dve.wait_ge(x_step, b * 4 + 1)
    nc.vector.bn_stats(x_stats[:], x_new[:]).then_inc(x_step, 1)
    nc.vector.tensor_scalar(x[:, b, :], x_new[:], 1.0, None, ALU.mult).then_inc(x_step, 1)
    dve.wait_ge(x_step, b * 4 + 3)
    nc.vector.tensor_scalar(stats[:, b, :], x_stats[:], 1.0, None, ALU.mult).then_inc(x_step, 1)


def aggregate(nc, dve, stats, mv, mv_step):
    for b in range(B):
        nc.vector.bn_aggr(mv[:, b, :], stats[:, b, :]).then_inc(mv_step, 1)


def single_rstd(nc, pool, mv, half, rstd, mv_step, rstd_step):
    nc.gpsimd.memset(half[:], -0.5).then_inc(rstd_step, 1)
    pool.wait_ge(mv_step, B)
    nc.gpsimd.tensor_scalar(rstd[:], mv[:, :, 1], LN_EPS, None, ALU.add).then_inc(rstd_step, 1)
    pool.wait_ge(rstd_step, 2)
    nc.gpsimd.tensor_tensor(rstd[:], rstd[:], half[0:S, :], ALU.pow).then_inc(rstd_step, 1)


def double_rstd(nc, pool, mv, half, rstd, rvar, rstd2, mv_step, rstd_step):
    nc.gpsimd.memset(half[:], -0.5).then_inc(rstd_step, 1)
    pool.wait_ge(mv_step, B)
    nc.gpsimd.tensor_scalar(rvar[:], mv[:, :, 1], LN_EPS, None, ALU.add).then_inc(rstd_step, 1)
    pool.wait_ge(rstd_step, 2)
    nc.gpsimd.tensor_tensor(rstd[:], rvar[:], half[0:S, :], ALU.pow).then_inc(rstd_step, 1)
    pool.wait_ge(rstd_step, 3)
    nc.gpsimd.tensor_tensor(rvar[:], mv[:, :, 1], rstd[:], ALU.mult).then_inc(rstd_step, 1)
    pool.wait_ge(rstd_step, 4)
    nc.gpsimd.tensor_tensor(rvar[:], rvar[:], rstd[:], ALU.mult).then_inc(rstd_step, 1)
    pool.wait_ge(rstd_step, 5)
    nc.gpsimd.tensor_scalar(rvar[:], rvar[:], LN_EPS, None, ALU.add).then_inc(rstd_step, 1)
    pool.wait_ge(rstd_step, 6)
    nc.gpsimd.tensor_tensor(rstd2[:], rvar[:], half[0:S, :], ALU.pow).then_inc(rstd_step, 1)
    pool.wait_ge(rstd_step, 7)
    nc.gpsimd.tensor_tensor(rstd2[:], rstd2[:], rstd[:], ALU.mult).then_inc(rstd_step, 1)


def l0_attention(nc, x, stats, ident, passed, A):
    H, DH = 8, 128
    SCALE = float(DH) ** -0.5
    G = B // 2
    with ExitStack() as ctx:
        ph = Phase(nc, ctx, "l0a")
        wq, wk, wv = ph.sb("wq", [128, KC, H * DH]), ph.sb("wk", [128, KC, DH]), ph.sb("wv", [128, KC, DH])
        wo = ph.sb("wo", [128, H, D])
        pos_q, pos_k = ph.sb("pos_q", [DH, S]), ph.sb("pos_k", [DH, 1])
        causal = ph.sb("causal", [S, S])
        rstd = ph.sb("rstd", [S, B])
        half = ph.sb("half", [S, B])
        xn = ph.sb("xn", [S, 2, D])
        xT = ph.sb("xT", [128, KC, PAIR])
        qT, kT = ph.sb("qT", [DH, H, PAIR]), ph.sb("kT", [DH, PAIR])
        v = ph.sb("v", [S, 2, DH])
        p = ph.sb("p", [S, 2, H, S])
        pn = ph.sb("pn", [S, 2, H, S])
        pT = ph.sb("pT", [S, 2, H, S])
        oT = ph.sb("oT", [DH, 2, H, S])
        top, total, inv = ph.sb("top", [S, 2, H]), ph.sb("total", [S, 2, H]), ph.sb("inv", [S, 2, H])
        mv = ph.sb("mv", [S, B, 2])
        x_new, x_stats = ph.sb("x_new", [S, D]), ph.sb("x_stats", [S, 6])

        score_ps = [ph.banks("score0", 2), ph.banks("score1", 2)]
        q_ps = ph.banks("q", 2)
        v_ps, xT_ps = ph.banks("v", 1), ph.banks("xT", 1)

        attn_w, const_w = ph.sem("attn_w"), ph.sem("const_w")
        mv_step, rstd_step = ph.sem("mv_step"), ph.sem("rstd_step")
        xn_ready, xT_done, xT_ready = ph.sem("xn_ready"), ph.sem("xT_done"), ph.sem("xT_ready")
        q_done, q_ready, k_ready = ph.sem("q_done"), ph.sem("q_ready"), ph.sem("k_ready")
        v_done, v_ready = ph.sem("v_done"), ph.sem("v_ready")
        score_done, softmax_step, exp_ready = ph.sem("score_done"), ph.sem("softmax_step"), ph.sem("exp_ready")
        pn_ready, pT_done, pT_ready = ph.sem("pn_ready"), ph.sem("pT_done"), ph.sem("pT_ready")
        o_done, o_ready, y_done, x_step = ph.sem("o_done"), ph.sem("o_ready"), ph.sem("y_done"), ph.sem("x_step")

        block = ctx.enter_context(nc.Block())

        @block.sync
        def _(sp):
            sp.dma_start(wq[:], A["l0a_wq"].rearrange("(c p) n -> p c n", p=128)).then_inc(attn_w, 16)
            sp.dma_start(wk[:], A["l0a_wk"].rearrange("(c p) n -> p c n", p=128)).then_inc(attn_w, 16)
            sp.dma_start(wv[:], A["l0a_wv"].rearrange("(c p) n -> p c n", p=128)).then_inc(attn_w, 16)
            sp.dma_start(wo[:], A["l0a_wo"].rearrange("(h p) n -> p h n", p=128)).then_inc(attn_w, 16)
            sp.dma_start(pos_q[:], A["pos_q"]).then_inc(const_w, 16)
            sp.dma_start(pos_k[:], A["pos_k"]).then_inc(const_w, 16)
            sp.dma_start(causal[:], A["causal"]).then_inc(const_w, 16)

        @block.gpsimd
        def _(pool):
            single_rstd(nc, pool, mv, half, rstd, mv_step, rstd_step)

            def body(g, first, last):
                for j in range(2):
                    b = g * 2 + j
                    pool.wait_ge(softmax_step, b * 5 + 5)
                    since(pool, pT_done, b - 1)
                    nc.gpsimd.tensor_tensor(pn[:, j], p[:, j], inv[:, j, :, None].broadcast_to([S, H, S]),
                                            ALU.mult).then_inc(pn_ready, 1)
            over_steps(pool, body, G)

        @block.vector
        def _(dve):
            def norm(g):
                for j in range(2):
                    b = g * 2 + j
                    if j == 0:
                        since(dve, xT_done, g)
                    nc.vector.tensor_scalar(xn[:, j], x[:, b, :], mv[:, b, 0:1], rstd[:, bass.ds(b, 1)],
                                            ALU.subtract, ALU.mult).then_inc(xn_ready, 1)

            def q_add(g):
                for i in range(H // 2):
                    dve.wait_ge(q_done, g * 5 + i + 1)
                    if i == 0:
                        since(dve, score_done, g * 2)
                    nc.vector.tensor_tensor(
                        qT[:, 2 * i:2 * i + 2, :].rearrange("p h (j t) -> p (h j) t", j=2),
                        q_ps[:, i % 2, 0:2 * PAIR].rearrange("p (a t) -> p a t", t=S),
                        pos_q[:, None, :].broadcast_to([DH, 4, S]), ALU.add).then_inc(q_ready, 1)

            def softmax(g, j):
                b = g * 2 + j
                dve.wait_ge(score_done, b + 1)
                since(dve, pn_ready, b - 1)
                pj = p[:, j].rearrange("p (a h) s -> p a h s", a=2)
                for a in range(2):
                    last = nc.vector.tensor_tensor(
                        pj[:, a], score_ps[j][0:S, a, 0:4 * S].rearrange("p (h s) -> p h s", h=4),
                        causal[:, None, :].broadcast_to([S, 4, S]), ALU.add)
                last.then_inc(softmax_step, 1)
                dve.wait_ge(softmax_step, b * 5 + 1)
                nc.vector.tensor_reduce(top[:, j], p[:, j], AX.X, ALU.max).then_inc(softmax_step, 1)
                dve.wait_ge(softmax_step, b * 5 + 2)
                nc.vector.tensor_tensor(p[:, j], p[:, j], top[:, j, :, None].broadcast_to([S, H, S]),
                                        ALU.subtract).then_inc(softmax_step, 1)

            def sums(g, j):
                b = g * 2 + j
                dve.wait_ge(exp_ready, b + 1)
                nc.vector.tensor_reduce(total[:, j], p[:, j], AX.X, ALU.add).then_inc(softmax_step, 1)
                dve.wait_ge(softmax_step, b * 5 + 4)
                nc.vector.reciprocal(inv[:, j], total[:, j]).then_inc(softmax_step, 1)

            def update(g, j):
                b = g * 2 + j
                dve.wait_ge(y_done, b + 1)
                update_x(nc, dve, x, stats, x_new, x_stats, score_ps[j][0:S, 0, 0:D], b, x_step)

            aggregate(nc, dve, stats, mv, mv_step)
            dve.wait_ge(rstd_step, 3)
            norm(0)
            dve.wait_ge(const_w, 48)
            q_add(0)

            def body(g, first, last):
                softmax(g, 0)
                if not last:
                    norm(g + 1)
                sums(g, 0)
                softmax(g, 1)
                sums(g, 1)
                if not last:
                    q_add(g + 1)
                update(g, 0)
                update(g, 1)
            over_steps(dve, body, G)

        @block.scalar
        def _(act):
            def copy_xT(g):
                act.wait_ge(xT_done, g + 1)
                since(act, v_done, g)
                nc.scalar.activation(xT[:], xT_ps[:, 0, 0:KC * PAIR].rearrange("p (c t) -> p c t", c=KC),
                                     ACT.Copy).then_inc(xT_ready, 1)

            def add_k(g):
                act.wait_ge(q_done, g * 5 + 5)
                since(act, score_done, g * 2)
                nc.scalar.activation(kT[:], q_ps[:, 0, 0:PAIR], ACT.Identity, bias=pos_k[:, 0:1]).then_inc(k_ready, 1)

            def body(g, first, last):
                act.wait_ge(v_done, g + 1)
                since(act, o_done, g * 2)
                nc.scalar.activation(v[:], v_ps[0:S, 0, 0:2 * DH].rearrange("p (j d) -> p j d", j=2),
                                     ACT.Copy).then_inc(v_ready, 1)
                act.wait_ge(softmax_step, g * 10 + 3)
                nc.scalar.activation(p[:, 0], p[:, 0], ACT.Exp, scale=SCALE).then_inc(exp_ready, 1)
                if not last:
                    copy_xT(g + 1)
                act.wait_ge(softmax_step, g * 10 + 8)
                nc.scalar.activation(p[:, 1], p[:, 1], ACT.Exp, scale=SCALE).then_inc(exp_ready, 1)
                if not last:
                    add_k(g + 1)
                for j in range(2):
                    b = g * 2 + j
                    act.wait_ge(pT_done, b + 1)
                    since(act, o_done, b - 1)
                    nc.scalar.activation(pT[:, j].rearrange("p (a h) s -> p a (h s)", a=2),
                                         score_ps[j][0:S, :, 0:4 * S], ACT.Copy).then_inc(pT_ready, 1)
                for j in range(2):
                    b = g * 2 + j
                    act.wait_ge(o_done, b + 1)
                    since(act, y_done, b - 1)
                    for a in range(2):
                        bank = q_ps[:, a, :] if j == 0 else (v_ps, xT_ps)[a][:, 0, :]
                        done = nc.scalar.activation(oT[:, j].rearrange("p (a h) s -> p a (h s)", a=2)[:, a],
                                                    bank[:, 0:4 * S], ACT.Copy)
                    done.then_inc(o_ready, 1)

            act.wait_ge(const_w, 48)
            copy_xT(0)
            add_k(0)
            over_steps(act, body, G)

        @block.tensor
        def _(pe):
            def transpose_x(g):
                pe.wait_ge(xn_ready, g * 2 + 2)
                since(pe, o_ready, g * 2 - 2)
                for c in range(KC):
                    for j in range(2):
                        at = c * PAIR + j * S
                        done = nc.tensor.transpose(xT_ps[:, 0, at:at + S], xn[:, j, c * 128:(c + 1) * 128],
                                                   ident[0:S, 0:S])
                done.then_inc(xT_done, 1)

            def project_qk(g):
                pe.wait_ge(xT_ready, g + 1)
                if isinstance(g, int) and g == 0:
                    pe.wait_ge(attn_w, 64)
                for i in range(H // 2 + 1):
                    n = g * 5 + i
                    if i < 2:
                        since(pe, o_ready, g * 2 - 2)
                    else:
                        pe.wait_ge(q_ready, g * 4 + i - 1)
                    for k in range(2 if i < H // 2 else 1):
                        for c in range(KC):
                            w = wq[:, c, (2 * i + k) * DH:(2 * i + k + 1) * DH] if i < H // 2 else wk[:, c, :]
                            done = nc.tensor.matmul(q_ps[:, i % 2, k * PAIR:(k + 1) * PAIR], w, xT[:, c, :],
                                                    start=(c == 0), stop=(c == KC - 1))
                    done.then_inc(q_done, 1)

            def body(g, first, last):
                for j in range(2):
                    if j == 0:
                        pe.wait_ge(q_ready, g * 4 + 4)
                        pe.wait_ge(k_ready, g + 1)
                    b = g * 2 + j
                    since(pe, x_step, b * 4 - 7)
                    for h in range(H):
                        done = nc.tensor.matmul(score_ps[j][0:S, h // 4, (h % 4) * S:(h % 4 + 1) * S],
                                                qT[:, h, j * S:(j + 1) * S], kT[:, j * S:(j + 1) * S],
                                                start=True, stop=True)
                    done.then_inc(score_done, 1)
                since(pe, o_ready, g * 2)
                for j in range(2):
                    for c in range(KC):
                        done = nc.tensor.matmul(v_ps[0:S, 0, j * DH:(j + 1) * DH], xT[:, c, j * S:(j + 1) * S],
                                                wv[:, c, :], start=(c == 0), stop=(c == KC - 1))
                done.then_inc(v_done, 1)
                if not last:
                    transpose_x(g + 1)
                    project_qk(g + 1)
                for j in range(2):
                    b = g * 2 + j
                    pe.wait_ge(pn_ready, b + 1)
                    for h in range(H):
                        done = nc.tensor.transpose(score_ps[j][0:S, h // 4, (h % 4) * S:(h % 4 + 1) * S],
                                                   pn[:, j, h, :], ident[0:S, 0:S])
                    done.then_inc(pT_done, 1)
                for j in range(2):
                    b = g * 2 + j
                    pe.wait_ge(pT_ready, b + 1)
                    if j == 0:
                        pe.wait_ge(v_ready, g + 1)
                        if not last:
                            pe.wait_ge(k_ready, g + 2)
                            pe.wait_ge(q_ready, g * 4 + 8)
                    elif not last:
                        pe.wait_ge(xT_ready, g + 2)
                    for a in range(2):
                        bank = q_ps[:, a, :] if j == 0 else (v_ps, xT_ps)[a][:, 0, :]
                        done = nc.tensor.matmul(bank[:, 0:4 * S], v[:, j, :],
                                                pT[:, j, 4 * a:4 * a + 4, :], start=True, stop=True)
                    done.then_inc(o_done, 1)
                for j in range(2):
                    b = g * 2 + j
                    pe.wait_ge(o_ready, b + 1)
                    for h in range(H):
                        done = nc.tensor.matmul(score_ps[j][0:S, 0, 0:D], oT[:, j, h, :], wo[:, h, :],
                                                start=(h == 0), stop=(h == H - 1))
                    done.then_inc(y_done, 1)

            transpose_x(0)
            project_qk(0)
            over_steps(pe, body, G)


def l0_cross_attention(nc, x, stats, ident, passed, A):
    H, DH = 16, 64
    INNER = H * DH
    NC, CT = 3, N // 3
    KEYS = 488
    KT = KEYS // 4
    SCALE = float(DH) ** -0.5
    with ExitStack() as ctx:
        ph = Phase(nc, ctx, "l0x")
        wq, wkv = ph.sb("wq", [128, KC, INNER]), ph.sb("wkv", [128, KC, 2 * INNER])
        wout = ph.sb("wout", [128, INNER // 128, D])
        affine = ph.sb("affine", [128, 4, KC])
        mv, half = ph.sb("mv", [S, B, 2]), ph.sb("half", [128, B])
        rstd, rvar, rstd2 = ph.sb("rstd", [S, B]), ph.sb("rvar", [S, B]), ph.sb("rstd2", [S, B])
        c_in, c_norm = ph.sb("c_in", [CT, NC, D]), ph.sb("c_norm", [CT, NC, D])
        c_stats, c_mv = ph.sb("c_stats", [CT, NC, 6]), ph.sb("c_mv", [CT, NC, 2])
        c_var, c_rstd = ph.sb("c_var", [CT, NC]), ph.sb("c_rstd", [CT, NC])
        lat = ph.sb("lat", [S, D])
        mask_in, bias = ph.sb("mask_in", [S, MASK_WORDS], U32), ph.sb("bias", [S, KEYS])
        wkv_hi, wkv_lo = ph.sb("wkv_hi", [128, KC, 2 * INNER], F32R), ph.sb("wkv_lo", [128, KC, 2 * INNER], F32R)
        kvT = ph.sb("kvT", [128, KC, KEYS])
        kvT_hi, kvT_lo = ph.sb("kvT_hi", [128, KC, KEYS], F32R), ph.sb("kvT_lo", [128, KC, KEYS], F32R)
        q_hi, q_lo = ph.sb("q_hi", [128, 2, H // 2, S], F32R), ph.sb("q_lo", [128, 2, H // 2, S], F32R)
        kT_hi, kT_lo = ph.sb("kT_hi", [128, H // 2, KEYS], F32R), ph.sb("kT_lo", [128, H // 2, KEYS], F32R)
        v = ph.sb("v", [KT, 4, INNER])
        s_sb, p = ph.sb("s", [S, 2, KEYS]), ph.sb("p", [S, 3, KEYS])
        low, total = ph.sb("low", [S, H]), ph.sb("total", [S, H])
        inv, inv_total = ph.sb("inv", [S, 2]), ph.sb("inv_total", [S, 2, S])
        pT = ph.sb("pT", [KT, 2, 4 * S])
        oT = ph.sb("oT", [128, INNER // 128, S])
        x_new, x_stats = ph.sb("x_new", [S, D]), ph.sb("x_stats", [S, 6])

        score_ps, pT_ps, oT_ps = ph.banks("score", 2), ph.banks("pT", 2), ph.banks("oT", 2)
        proj_ps = ph.banks("proj", 2)

        weight_w, const_w, ctx_w, mask_w = ph.sem("weight_w"), ph.sem("const_w"), ph.sem("ctx_w"), ph.sem("mask_w")
        mv_step, rstd_step, zeroed = ph.sem("mv_step"), ph.sem("rstd_step"), ph.sem("zeroed")
        c_step, c_rstd_step = ph.sem("c_step"), ph.sem("c_rstd_step")
        norm_ready, bias_ready = ph.sem("norm_ready"), ph.sem("bias_ready")
        proj_done, kvT_ready = ph.sem("proj_done"), ph.sem("kvT_ready")
        v_even_ready, v_odd_ready = ph.sem("v_even_ready"), ph.sem("v_odd_ready")
        score_done, masked_ready, exp_ready = ph.sem("score_done"), ph.sem("masked_ready"), ph.sem("exp_ready")
        pT_done, pT_even_ready, pT_odd_ready = ph.sem("pT_done"), ph.sem("pT_even_ready"), ph.sem("pT_odd_ready")
        pv_done, inv_step = ph.sem("pv_done"), ph.sem("inv_step")
        oT_even_ready, oT_odd_ready = ph.sem("oT_even_ready"), ph.sem("oT_odd_ready")
        act_start, w_lo_ready = ph.sem("act_start"), ph.sem("w_lo_ready")
        hi_ready, lo_ready = ph.sem("hi_ready"), ph.sem("lo_ready")
        y_done, x_step = ph.sem("y_done"), ph.sem("x_step")

        T0, Q0, K0, V0, USES = 0, 2, 4, 12, 20
        SPLIT_Q, SPLIT_K, SPLITS = 2, 4, 12
        PARTS = [(c, slice(n * INNER, (n + 1) * INNER)) for n in range(2) for c in range(KC)]

        def key_bank(i):
            return (proj_ps, score_ps)[i // 2 % 2][:, i % 2, 0:KEYS]

        block = ctx.enter_context(nc.Block())

        @block.sync
        def _(sp):
            sp.dma_start(affine[:], A["l0x_affine"]).then_inc(const_w, 16)
            def load_ctx(b):
                sp.dma_start(c_in[:], A["ctx"][bass.ds(b, 1)].rearrange("b (c p) d -> p (b c) d", p=CT)
                             ).then_inc(ctx_w, 16)
                sp.dma_start(mask_in[:], A["ctx_mask"][bass.ds(b, 1), :].broadcast_to([S, MASK_WORDS])).then_inc(mask_w, 16)

            load_ctx(0)
            sp.dma_start(wq[:], A["l0x_wq"].rearrange("(c p) n -> p c n", p=128)).then_inc(weight_w, 16)
            sp.dma_start(wkv[:], A["l0x_wkv"].rearrange("(c p) n -> p c n", p=128)).then_inc(weight_w, 16)
            sp.dma_start(wout[:], A["l0x_wout"].rearrange("(c p) n -> p c n", p=128)).then_inc(weight_w, 16)
            with sp.Fori(1, B) as b:
                sp.wait_ge(norm_ready, b * 4)
                sp.wait_ge(bias_ready, b)
                load_ctx(b)

        @block.gpsimd
        def _(pool):
            nc.gpsimd.memset(half[:], -0.5).then_inc(zeroed, 1)
            nc.gpsimd.memset(kvT[:, :, N + S:KEYS], 0.0).then_inc(zeroed, 1)
            nc.gpsimd.memset(bias[:, N:N + S], 0.0).then_inc(zeroed, 1)
            nc.gpsimd.memset(bias[:, N + S:KEYS], NEG).then_inc(zeroed, 1)

            def context_rstd(b):
                since(pool, norm_ready, b * 4)
                wait_apart(pool, c_step, b * 6 + 6, passed)
                nc.gpsimd.tensor_scalar(c_var[:], c_mv[:, :, 1], LN_EPS, None, ALU.add).then_inc(c_rstd_step, 1)
                pool.wait_ge(c_rstd_step, b * 2 + 1)
                nc.gpsimd.tensor_tensor(c_rstd[:], c_var[:], half[0:CT, 0:NC], ALU.pow).then_inc(c_rstd_step, 1)

            def mask_bias(b):
                since(pool, mask_w, b * 16 + 16)
                wait_apart(pool, masked_ready, b * H, passed)
                nc.gpsimd.tensor_scalar(bias[:, 0:N], mask_in[:].bitcast(U8)[:, 0:N], 1.0, -NEG, ALU.subtract, ALU.mult
                                        ).then_inc(bias_ready, 1)

            pool.wait_ge(zeroed, 4)
            context_rstd(0)
            pool.wait_ge(mv_step, B)
            nc.gpsimd.tensor_scalar(rvar[:], mv[:, :, 1], LN_EPS, None, ALU.add).then_inc(rstd_step, 1)
            pool.wait_ge(rstd_step, 1)
            nc.gpsimd.tensor_tensor(rstd[:], rvar[:], half[0:S, :], ALU.pow).then_inc(rstd_step, 1)
            pool.wait_ge(rstd_step, 2)
            nc.gpsimd.tensor_tensor(rvar[:], mv[:, :, 1], rstd[:], ALU.mult).then_inc(rstd_step, 1)
            pool.wait_ge(rstd_step, 3)
            nc.gpsimd.tensor_tensor(rvar[:], rvar[:], rstd[:], ALU.mult).then_inc(rstd_step, 1)
            pool.wait_ge(rstd_step, 4)
            nc.gpsimd.tensor_scalar(rvar[:], rvar[:], LN_EPS, None, ALU.add).then_inc(rstd_step, 1)
            pool.wait_ge(rstd_step, 5)
            nc.gpsimd.tensor_tensor(rstd2[:], rvar[:], half[0:S, :], ALU.pow).then_inc(rstd_step, 1)
            pool.wait_ge(rstd_step, 6)
            nc.gpsimd.tensor_tensor(rstd2[:], rstd2[:], rstd[:], ALU.mult).then_inc(rstd_step, 1)
            mask_bias(0)
            with pool.Fori(1, B) as b:
                context_rstd(b)
                mask_bias(b)

        @block.vector
        def _(dve):
            def context_stats(b):
                dve.wait_ge(ctx_w, b * 16 + 16)
                for t in range(NC):
                    nc.vector.bn_stats(c_stats[:, t, :], c_in[:, t, :]).then_inc(c_step, 1)
                for t in range(NC):
                    wait_apart(dve, c_step, b * 6 + t + 1, passed)
                    nc.vector.bn_aggr(c_mv[:, t, :], c_stats[:, t, :]).then_inc(c_step, 1)

            def normalise(b):
                since(dve, proj_done, b * USES - USES + 2)
                dve.wait_ge(c_rstd_step, b * 2 + 2)
                for t in range(NC):
                    nc.vector.tensor_scalar(c_norm[:, t, :], c_in[:, t, :], c_mv[:, t, 0:1], c_rstd[:, t:t + 1],
                                            ALU.subtract, ALU.mult).then_inc(norm_ready, 1)
                nc.vector.tensor_scalar(lat[:], x[:, b, :], mv[:, b, 0:1], rstd2[:, bass.ds(b, 1)],
                                        ALU.subtract, ALU.mult).then_inc(norm_ready, 1)

            def transposed_inputs(b):
                for c in range(KC):
                    dve.wait_ge(proj_done, b * USES + T0 + c + 1)
                    for (lo, hi, a) in ((0, N, 0), (N, N + S, 2)):
                        done = nc.vector.tensor_scalar(kvT[:, c, lo:hi], proj_ps[:, c, lo:hi], affine[:, a, c:c + 1],
                                                       affine[:, a + 1, c:c + 1], ALU.mult, ALU.add)
                    done.then_inc(kvT_ready, 1)

            def split_inputs(b):
                for c in range(KC):
                    dve.wait_ge(hi_ready, b * SPLITS + c + 1)
                    nc.vector.tensor_tensor(kvT_lo[:, c, :], kvT[:, c, :], kvT_hi[:, c, :].bitcast(F32), ALU.subtract
                                            ).then_inc(lo_ready, 1)

            def split_queries_and_keys(b):
                for i in range(2):
                    dve.wait_ge(hi_ready, b * SPLITS + SPLIT_Q + i + 1)
                    for a in range(2):
                        half_of = slice(a * DH, (a + 1) * DH)
                        done = nc.vector.tensor_tensor(
                            q_lo[half_of, a, 4 * i:4 * i + 4, :].rearrange("p h s -> p (h s)"),
                            proj_ps[half_of, i, 0:4 * S],
                            q_hi[half_of, a, 4 * i:4 * i + 4, :].rearrange("p h s -> p (h s)").bitcast(F32), ALU.subtract)
                    done.then_inc(lo_ready, 1)
                for i in range(8):
                    dve.wait_ge(hi_ready, b * SPLITS + SPLIT_K + i + 1)
                    nc.vector.tensor_tensor(kT_lo[:, i, :], key_bank(i), kT_hi[:, i, :].bitcast(F32), ALU.subtract
                                            ).then_inc(lo_ready, 1)

            def values(b):
                for i in range(1, 8, 2):
                    dve.wait_ge(proj_done, b * USES + V0 + i + 1)
                    nc.vector.tensor_copy(v[:, i // 2, 512:1024], proj_ps[0:KT, 1, :]).then_inc(v_odd_ready, 1)

            def mask_score(b, h):
                if h == 0:
                    dve.wait_ge(bias_ready, b + 1)
                since(dve, exp_ready, b * H + h - 1)
                wait_apart(dve, score_done, b * H + h + 1, passed)
                nc.vector.tensor_tensor_reduce(s_sb[:, h % 2, :], score_ps[0:S, h % 2, 0:KEYS], bias[:], -SCALE, 3.4e38,
                                               ALU.add, ALU.min, low[:, h:h + 1]).then_inc(masked_ready, 1)

            def copy_pT(b, h):
                if h % 2 == 1:
                    since(dve, pv_done, b * H + h - 1)
                    dve.wait_ge(pT_done, b * H + h + 1)
                    nc.vector.tensor_copy(pT[:, 1, :], pT_ps[0:KT, 1, 0:4 * S]).then_inc(pT_odd_ready, 1)

            def invert_total(b, h):
                since(dve, pT_done, b * H + h - 1)
                dve.wait_ge(exp_ready, b * H + h + 1)
                nc.vector.reciprocal(inv[:, h % 2:h % 2 + 1], total[:, h:h + 1]).then_inc(inv_step, 1)
                dve.wait_ge(inv_step, (b * H + h) * 2 + 1)
                nc.vector.tensor_scalar(inv_total[:, h % 2, :], ident[0:S, 0:S], inv[:, h % 2:h % 2 + 1], None, ALU.mult
                                        ).then_inc(inv_step, 1)

            def copy_oT(b):
                dve.wait_ge(pv_done, b * H + H)
                since(dve, y_done, b)
                nc.vector.tensor_copy(oT[:, 4:8, :].rearrange("p h s -> p (h s)"), oT_ps[:, 1, 0:4 * S]
                                      ).then_inc(oT_odd_ready, 1)

            def update(b):
                dve.wait_ge(y_done, b + 1)
                update_x(nc, dve, x, stats, x_new, x_stats, proj_ps[0:S, 1, 0:D], b, x_step)

            aggregate(nc, dve, stats, mv, mv_step)
            context_stats(0)
            dve.wait_ge(rstd_step, 7)
            dve.wait_ge(const_w, 16)
            normalise(0)
            for n, (c, part) in enumerate(PARTS):
                dve.wait_ge(act_start, n + 3)
                nc.vector.tensor_tensor(wkv_lo[:, c, part], wkv[:, c, part],
                                        wkv_hi[:, c, part].bitcast(F32), ALU.subtract).then_inc(w_lo_ready, 1)

            def body(b, first, last):
                if not first:
                    invert_total(b - 1, H - 1)
                transposed_inputs(b)
                if not first:
                    copy_pT(b - 1, H - 1)
                split_inputs(b)
                if not first:
                    copy_oT(b - 1)
                split_queries_and_keys(b)
                values(b)
                for h in range(H):
                    mask_score(b, h)
                    if h >= 1:
                        invert_total(b, h - 1)
                    if h >= 2:
                        copy_pT(b, h - 2)
                    if h == 2 and not first:
                        update(b - 1)
                    if h == 4 and not last:
                        context_stats(b + 1)
                    if h == 8 and not last:
                        normalise(b + 1)
            over_steps(dve, body, B)
            invert_total(B - 1, H - 1)
            copy_pT(B - 1, H - 1)
            copy_oT(B - 1)
            update(B - 1)

        @block.scalar
        def _(act):
            def round_inputs(b):
                for c in range(KC):
                    act.wait_ge(kvT_ready, b * KC + c + 1)
                    nc.scalar.activation(kvT_hi[:, c, :], kvT[:, c, :], ACT.Copy).then_inc(hi_ready, 1)

            def round_queries_and_keys(b):
                if isinstance(b, int) and b == 0:
                    act.wait_ge(act_start, 2)
                for i in range(2):
                    act.wait_ge(proj_done, b * USES + Q0 + i + 1)
                    for a in range(2):
                        half_of = slice(a * DH, (a + 1) * DH)
                        done = nc.scalar.activation(
                            q_hi[half_of, a, 4 * i:4 * i + 4, :].rearrange("p h s -> p (h s)"),
                            proj_ps[half_of, i, 0:4 * S], ACT.Copy)
                    done.then_inc(hi_ready, 1)
                for i in range(8):
                    act.wait_ge(proj_done, b * USES + K0 + i + 1)
                    nc.scalar.activation(kT_hi[:, i, :], key_bank(i), ACT.Copy).then_inc(hi_ready, 1)

            def values(b):
                for i in range(0, 8, 2):
                    act.wait_ge(proj_done, b * USES + V0 + i + 1)
                    nc.scalar.activation(v[:, i // 2, 0:512], proj_ps[0:KT, 0, :], ACT.Copy).then_inc(v_even_ready, 1)

            def exp(b, h):
                act.wait_ge(masked_ready, b * H + h + 1)
                if h >= 3:
                    act.wait_ge(pT_done, b * H + h - 2)
                nc.scalar.activation(p[:, h % 3, :], s_sb[:, h % 2, :], ACT.Exp, scale=-1.0, bias=low[:, h:h + 1],
                                     accum_out=total[:, h:h + 1]).then_inc(exp_ready, 1)

            def copy_pT(b, h):
                if h % 2 == 0:
                    since(act, pv_done, b * H + h - 1)
                    act.wait_ge(pT_done, b * H + h + 1)
                    nc.scalar.activation(pT[:, 0, :], pT_ps[0:KT, 0, 0:4 * S], ACT.Copy).then_inc(pT_even_ready, 1)

            def copy_oT(b):
                act.wait_ge(pv_done, b * H + H)
                since(act, y_done, b)
                nc.scalar.activation(oT[:, 0:4, :].rearrange("p h s -> p (h s)"), oT_ps[:, 0, 0:4 * S], ACT.Copy
                                     ).then_inc(oT_even_ready, 1)

            act.wait_ge(zeroed, 4)
            for q in (q_hi, q_lo):
                nc.scalar.activation(q[:].rearrange("p a h s -> p (a h) s"), ident[:, None, 0:S].broadcast_to([128, H, S]),
                                     ACT.Copy, scale=0.0).then_inc(act_start, 1)
            act.wait_ge(weight_w, 48)
            for n, (c, part) in enumerate(PARTS):
                nc.scalar.activation(wkv_hi[:, c, part], wkv[:, c, part], ACT.Copy).then_inc(act_start, 1)

            def body(b, first, last):
                if not first:
                    copy_pT(b - 1, H - 2)
                round_inputs(b)
                if not first:
                    copy_oT(b - 1)
                round_queries_and_keys(b)
                values(b)
                if not first:
                    act.wait_ge(inv_step, b * H * 2)
                for h in range(H):
                    exp(b, h)
                    if h >= 2:
                        copy_pT(b, h - 2)
            over_steps(act, body, B)
            copy_pT(B - 1, H - 2)
            copy_oT(B - 1)

        @block.tensor
        def _(pe):
            def exact_product(out, a_hi, a_lo, b_hi, b_lo, first, last):
                nc.tensor.matmul(out, a_hi, b_hi, start=first, stop=False)
                nc.tensor.matmul(out, a_hi, b_lo, start=False, stop=False)
                return nc.tensor.matmul(out, a_lo, b_hi, start=False, stop=last)

            def transpose_inputs(b):
                pe.wait_ge(norm_ready, b * 4 + 4)
                for c in range(KC):
                    since(pe, (v_even_ready, v_odd_ready)[c], b * 4)
                    for t in range(NC):
                        nc.tensor.transpose(proj_ps[:, c, t * CT:(t + 1) * CT], c_norm[:, t, c * 128:(c + 1) * 128],
                                            ident[0:CT, 0:CT])
                    nc.tensor.transpose(proj_ps[:, c, N:N + S], lat[:, c * 128:(c + 1) * 128], ident[0:S, 0:S]
                                        ).then_inc(proj_done, 1)

            def project_q_and_k(b):
                pe.wait_ge(kvT_ready, b * KC + KC)
                for i in range(2):
                    for k in range(4):
                        at = (4 * i + k) * 128
                        for c in range(KC):
                            done = nc.tensor.matmul(proj_ps[:, i, k * S:(k + 1) * S], wq[:, c, at:at + 128],
                                                    kvT[:, c, N:N + S], start=(c == 0), stop=(c == KC - 1))
                    done.then_inc(proj_done, 1)
                for i in range(8):
                    if i < 2:
                        pe.wait_ge(lo_ready, b * SPLITS + SPLIT_Q + i + 1)
                    elif i < 4:
                        since(pe, masked_ready, b * H)
                    else:
                        pe.wait_ge(lo_ready, b * SPLITS + SPLIT_K + i - 3)
                    at = slice(i * 128, (i + 1) * 128)
                    for c in range(KC):
                        done = exact_product(key_bank(i), wkv_hi[:, c, at], wkv_lo[:, c, at],
                                             kvT_hi[:, c, :], kvT_lo[:, c, :], c == 0, c == KC - 1)
                    done.then_inc(proj_done, 1)

            def project_v(b):
                for i in range(8):
                    if i < 2:
                        pe.wait_ge(lo_ready, b * SPLITS + SPLIT_K + 4 + i + 1)
                    else:
                        pe.wait_ge((v_even_ready, v_odd_ready)[i % 2], b * 4 + i // 2)
                    keys = slice((i // 2) * KT, (i // 2 + 1) * KT)
                    at = slice(INNER + (i % 2) * 512, INNER + (i % 2) * 512 + 512)
                    for c in range(KC):
                        done = exact_product(proj_ps[0:KT, i % 2, :], kvT_hi[:, c, keys], kvT_lo[:, c, keys],
                                             wkv_hi[:, c, at], wkv_lo[:, c, at], c == 0, c == KC - 1)
                    done.then_inc(proj_done, 1)

            def score(b, h):
                if h == 0:
                    pe.wait_ge(lo_ready, b * SPLITS + SPLITS)
                since(pe, masked_ready, b * H + h - 1)
                exact_product(score_ps[0:S, h % 2, 0:KEYS], q_hi[:, h % 2, h // 2, :], q_lo[:, h % 2, h // 2, :],
                              kT_hi[:, h // 2, :], kT_lo[:, h // 2, :], True, True).then_inc(score_done, 1)

            def transpose_p(b, h):
                since(pe, (pT_even_ready, pT_odd_ready)[h % 2], b * (H // 2) + h // 2)
                pe.wait_ge(inv_step, (b * H + h) * 2 + 2)
                for t in range(4):
                    done = nc.tensor.matmul(pT_ps[0:KT, h % 2, t * S:(t + 1) * S], p[:, h % 3, t * KT:(t + 1) * KT],
                                            inv_total[:, h % 2, :], start=True, stop=True)
                done.then_inc(pT_done, 1)

            def weigh_values(b, h):
                if h == 0:
                    pe.wait_ge(v_even_ready, b * 4 + 4)
                    pe.wait_ge(v_odd_ready, b * 4 + 4)
                    since(pe, oT_even_ready, b)
                    since(pe, oT_odd_ready, b)
                pe.wait_ge((pT_even_ready, pT_odd_ready)[h % 2], b * (H // 2) + h // 2 + 1)
                i, at = h // 2, (h % 2) * DH
                for t in range(4):
                    done = nc.tensor.matmul(oT_ps[at:at + DH, i // 4, (i % 4) * S:(i % 4 + 1) * S],
                                            v[:, t, h * DH:(h + 1) * DH], pT[:, h % 2, t * S:(t + 1) * S],
                                            start=(t == 0), stop=(t == 3))
                done.then_inc(pv_done, 1)

            def finish_heads(b):
                transpose_p(b, H - 2)
                weigh_values(b, H - 3)
                transpose_p(b, H - 1)
                weigh_values(b, H - 2)
                weigh_values(b, H - 1)

            def project_out(b, emptied):
                since(pe, v_odd_ready, emptied)
                pe.wait_ge(oT_even_ready, b + 1)
                pe.wait_ge(oT_odd_ready, b + 1)
                for c in range(INNER // 128):
                    done = nc.tensor.matmul(proj_ps[0:S, 1, 0:D], oT[:, c, :], wout[:, c, :],
                                            start=(c == 0), stop=(c == INNER // 128 - 1))
                done.then_inc(y_done, 1)

            def body(b, first, last):
                transpose_inputs(b)
                if first:
                    pe.wait_ge(weight_w, 48)
                    pe.wait_ge(w_lo_ready, len(PARTS))
                if not first:
                    finish_heads(b - 1)
                project_q_and_k(b)
                project_v(b)
                for h in range(H):
                    score(b, h)
                    if h == 1 and not first:
                        project_out(b - 1, b * 4 + 4)
                    if h >= 2:
                        transpose_p(b, h - 2)
                    if h >= 3:
                        weigh_values(b, h - 3)
                if not first:
                    pe.wait_ge(x_step, b * 4 - 3)
            over_steps(pe, body, B)
            finish_heads(B - 1)
            project_out(B - 1, B * 4)


def l0_experts(nc, x, stats, ident, passed, A):
    E, F = 8, 1024
    FC = F // 128
    TILES = (B * S + E * 127) // 128
    with ExitStack() as ctx:
        ph = Phase(nc, ctx, "l0f")
        w1 = ph.sb("w1", [128, KC, E * F])
        wo, wr = ph.sb("wo", [128, FC, D]), ph.sb("wr", [128, KC, E])
        rows = ph.sb("rows", [128, 3, D])
        before, ones = ph.sb("before", [S, S]), ph.sb("ones", [S, S])
        expert_no, tile_no = ph.sb("expert_no", [S, E]), ph.sb("tile_no", [1, TILES])
        mv, half, rstd = ph.sb("mv", [S, B, 2]), ph.sb("half", [S, B]), ph.sb("rstd", [S, B])
        x1 = ph.sb("x1", [S, B, D])
        x1T = ph.sb("x1T", [128, 2, 2, KC, S])
        logits, best, best_no = ph.sb("logits", [S, B, E]), ph.sb("best", [S, B, 8]), ph.sb("best_no", [S, B, 8], U32)
        expert = ph.sb("expert", [S, B])
        one_hot, rank = ph.sb("one_hot", [S, B, E]), ph.sb("rank", [S, B, E])
        sums = ph.sb("sums", [S, 2, B, E])
        tiles, tiles_i = ph.sb("tiles", [S, 4, E]), ph.sb("tiles_i", [S, E], mybir.dt.int32)
        slot, slot_i = ph.sb("slot", [S, B]), ph.sb("slot_i", [S, B], U32)
        after = ph.sb("after", [1, TILES, E])
        tile_expert, tile_expert_i = ph.sb("tile_expert", [1, TILES]), ph.sb("tile_expert_i", [1, TILES], mybir.dt.int32)
        zeros = ph.sb("zeros", [128, D])
        xs, xsT = ph.sb("xs", [128, D]), ph.sb("xsT", [128, KC, 128])
        b1 = ph.sb("b1", [128, F])
        pre, h, hT = ph.sb("pre", [128, F]), ph.sb("h", [128, F]), ph.sb("hT", [128, FC, 128])
        ys = ph.sb("ys", [128, D])
        y = ph.sb("y", [S, B, D])
        y_stats, y_mv = ph.sb("y_stats", [S, B, 6]), ph.sb("y_mv", [S, B, 2])
        y_rstd = ph.sb("y_rstd", [S, B])
        sorted_x = nc.dram_tensor("sorted_x", ((TILES + 1) * 128, D), F32, kind="Internal").ap()
        sorted_y = nc.dram_tensor("sorted_y", (TILES * 128, D), F32, kind="Internal").ap()

        route_ps, xT_ps = ph.banks("route", 1), ph.banks("xT", 1)
        pre_ps, hT_ps, y_ps = ph.banks("pre", 2), ph.banks("hT", 2), ph.banks("y", 1)

        weight_w, const_w = ph.sem("weight_w"), ph.sem("const_w")
        mv_step, rstd_step, zeroed, padded = ph.sem("mv_step"), ph.sem("rstd_step"), ph.sem("zeroed"), ph.sem("padded")
        x1_ready, xT_done, xT_ready = ph.sem("x1_ready"), ph.sem("xT_done"), ph.sem("xT_ready")
        router_done, route_step, one_hot_ready = ph.sem("router_done"), ph.sem("route_step"), ph.sem("one_hot_ready")
        rank_done = ph.sem("rank_done")
        scattered, xs_w, b1_w = ph.sem("scattered"), ph.sem("xs_w"), ph.sem("b1_w")
        xsT_done, xsT_ready, pre_done = ph.sem("xsT_done"), ph.sem("xsT_ready"), ph.sem("pre_done")
        pre_ready, hT_done = ph.sem("pre_ready"), ph.sem("hT_done")
        hT_even_ready, hT_odd_ready = ph.sem("hT_even_ready"), ph.sem("hT_odd_ready")
        gelu_ready, y_done, ys_ready, ys_w = ph.sem("gelu_ready"), ph.sem("y_done"), ph.sem("ys_ready"), ph.sem("ys_w")
        gathered, y_step, y_rstd_ready, x_step = ph.sem("gathered"), ph.sem("y_step"), ph.sem("y_rstd_ready"), ph.sem("x_step")

        slot_ready, normed, scaled = ph.sem("slot_ready"), ph.sem("normed"), ph.sem("scaled")
        block = ctx.enter_context(nc.Block())

        @block.sync
        def _(sp):
            sp.dma_start(wr[:], A["l0f_wr"].rearrange("(c p) n -> p c n", p=128)).then_inc(const_w, 16)
            sp.dma_start(before[:], A["before"]).then_inc(const_w, 16)
            sp.dma_start(expert_no[:], A["expert_no"].broadcast_to([S, E])).then_inc(const_w, 16)
            sp.dma_start(tile_no[:], A["tile_no"]).then_inc(const_w, 16)
            sp.dma_start(rows[:], A["l0f_rows"].broadcast_to([128, 3, D])).then_inc(const_w, 16)
            for c in range(KC):
                sp.dma_start(w1[:, c, :].rearrange("p (e n) -> p e n", e=E),
                             A["l0f_w1"][:, c * 128:(c + 1) * 128, :].rearrange("e p n -> p e n")).then_inc(weight_w, 16)
            sp.dma_start(wo[:], A["l0f_wo"].rearrange("(c p) n -> p c n", p=128)).then_inc(weight_w, 16)
            sp.wait_ge(zeroed, 3)
            sp.dma_start(sorted_x.rearrange("(t p) d -> p t d", p=128),
                         zeros[:, None, :].broadcast_to([128, TILES + 1, D])).then_inc(padded, 16)

            def load_b1(i):
                e = sp.value_load(tile_expert_i[0:1, bass.ds(i, 1)], min_val=0, max_val=(E - 1) * F)
                sp.dma_start(b1[:], A["l0f_b1"][:, bass.ds(e, F)].broadcast_to([128, F])).then_inc(b1_w, 16)

            def load_tile(i):
                sp.dma_start(xs[:], sorted_x[bass.ds(i * 128, 128), :]).then_inc(xs_w, 16)

            def store_tile(i):
                sp.wait_ge(ys_ready, i + 1)
                sp.dma_start(sorted_y[bass.ds(i * 128, 128), :], ys[:]).then_inc(ys_w, 16)

            sp.wait_ge(scattered, 16 * B)
            load_tile(0)
            sp.wait_ge(xsT_done, 1)
            load_tile(1)
            sp.wait_ge(slot_ready, 2)
            load_b1(0)
            with sp.Fori(0, TILES - 1) as i:
                sp.wait_ge(xsT_done, i + 2)
                load_tile(i + 2)
                sp.wait_ge(pre_ready, i + 1)
                load_b1(i + 1)
                store_tile(i)
            store_tile(TILES - 1)

        @block.gpsimd
        def _(pool):
            nc.gpsimd.memset(half[:], -0.5).then_inc(zeroed, 1)
            nc.gpsimd.memset(ones[:], 1.0).then_inc(zeroed, 1)
            nc.gpsimd.memset(zeros[:], 0.0).then_inc(zeroed, 1)
            pool.wait_ge(zeroed, 3)
            pool.wait_ge(mv_step, B)
            nc.gpsimd.tensor_scalar(rstd[:], mv[:, :, 1], LN_EPS, None, ALU.add).then_inc(rstd_step, 1)
            pool.wait_ge(rstd_step, 1)
            nc.gpsimd.tensor_tensor(rstd[:], rstd[:], half[:], ALU.pow).then_inc(rstd_step, 1)
            pool.wait_ge(x1_ready, B)
            pool.wait_ge(padded, 16)
            pool.wait_ge(slot_ready, 1)
            for b in range(B):
                nc.gpsimd.indirect_dma_start(sorted_x, bass.IndirectOffsetOnAxis(slot_i[:, b:b + 1], 0), x1[:, b, :],
                                             None).then_inc(scattered, 16)
            pool.wait_ge(ys_w, 16 * TILES)
            for b in range(B):
                nc.gpsimd.indirect_dma_start(y[:, b, :], None, sorted_y,
                                             bass.IndirectOffsetOnAxis(slot_i[:, b:b + 1], 0)).then_inc(gathered, 16)
            pool.wait_ge(y_step, 3 * B)
            nc.gpsimd.tensor_scalar(y_rstd[:], y_mv[:, :, 1], 1e-12, None, ALU.add).then_inc(y_rstd_ready, 1)
            pool.wait_ge(y_rstd_ready, 1)
            nc.gpsimd.tensor_tensor(y_rstd[:], y_rstd[:], half[:], ALU.pow).then_inc(y_rstd_ready, 1)
            for b in range(B):
                pool.wait_ge(normed, b + 1)
                nc.gpsimd.tensor_tensor(y[:, b, :], y[:, b, :], rows[0:S, 1, :], ALU.mult).then_inc(scaled, 1)
                pool.wait_ge(scaled, 2 * b + 1)
                nc.gpsimd.tensor_tensor(y[:, b, :], y[:, b, :], rows[0:S, 2, :], ALU.add).then_inc(scaled, 1)

        @block.vector
        def _(dve):
            steps = [0]

            def step(instruction):
                steps[0] += 1
                instruction.then_inc(route_step, 1)
                dve.wait_ge(route_step, steps[0])

            aggregate(nc, dve, stats, mv, mv_step)
            dve.wait_ge(rstd_step, 2)
            for b in range(B):
                nc.vector.tensor_scalar(x1[:, b, :], x[:, b, :], mv[:, b, 0:1], rstd[:, b:b + 1],
                                        ALU.subtract, ALU.mult).then_inc(x1_ready, 1)
            dve.wait_ge(router_done, B // 2)
            step(nc.vector.tensor_copy(logits[:].rearrange("p b e -> p (b e)"), route_ps[0:S, 0, 0:B * E]))
            for b in range(B):
                nc.vector.max(best[:, b, :], logits[:, b, :]).then_inc(route_step, 1)
            for b in range(B):
                dve.wait_ge(route_step, b + 2)
                nc.vector.max_index(best_no[:, b, :], best[:, b, :], logits[:, b, :]).then_inc(route_step, 1)
            steps[0] += 2 * B
            dve.wait_ge(route_step, steps[0])
            step(nc.vector.tensor_copy(expert[:], best_no[:, :, 0]))
            dve.wait_ge(const_w, 80)
            nc.vector.tensor_tensor(one_hot[:], expert_no[:, None, :].broadcast_to([S, B, E]),
                                    expert[:, :, None].broadcast_to([S, B, E]), ALU.is_equal).then_inc(one_hot_ready, 1)
            dve.wait_ge(rank_done, 1)
            nc.vector.tensor_copy(rank[:].rearrange("p b e -> p (b e)"), route_ps[0:S, 0, 128:256])
            step(nc.vector.tensor_copy(sums[:, 0].rearrange("p b e -> p (b e)"), route_ps[0:S, 0, 256:384]))
            for n, d in enumerate((1, 2, 4, 8)):
                a, z = sums[:, n % 2], sums[:, (n + 1) % 2]
                nc.vector.tensor_copy(z[:, 0:d, :], a[:, 0:d, :])
                step(nc.vector.tensor_tensor(z[:, d:B, :], a[:, d:B, :], a[:, 0:B - d, :], ALU.add))
            step(nc.vector.tensor_scalar(tiles_i[:], sums[:, 0, B - 1, :], 127.0, None, ALU.add))
            step(nc.vector.tensor_scalar(tiles_i[:], tiles_i[:], 7, None, ALU.arith_shift_right))
            step(nc.vector.tensor_copy(tiles[:, 0, :], tiles_i[:]))
            for n, d in enumerate((1, 2, 4)):
                nc.vector.tensor_copy(tiles[:, n + 1, 0:d], tiles[:, n, 0:d])
                step(nc.vector.tensor_tensor(tiles[:, n + 1, d:E], tiles[:, n, d:E], tiles[:, n, 0:E - d], ALU.add))
            step(nc.vector.tensor_tensor(tiles[:, 0, :], tiles[:, 3, :], tiles[:, 0, :], ALU.subtract))
            step(nc.vector.tensor_scalar(tiles[:, 1, :], tiles[:, 0, :], 128.0, None, ALU.mult))
            step(nc.vector.tensor_tensor(rank[:, 1:B, :], rank[:, 1:B, :], sums[:, 0, 0:B - 1, :], ALU.add))
            step(nc.vector.tensor_tensor(rank[:], rank[:], tiles[:, 1:2, :].broadcast_to([S, B, E]), ALU.add))
            step(nc.vector.tensor_tensor(rank[:], rank[:], one_hot[:], ALU.mult))
            step(nc.vector.tensor_reduce(slot[:], rank[:], AX.X, ALU.add))
            nc.vector.tensor_copy(slot_i[:], slot[:]).then_inc(slot_ready, 1)
            step(nc.vector.tensor_tensor(after[:], tile_no[:, :, None].broadcast_to([1, TILES, E]),
                                         tiles[0:1, 3:4, :].broadcast_to([1, TILES, E]), ALU.is_ge))
            step(nc.vector.tensor_reduce(tile_expert[:], after[:], AX.X, ALU.add))
            step(nc.vector.tensor_scalar(tile_expert[:], tile_expert[:], float(E - 1), float(F), ALU.min, ALU.mult))
            nc.vector.tensor_copy(tile_expert_i[:], tile_expert[:]).then_inc(slot_ready, 1)

            def add_bias(i):
                since(dve, pre_done, i + 1)
                dve.wait_ge(b1_w, i * 16 + 16)
                since(dve, gelu_ready, i)
                nc.vector.tensor_tensor(pre[:], pre_ps[:].rearrange("p a n -> p (a n)"), b1[:], ALU.add
                                        ).then_inc(pre_ready, 1)

            def tile(i, first, last):
                dve.wait_ge(hT_done, i * 2 + 2)
                since(dve, y_done, i)
                nc.vector.tensor_copy(hT[:, 4:8, :].rearrange("p f t -> p (f t)"), hT_ps[:, 1, :]).then_inc(hT_odd_ready, 1)
                if not last:
                    add_bias(i + 1)
                dve.wait_ge(y_done, i + 1)
                since(dve, ys_w, i * 16)
                nc.vector.tensor_tensor(ys[:], y_ps[:, 0, 0:D], rows[:, 0, :], ALU.add).then_inc(ys_ready, 1)
            add_bias(0)
            over_steps(dve, tile, TILES)

            dve.wait_ge(gathered, 16 * B)
            for b in range(B):
                nc.vector.tensor_tensor(y[:, b, :], y[:, b, :], x1[:, b, :], ALU.add).then_inc(y_step, 1)
            for b in range(B):
                dve.wait_ge(y_step, b + 1)
                nc.vector.bn_stats(y_stats[:, b, :], y[:, b, :]).then_inc(y_step, 1)
            for b in range(B):
                dve.wait_ge(y_step, B + b + 1)
                nc.vector.bn_aggr(y_mv[:, b, :], y_stats[:, b, :]).then_inc(y_step, 1)
            dve.wait_ge(y_rstd_ready, 2)
            for b in range(B):
                nc.vector.tensor_scalar(y[:, b, :], y[:, b, :], y_mv[:, b, 0:1], y_rstd[:, b:b + 1],
                                        ALU.subtract, ALU.mult).then_inc(normed, 1)
            for b in range(B):
                dve.wait_ge(scaled, 2 * b + 2)
                nc.vector.tensor_tensor(x[:, b, :], x[:, b, :], y[:, b, :], ALU.add).then_inc(x_step, 1)
            for b in range(B):
                dve.wait_ge(x_step, b + 1)
                nc.vector.bn_stats(stats[:, b, :], x[:, b, :])

        @block.scalar
        def _(act):
            for g in range(B // 2):
                act.wait_ge(xT_done, g + 1)
                if g >= 2:
                    act.wait_ge(router_done, g - 1)
                nc.scalar.activation(x1T[:, g % 2].rearrange("p j c t -> p (j c t)"),
                                     (xT_ps, y_ps)[g % 2][:, 0, 0:2 * KC * S], ACT.Copy).then_inc(xT_ready, 1)

            def tile_input(i):
                since(act, pre_done, i)
                act.wait_ge(xsT_done, i + 1)
                nc.scalar.activation(xsT[:].rearrange("p c t -> p (c t)"), xT_ps[:, 0, 0:KC * 128], ACT.Copy
                                     ).then_inc(xsT_ready, 1)

            def activate(i):
                act.wait_ge(pre_ready, i + 1)
                since(act, hT_done, i * 2)
                nc.scalar.activation(h[:], pre[:], ACT.Gelu).then_inc(gelu_ready, 1)

            def tile(i, first, last):
                act.wait_ge(hT_done, i * 2 + 1)
                since(act, y_done, i)
                nc.scalar.activation(hT[:, 0:4, :].rearrange("p f t -> p (f t)"), hT_ps[:, 0, :], ACT.Copy
                                     ).then_inc(hT_even_ready, 1)
                if not last:
                    tile_input(i + 2)
                    activate(i + 1)

            tile_input(0)
            activate(0)
            tile_input(1)
            over_steps(act, tile, TILES)

        @block.tensor
        def _(pe):
            pe.wait_ge(const_w, 80)
            for g in range(B // 2 + 1):
                if g < B // 2:
                    pe.wait_ge(x1_ready, 2 * g + 2)
                    if g >= 2:
                        pe.wait_ge(xT_ready, g - 1)
                    bank = (xT_ps, y_ps)[g % 2]
                    for j in range(2):
                        for c in range(KC):
                            at = (j * KC + c) * S
                            done = nc.tensor.transpose(bank[:, 0, at:at + S],
                                                       x1[:, 2 * g + j, c * 128:(c + 1) * 128], ident[0:S, 0:S])
                    done.then_inc(xT_done, 1)
                if g >= 1:
                    pe.wait_ge(xT_ready, g)
                    for j in range(2):
                        b = 2 * (g - 1) + j
                        for c in range(KC):
                            done = nc.tensor.matmul(route_ps[0:S, 0, b * E:(b + 1) * E], x1T[:, (g - 1) % 2, j, c, :],
                                                    wr[:, c, :], start=(c == 0), stop=(c == KC - 1))
                    done.then_inc(router_done, 1)
            pe.wait_ge(one_hot_ready, 1)
            for n, m in enumerate((before, ones)):
                done = nc.tensor.matmul(route_ps[0:S, 0, (n + 1) * 128:(n + 2) * 128], m[:],
                                        one_hot[:].rearrange("p b e -> p (b e)"), start=True, stop=True)
            done.then_inc(rank_done, 1)

            def transpose_tile(i):
                since(pe, xs_w, i * 16 + 16)
                since(pe, xsT_ready, i)
                for c in range(KC):
                    done = nc.tensor.transpose(xT_ps[:, 0, c * 128:(c + 1) * 128], xs[:, c * 128:(c + 1) * 128], ident[:])
                done.then_inc(xsT_done, 1)

            def multiply(i):
                e = pe.value_load(tile_expert_i[0:1, bass.ds(i, 1)], min_val=0, max_val=(E - 1) * F)
                pe.wait_ge(xsT_ready, i + 1)
                since(pe, pre_ready, i)
                for a in range(2):
                    for c in range(KC):
                        done = nc.tensor.matmul(pre_ps[:, a, :], xsT[:, c, :], w1[:, c, bass.ds(e + a * 512, 512)],
                                                start=(c == 0), stop=(c == KC - 1))
                done.then_inc(pre_done, 1)

            def tile(i, first, last):
                pe.wait_ge(gelu_ready, i + 1)
                since(pe, hT_even_ready, i)
                since(pe, hT_odd_ready, i)
                for f in range(FC):
                    done = nc.tensor.transpose(hT_ps[:, f // 4, (f % 4) * 128:(f % 4 + 1) * 128],
                                               h[:, f * 128:(f + 1) * 128], ident[:])
                    if f % 4 == 3:
                        done.then_inc(hT_done, 1)
                if not last:
                    multiply(i + 1)
                    transpose_tile(i + 2)
                pe.wait_ge(hT_even_ready, i + 1)
                pe.wait_ge(hT_odd_ready, i + 1)
                since(pe, ys_ready, i)
                for f in range(FC):
                    done = nc.tensor.matmul(y_ps[:, 0, 0:D], hT[:, f, :], wo[:, f, :],
                                            start=(f == 0), stop=(f == FC - 1))
                done.then_inc(y_done, 1)

            transpose_tile(0)
            pe.wait_ge(slot_ready, 2)
            pe.wait_ge(weight_w, 16 * (KC + 1))
            multiply(0)
            transpose_tile(1)
            over_steps(pe, tile, TILES)


def l1_attention(nc, x, stats, ident, passed, A):
    H, DH = 16, 64
    HP = H // 2
    SCALE = float(DH) ** -0.5
    G = B // 2
    with ExitStack() as ctx:
        ph = Phase(nc, ctx, "l1a")
        wq, wk = ph.sb("wq", [128, KC, H * DH]), ph.sb("wk", [128, KC, 2 * DH])
        wv, wo = ph.sb("wv", [128, KC, DH]), ph.sb("wo", [128, HP, D])
        gamma, causal = ph.sb("gamma", [128, 1, KC]), ph.sb("causal", [S, S])
        mv, half = ph.sb("mv", [S, B, 2]), ph.sb("half", [S, B])
        rstd, rvar, rstd2 = ph.sb("rstd", [S, B]), ph.sb("rvar", [S, B]), ph.sb("rstd2", [S, B])
        x1, x2 = ph.sb("x1", [S, 2, D]), ph.sb("x2", [S, 2, D])
        x1T, x2T = ph.sb("x1T", [128, KC, PAIR]), ph.sb("x2T", [128, KC, PAIR])
        qT, kT = ph.sb("qT", [128, HP, PAIR]), ph.sb("kT", [128, PAIR])
        v, v_next = ph.sb("v", [S, 2, DH]), ph.sb("v_next", [S, 2, DH])
        p, pn = ph.sb("p", [S, 2, H, S]), ph.sb("pn", [S, 2, H, S])
        pT, oT = ph.sb("pT", [S, H, S]), ph.sb("oT", [128, 2, HP, S])
        top, total, inv = ph.sb("top", [S, 2, H]), ph.sb("total", [S, 2, H]), ph.sb("inv", [S, 2, H])
        x_new, x_stats = ph.sb("x_new", [S, D]), ph.sb("x_stats", [S, 6])

        score_ps = ph.banks("score", 4)
        proj_ps = ph.banks("proj", 2)
        in_ps = ph.banks("in", 2)

        weight_w, const_w = ph.sem("weight_w"), ph.sem("const_w")
        mv_step, rstd_step = ph.sem("mv_step"), ph.sem("rstd_step")
        norm_ready, inT_done, inT_ready = ph.sem("norm_ready"), ph.sem("inT_done"), ph.sem("inT_ready")
        proj_done, proj_ready, v_ready = ph.sem("proj_done"), ph.sem("proj_ready"), ph.sem("v_ready")
        score_done, softmax_step, exp_ready = ph.sem("score_done"), ph.sem("softmax_step"), ph.sem("exp_ready")
        pn_ready, pT_done, pT_ready = ph.sem("pn_ready"), ph.sem("pT_done"), ph.sem("pT_ready")
        o_done, o_ready, y_done, x_step = ph.sem("o_done"), ph.sem("o_ready"), ph.sem("y_done"), ph.sem("x_step")

        block = ctx.enter_context(nc.Block())

        @block.sync
        def _(sp):
            sp.dma_start(gamma[:], A["l1a_gamma"]).then_inc(const_w, 16)
            sp.dma_start(causal[:], A["causal"]).then_inc(const_w, 16)
            sp.dma_start(wq[:], A["l1a_wq"].rearrange("(c p) n -> p c n", p=128)).then_inc(weight_w, 16)
            sp.dma_start(wk[:], A["l1a_wk"].rearrange("(c p) n -> p c n", p=128)).then_inc(weight_w, 16)
            sp.dma_start(wv[:], A["l1a_wv"].rearrange("(c p) n -> p c n", p=128)).then_inc(weight_w, 16)
            sp.dma_start(wo[:], A["l1a_wo"].rearrange("(c p) n -> p c n", p=128)).then_inc(weight_w, 16)

        @block.gpsimd
        def _(pool):
            double_rstd(nc, pool, mv, half, rstd, rvar, rstd2, mv_step, rstd_step)

            def body(g, first, last):
                for j in range(2):
                    b = g * 2 + j
                    pool.wait_ge(softmax_step, b * 5 + 5)
                    since(pool, pT_done, b - 1)
                    nc.gpsimd.tensor_tensor(pn[:, j], p[:, j], inv[:, j, :, None].broadcast_to([S, H, S]),
                                            ALU.mult).then_inc(pn_ready, 1)
            over_steps(pool, body, G)

        @block.vector
        def _(dve):
            def norm(g):
                for j in range(2):
                    b = g * 2 + j
                    if j == 0:
                        since(dve, inT_done, g * 2)
                    nc.vector.tensor_scalar(x1[:, j], x[:, b, :], mv[:, b, 0:1], rstd[:, bass.ds(b, 1)],
                                            ALU.subtract, ALU.mult).then_inc(norm_ready, 1)
                    nc.vector.tensor_scalar(x2[:, j], x[:, b, :], mv[:, b, 0:1], rstd2[:, bass.ds(b, 1)],
                                            ALU.subtract, ALU.mult).then_inc(norm_ready, 1)

            def softmax(g, j):
                b = g * 2 + j
                dve.wait_ge(score_done, b + 1)
                since(dve, pn_ready, b - 1)
                nc.vector.tensor_tensor(
                    p[:, j].rearrange("p (a h) s -> p a h s", a=4),
                    score_ps[0:S, :, 0:4 * S].rearrange("p a (h s) -> p a h s", h=4),
                    causal[:, None, None, :].broadcast_to([S, 4, 4, S]), ALU.add).then_inc(softmax_step, 1)
                dve.wait_ge(softmax_step, b * 5 + 1)
                nc.vector.tensor_reduce(top[:, j], p[:, j], AX.X, ALU.max).then_inc(softmax_step, 1)
                dve.wait_ge(softmax_step, b * 5 + 2)
                nc.vector.tensor_tensor(p[:, j], p[:, j], top[:, j, :, None].broadcast_to([S, H, S]),
                                        ALU.subtract).then_inc(softmax_step, 1)

            def sums(g, j):
                b = g * 2 + j
                dve.wait_ge(exp_ready, b + 1)
                nc.vector.tensor_reduce(total[:, j], p[:, j], AX.X, ALU.add).then_inc(softmax_step, 1)
                dve.wait_ge(softmax_step, b * 5 + 4)
                nc.vector.reciprocal(inv[:, j], total[:, j]).then_inc(softmax_step, 1)

            def update(g, j):
                b = g * 2 + j
                dve.wait_ge(y_done, b + 1)
                update_x(nc, dve, x, stats, x_new, x_stats, in_ps[0:S, j, 0:D], b, x_step)

            aggregate(nc, dve, stats, mv, mv_step)
            dve.wait_ge(rstd_step, 8)
            norm(0)
            dve.wait_ge(const_w, 32)

            def body(g, first, last):
                softmax(g, 0)
                if not last:
                    norm(g + 1)
                sums(g, 0)
                softmax(g, 1)
                sums(g, 1)
                update(g, 0)
                update(g, 1)
            over_steps(dve, body, G)

        @block.scalar
        def _(act):
            def copy_inputs(g):
                act.wait_ge(inT_done, g * 2 + 1)
                since(act, proj_done, g * 5)
                nc.scalar.activation(x1T[:].rearrange("p c t -> p (c t)"), in_ps[:, 0, 0:KC * PAIR], ACT.Copy
                                     ).then_inc(inT_ready, 1)
                act.wait_ge(inT_done, g * 2 + 2)
                for c in range(KC):
                    done = nc.scalar.activation(x2T[:, c, :], in_ps[:, 1, c * PAIR:(c + 1) * PAIR], ACT.Copy,
                                                scale=gamma[:, 0, c:c + 1])
                done.then_inc(inT_ready, 1)

            def copy_projections(g):
                for i in range(4):
                    act.wait_ge(proj_done, g * 5 + i + 1)
                    if i == 0:
                        since(act, score_done, g * 2)
                    nc.scalar.activation(qT[:, 2 * i:2 * i + 2, :].rearrange("p h t -> p (h t)"),
                                         proj_ps[:, i % 2, 0:2 * PAIR], ACT.Copy).then_inc(proj_ready, 1)
                act.wait_ge(proj_done, g * 5 + 5)
                nc.scalar.activation(kT[:], proj_ps[:, 0, 0:PAIR], ACT.Copy)
                nc.scalar.activation(v_next[:].rearrange("p j d -> p (j d)"), proj_ps[0:S, 0, 256:256 + 2 * DH],
                                     ACT.Copy).then_inc(proj_ready, 1)

            def take_v(g):
                since(act, o_done, g * 2)
                act.wait_ge(proj_ready, g * 5 + 5)
                nc.scalar.activation(v[:], v_next[:], ACT.Copy).then_inc(v_ready, 1)

            def exp(g, j):
                act.wait_ge(softmax_step, (g * 2 + j) * 5 + 3)
                nc.scalar.activation(p[:, j], p[:, j], ACT.Exp, scale=SCALE).then_inc(exp_ready, 1)

            act.wait_ge(const_w, 32)
            copy_inputs(0)
            copy_projections(0)
            take_v(0)

            def body(g, first, last):
                exp(g, 0)
                if not last:
                    copy_inputs(g + 1)
                exp(g, 1)
                if not last:
                    copy_projections(g + 1)
                for j in range(2):
                    b = g * 2 + j
                    act.wait_ge(pT_done, b + 1)
                    since(act, o_done, b)
                    for a in range(2):
                        done = nc.scalar.activation(
                            pT[:, 8 * a:8 * a + 8, :].rearrange("p (a h) s -> p a (h s)", a=2),
                            score_ps[0:S, 2 * a:2 * a + 2, 0:4 * S], ACT.Copy)
                    done.then_inc(pT_ready, 1)
                    act.wait_ge(o_done, b + 1)
                    since(act, y_done, b - 1)
                    nc.scalar.activation(oT[:, j].rearrange("p (a h) s -> p a (h s)", a=2), proj_ps[:, :, 0:4 * S],
                                         ACT.Copy).then_inc(o_ready, 1)
                if not last:
                    take_v(g + 1)
            over_steps(act, body, G)

        @block.tensor
        def _(pe):
            def transpose_inputs(g):
                pe.wait_ge(norm_ready, g * 4 + 4)
                since(pe, x_step, g * 8 - 11)
                for n, src in enumerate((x1, x2)):
                    for c in range(KC):
                        for j in range(2):
                            at = c * PAIR + j * S
                            done = nc.tensor.transpose(in_ps[:, n, at:at + S], src[:, j, c * 128:(c + 1) * 128],
                                                       ident[0:S, 0:S])
                    done.then_inc(inT_done, 1)

            def project(g):
                pe.wait_ge(inT_ready, g * 2 + 2)
                for i in range(4):
                    if i < 2:
                        since(pe, o_ready, g * 2 - 2)
                    else:
                        pe.wait_ge(proj_ready, g * 5 + i - 1)
                    for k in range(2):
                        for c in range(KC):
                            at = (2 * i + k) * 128
                            done = nc.tensor.matmul(proj_ps[:, i % 2, k * PAIR:(k + 1) * PAIR], wq[:, c, at:at + 128],
                                                    x2T[:, c, :], start=(c == 0), stop=(c == KC - 1))
                    done.then_inc(proj_done, 1)
                pe.wait_ge(proj_ready, g * 5 + 3)
                for c in range(KC):
                    nc.tensor.matmul(proj_ps[:, 0, 0:PAIR], wk[:, c, :], x1T[:, c, :], start=(c == 0), stop=(c == KC - 1))
                for j in range(2):
                    for c in range(KC):
                        done = nc.tensor.matmul(proj_ps[0:S, 0, 256 + j * DH:256 + (j + 1) * DH],
                                                x1T[:, c, j * S:(j + 1) * S], wv[:, c, :],
                                                start=(c == 0), stop=(c == KC - 1))
                done.then_inc(proj_done, 1)

            def body(g, first, last):
                pe.wait_ge(proj_ready, g * 5 + 5)
                for j in range(2):
                    b = g * 2 + j
                    if j == 0:
                        since(pe, pT_ready, b)
                    else:
                        pe.wait_ge(softmax_step, b * 5 - 4)
                    for n in range(H):
                        at = (n // HP) * DH
                        done = nc.tensor.matmul(score_ps[0:S, n // 4, (n % 4) * S:(n % 4 + 1) * S],
                                                qT[at:at + DH, n % HP, j * S:(j + 1) * S],
                                                kT[at:at + DH, j * S:(j + 1) * S], start=True, stop=True)
                    done.then_inc(score_done, 1)
                if not last:
                    transpose_inputs(g + 1)
                    project(g + 1)

                def transpose_p(j):
                    b = g * 2 + j
                    if j == 0:
                        pe.wait_ge(softmax_step, b * 5 + 6)
                    else:
                        pe.wait_ge(pT_ready, b)
                    pe.wait_ge(pn_ready, b + 1)
                    for n in range(H):
                        done = nc.tensor.transpose(score_ps[0:S, n // 4, (n % 4) * S:(n % 4 + 1) * S], pn[:, j, n, :],
                                                   ident[0:S, 0:S])
                    done.then_inc(pT_done, 1)

                def weigh_values(j):
                    b = g * 2 + j
                    pe.wait_ge(pT_ready, b + 1)
                    if j == 0:
                        pe.wait_ge(v_ready, g + 1)
                        if not last:
                            pe.wait_ge(proj_ready, g * 5 + 10)
                    else:
                        pe.wait_ge(o_ready, b)
                    for n in range(4):
                        at = (n // 2) * DH
                        done = nc.tensor.matmul(proj_ps[at:at + DH, n % 2, 0:4 * S], v[:, j, :],
                                                pT[:, 4 * n:4 * n + 4, :], start=True, stop=True)
                    done.then_inc(o_done, 1)

                def project_out(j):
                    b = g * 2 + j
                    pe.wait_ge(o_ready, b + 1)
                    if j == 0 and not last:
                        pe.wait_ge(inT_ready, g * 2 + 4)
                    for c in range(HP):
                        done = nc.tensor.matmul(in_ps[0:S, j, 0:D], oT[:, j, c, :], wo[:, c, :],
                                                start=(c == 0), stop=(c == HP - 1))
                    done.then_inc(y_done, 1)

                transpose_p(0)
                weigh_values(0)
                transpose_p(1)
                project_out(0)
                weigh_values(1)
                project_out(1)

            transpose_inputs(0)
            pe.wait_ge(weight_w, 64)
            project(0)
            over_steps(pe, body, G)


def l1_context_mix(nc, x, stats, ident, passed, A):
    HD = 16
    CT, NC = N // 3, 3
    with ExitStack() as ctx:
        ph = Phase(nc, ctx, "l1x")
        wq, wkv, wo = ph.sb("wq", [128, KC, D]), ph.sb("wkv", [128, KC, 2 * D]), ph.sb("wo", [128, KC, D])
        q_bias = ph.sb("q_bias", [128, 1, KC])
        kv_bias, rows = ph.sb("kv_bias", [CT, 2 * D]), ph.sb("rows", [S, 3, D])
        heads = ph.sb("heads", [128, 128])
        mv, half, rstd = ph.sb("mv", [S, B, 2]), ph.sb("half", [S, B]), ph.sb("rstd", [S, B])
        ctxT = ph.sb("ctxT", [128, KC, N])
        masked = ph.sb("masked", [S, MASK_WORDS], U32)
        flag = ph.sb("flag", [S, 1])
        kv, kTv = ph.sb("kv", [CT, NC, 2 * D]), ph.sb("kTv", [128, KC, 128])
        x1, x1T = ph.sb("x1", [S, D]), ph.sb("x1T", [128, KC, S])
        y_in = ph.sb("y_in", [S, D])
        qT, cT = ph.sb("qT", [128, KC, S]), ph.sb("cT", [128, KC, S])
        y, y_stats, y_mv, y_rstd = ph.sb("y", [S, D]), ph.sb("y_stats", [S, 6]), ph.sb("y_mv", [S, 2]), ph.sb("y_rstd", [S, 1])
        y_var = ph.sb("y_var", [S, 1])
        z = ph.sb("z", [S, D])
        x_new, x_stats = ph.sb("x_new", [S, D]), ph.sb("x_stats", [S, 6])

        kv_ps, kTv_ps, xT_ps = ph.banks("kv", 3), ph.banks("kTv", 1), ph.banks("xT", 1)
        qT_ps, cT_ps, o_ps = ph.banks("qT", 1), ph.banks("cT", 1), ph.banks("o", 1)

        weight_w, const_w, ctx_w, mask_w = ph.sem("weight_w"), ph.sem("const_w"), ph.sem("ctx_w"), ph.sem("mask_w")
        mv_step, rstd_step = ph.sem("mv_step"), ph.sem("rstd_step")
        x1_ready, xT_done, xT_ready = ph.sem("x1_ready"), ph.sem("xT_done"), ph.sem("xT_ready")
        kv_done, kv_ready, kTv_done, kTv_ready = ph.sem("kv_done"), ph.sem("kv_ready"), ph.sem("kTv_done"), ph.sem("kTv_ready")
        q_done, q_ready, c_done, c_ready = ph.sem("q_done"), ph.sem("q_ready"), ph.sem("c_done"), ph.sem("c_ready")
        o_done, flag_step, y_step = ph.sem("o_done"), ph.sem("flag_step"), ph.sem("y_step")
        y_rstd_step, z_step, x_step = ph.sem("y_rstd_step"), ph.sem("z_step"), ph.sem("x_step")
        y_in_ready = ph.sem("y_in_ready")

        block = ctx.enter_context(nc.Block())

        @block.sync
        def _(sp):
            def load_context(b):
                sp.dma_start(ctxT[:], A["ctxT"][bass.ds(b, 1)].rearrange("b (c p) n -> p (b c) n", p=128)
                             ).then_inc(ctx_w, 16)

            def load_mask(b):
                sp.dma_start(masked[:], A["score_mask"][bass.ds(b, 1)].rearrange("b s n -> s (b n)")).then_inc(mask_w, 16)

            sp.dma_start(wkv[:], A["l1x_wkv"].rearrange("(c p) n -> p c n", p=128)).then_inc(weight_w, 16)
            load_context(0)
            sp.dma_start(wq[:], A["l1x_wq"].rearrange("(c p) n -> p c n", p=128)).then_inc(weight_w, 16)
            sp.dma_start(wo[:], A["l1x_wo"].rearrange("(c p) n -> p c n", p=128)).then_inc(weight_w, 16)
            sp.dma_start(q_bias[:], A["l1x_q_bias"]).then_inc(const_w, 16)
            sp.dma_start(kv_bias[:], A["l1x_kv_bias"].broadcast_to([CT, 2 * D])).then_inc(const_w, 16)
            sp.dma_start(rows[:], A["l1x_rows"].broadcast_to([S, 3, D])).then_inc(const_w, 16)
            sp.dma_start(heads[:], A["heads"]).then_inc(const_w, 16)
            load_mask(0)
            with sp.Fori(1, B) as b:
                sp.wait_ge(kv_done, b * NC)
                load_context(b)
                sp.wait_ge(flag_step, b * 4 - 3)
                load_mask(b)

        @block.gpsimd
        def _(pool):
            single_rstd(nc, pool, mv, half, rstd, mv_step, rstd_step)

            def body(b, first, last):
                since(pool, x1_ready, b + 1)
                since(pool, y_step, b * 4 - 3)
                nc.gpsimd.tensor_tensor(y_in[:], x1[:], rows[:, 0, :], ALU.add).then_inc(y_in_ready, 1)
                wait_apart(pool, y_step, b * 4 + 3, passed)
                nc.gpsimd.tensor_scalar(y_var[:], y_mv[:, 1:2], LN_EPS, None, ALU.add).then_inc(y_rstd_step, 1)
                pool.wait_ge(y_rstd_step, b * 2 + 1)
                nc.gpsimd.tensor_tensor(y_rstd[:], y_var[:], half[:, 0:1], ALU.pow).then_inc(y_rstd_step, 1)
                pool.wait_ge(y_step, b * 4 + 4)
                since(pool, x_step, b * 4 - 3)
                nc.gpsimd.tensor_tensor(z[:], y[:], rows[:, 1, :], ALU.mult).then_inc(z_step, 1)
                pool.wait_ge(z_step, b * 2 + 1)
                nc.gpsimd.tensor_tensor(z[:], z[:], rows[:, 2, :], ALU.add).then_inc(z_step, 1)
            pool.wait_ge(const_w, 64)
            over_steps(pool, body, B)

        @block.vector
        def _(dve):
            def add_kv_bias(b):
                for t in range(NC):
                    since(dve, kv_done, b * NC + t + 1)
                    if t == 0:
                        since(dve, kTv_done, b)
                    nc.vector.tensor_tensor(kv[:, t, :], kv_ps[0:CT, t, :], kv_bias[:], ALU.add).then_inc(kv_ready, 1)

            def block_diagonal(b):
                since(dve, kTv_done, b + 1)
                since(dve, c_done, b)
                nc.vector.tensor_tensor(kTv[:], kTv_ps[:, 0, 0:KC * 128].rearrange("p (c n) -> p c n", c=KC),
                                        heads[:, None, :].broadcast_to([128, KC, 128]), ALU.mult).then_inc(kTv_ready, 1)

            def norm(b):
                since(dve, xT_done, b)
                since(dve, y_in_ready, b)
                nc.vector.tensor_scalar(x1[:], x[:, b, :], mv[:, b, 0:1], rstd[:, bass.ds(b, 1)],
                                        ALU.subtract, ALU.mult).then_inc(x1_ready, 1)

            def mask_flag(b):
                since(dve, mask_w, b * 16 + 16)
                nc.vector.tensor_reduce(flag[:], masked[:].bitcast(U8)[:, 0:N], AX.X, ALU.max).then_inc(flag_step, 1)
                dve.wait_ge(flag_step, b * 4 + 1)
                nc.vector.tensor_scalar(flag[:], flag[:], -1.0, 1.0, ALU.mult, ALU.add).then_inc(flag_step, 1)
                dve.wait_ge(flag_step, b * 4 + 2)
                nc.vector.reciprocal(flag[:], flag[:]).then_inc(flag_step, 1)
                dve.wait_ge(flag_step, b * 4 + 3)
                nc.vector.tensor_scalar(flag[:], flag[:], 0.0, None, ALU.mult).then_inc(flag_step, 1)

            def add_output(b):
                dve.wait_ge(o_done, b + 1)
                dve.wait_ge(flag_step, b * 4 + 4)
                dve.wait_ge(y_in_ready, b + 1)
                since(dve, z_step, b * 2 - 1)
                nc.vector.scalar_tensor_tensor(y[:], o_ps[0:S, 0, 0:D], flag[:, 0:1], y_in[:], ALU.add, ALU.add
                                               ).then_inc(y_step, 1)
                dve.wait_ge(y_step, b * 4 + 1)
                nc.vector.bn_stats(y_stats[:], y[:]).then_inc(y_step, 1)
                wait_apart(dve, y_step, b * 4 + 2, passed)
                nc.vector.bn_aggr(y_mv[:], y_stats[:]).then_inc(y_step, 1)

            def normalise(b):
                dve.wait_ge(y_rstd_step, b * 2 + 2)
                nc.vector.tensor_scalar(y[:], y[:], y_mv[:, 0:1], y_rstd[:, 0:1], ALU.subtract, ALU.mult
                                        ).then_inc(y_step, 1)

            def update(b):
                dve.wait_ge(z_step, b * 2 + 2)
                update_x(nc, dve, x, stats, x_new, x_stats, z[:], b, x_step)

            aggregate(nc, dve, stats, mv, mv_step)
            dve.wait_ge(rstd_step, 3)
            norm(0)
            dve.wait_ge(const_w, 64)
            add_kv_bias(0)
            block_diagonal(0)

            def body(b, first, last):
                if not first:
                    update(b - 1)
                if not last:
                    norm(b + 1)
                    add_kv_bias(b + 1)
                mask_flag(b)
                add_output(b)
                if not last:
                    block_diagonal(b + 1)
                normalise(b)
            over_steps(dve, body, B)
            update(B - 1)

        @block.scalar
        def _(act):
            act.wait_ge(const_w, 64)

            def body(b, first, last):
                act.wait_ge(xT_done, b + 1)
                nc.scalar.activation(x1T[:].rearrange("p c t -> p (c t)"), xT_ps[:, 0, 0:KC * S], ACT.Copy
                                     ).then_inc(xT_ready, 1)
                act.wait_ge(q_done, b + 1)
                for c in range(KC):
                    done = nc.scalar.activation(qT[:, c, :], qT_ps[:, 0, c * S:(c + 1) * S], ACT.Identity,
                                                bias=q_bias[:, 0, c:c + 1])
                done.then_inc(q_ready, 1)
                act.wait_ge(c_done, b + 1)
                nc.scalar.activation(cT[:].rearrange("p c t -> p (c t)"), cT_ps[:, 0, 0:KC * S], ACT.Copy
                                     ).then_inc(c_ready, 1)
            over_steps(act, body, B)

        @block.tensor
        def _(pe):
            def project_kv(b, t):
                if t == 0:
                    since(pe, ctx_w, b * 16 + 16)
                since(pe, kv_ready, b * NC - NC + t + 1)
                for c in range(KC):
                    done = nc.tensor.matmul(kv_ps[0:CT, t, :], ctxT[:, c, t * CT:(t + 1) * CT], wkv[:, c, :],
                                            start=(c == 0), stop=(c == KC - 1))
                done.then_inc(kv_done, 1)

            def multiply_kTv(b):
                since(pe, kTv_ready, b)
                for c in range(KC):
                    for t in range(NC):
                        since(pe, kv_ready, b * NC + t + 1)
                        done = nc.tensor.matmul(kTv_ps[:, 0, c * 128:(c + 1) * 128], kv[:, t, c * 128:(c + 1) * 128],
                                                kv[:, t, D + c * 128:D + (c + 1) * 128],
                                                start=(t == 0), stop=(t == NC - 1))
                done.then_inc(kTv_done, 1)

            pe.wait_ge(weight_w, 48)
            for t in range(NC):
                project_kv(0, t)
            multiply_kTv(0)

            def body(b, first, last):
                since(pe, x1_ready, b + 1)
                since(pe, xT_ready, b)
                for c in range(KC):
                    done = nc.tensor.transpose(xT_ps[:, 0, c * S:(c + 1) * S], x1[:, c * 128:(c + 1) * 128],
                                               ident[0:S, 0:S])
                done.then_inc(xT_done, 1)
                if not last:
                    project_kv(b + 1, 0)
                pe.wait_ge(xT_ready, b + 1)
                since(pe, q_ready, b)
                for u in range(KC):
                    for c in range(KC):
                        done = nc.tensor.matmul(qT_ps[:, 0, u * S:(u + 1) * S], wq[:, c, u * 128:(u + 1) * 128],
                                                x1T[:, c, :], start=(c == 0), stop=(c == KC - 1))
                done.then_inc(q_done, 1)
                if not last:
                    project_kv(b + 1, 1)
                pe.wait_ge(q_ready, b + 1)
                pe.wait_ge(kTv_ready, b + 1)
                since(pe, c_ready, b)
                for u in range(KC):
                    done = nc.tensor.matmul(cT_ps[:, 0, u * S:(u + 1) * S], kTv[:, u, :], qT[:, u, :],
                                            start=True, stop=True)
                done.then_inc(c_done, 1)
                if not last:
                    project_kv(b + 1, 2)
                pe.wait_ge(c_ready, b + 1)
                since(pe, y_step, b * 4 - 3)
                for u in range(KC):
                    done = nc.tensor.matmul(o_ps[0:S, 0, 0:D], cT[:, u, :], wo[:, u, :],
                                            start=(u == 0), stop=(u == KC - 1))
                done.then_inc(o_done, 1)
                if not last:
                    multiply_kTv(b + 1)
            over_steps(pe, body, B)


def l1_experts(nc, x, stats, ident, passed, A, out):
    E, R, F = 4, 4, 1024
    ER, FC = E * R, F // 128
    GB = 4
    G, GT = B // GB, GB * S
    with ExitStack() as ctx:
        ph = Phase(nc, ctx, "l1f")
        wi, wo = ph.sb("wi", [128, KC, F]), ph.sb("wo", [128, FC, D])
        wg, low_a, low_b = ph.sb("wg", [128, KC, E]), ph.sb("low_a", [128, KC, ER]), ph.sb("low_b", [ER, F])
        bg, expert_no = ph.sb("bg", [S, E]), ph.sb("expert_no", [S, E])
        mv, half, rstd = ph.sb("mv", [S, B, 2]), ph.sb("half", [S, B]), ph.sb("rstd", [S, B])
        x1, x1T = ph.sb("x1", [S, B, D]), ph.sb("x1T", [128, KC, B * S])
        logits, best, best_no = ph.sb("logits", [S, B, 8]), ph.sb("best", [S, B, 8]), ph.sb("best_no", [S, B, 8], U32)
        share, total = ph.sb("share", [S, B, 8]), ph.sb("total", [S, B])
        weight, ratio = ph.sb("weight", [S, B]), ph.sb("ratio", [S, B])
        chosen = ph.sb("chosen", [S, 2, B])
        one_hot = ph.sb("one_hot", [S, 2, B, E, R])
        low = ph.sb("low", [ER, B * S])
        low_first, low_change = ph.sb("low_first", [ER, B * S]), ph.sb("low_change", [ER, B * S])
        ratio_rows = ph.sb("ratio_rows", [128, B * S])
        z_first, z_second = ph.sb("z_first", [128, 4, GT]), ph.sb("z_second", [128, 2, GT])
        h = ph.sb("h", [128, FC, GT])

        result = ph.sb("result", [S, GB, D])

        z_ps, change_ps, y_ps = ph.banks("z", 2), ph.banks("change", 2), ph.banks("y", 2)
        gate_ps, ratio_ps = ph.banks("gate", 1), ph.banks("ratio", 1)

        weight_w, const_w, stored = ph.sem("weight_w"), ph.sem("const_w"), ph.sem("stored")
        mv_step, rstd_step = ph.sem("mv_step"), ph.sem("rstd_step")
        x1_ready, xT_done, xT_ready = ph.sem("x1_ready"), ph.sem("xT_done"), ph.sem("xT_ready")
        gate_done, low_ready, gate_step, exp_ready = ph.sem("gate_done"), ph.sem("low_ready"), ph.sem("gate_step"), ph.sem("exp_ready")
        one_hot_ready, one_hot_done = ph.sem("one_hot_ready"), ph.sem("one_hot_done")
        ratio_done, ratio_ready, masked_ready = ph.sem("ratio_done"), ph.sem("ratio_ready"), ph.sem("masked_ready")
        first_done, first_ready, change_done = ph.sem("first_done"), ph.sem("first_ready"), ph.sem("change_done")
        h_step, y_done, x_step = ph.sem("h_step"), ph.sem("y_done"), ph.sem("x_step")

        block = ctx.enter_context(nc.Block())

        @block.sync
        def _(sp):
            sp.dma_start(wg[:], A["l1f_wg"].rearrange("(c p) n -> p c n", p=128)).then_inc(const_w, 16)
            sp.dma_start(low_a[:], A["l1f_a"].rearrange("(c p) n -> p c n", p=128)).then_inc(const_w, 16)
            sp.dma_start(low_b[:], A["l1f_b"]).then_inc(const_w, 16)
            sp.dma_start(bg[:], A["l1f_bg"].broadcast_to([S, E])).then_inc(const_w, 16)
            sp.dma_start(expert_no[:], A["expert_no"][:, 0:E].broadcast_to([S, E])).then_inc(const_w, 16)
            sp.dma_start(wi[:], A["l1f_wi"].rearrange("(c p) n -> p c n", p=128)).then_inc(weight_w, 16)
            sp.dma_start(wo[:], A["l1f_wo"].rearrange("(c p) n -> p c n", p=128)).then_inc(weight_w, 16)
            with sp.Fori(0, G) as g:
                sp.wait_ge(x_step, g * GB + GB)
                sp.dma_start(out[bass.ds(g * GB, GB)].rearrange("b s d -> s b d"), result[:]).then_inc(stored, 16)
            sp.wait_ge(stored, 16 * G)

        @block.gpsimd
        def _(pool):
            single_rstd(nc, pool, mv, half, rstd, mv_step, rstd_step)

        @block.vector
        def _(dve):
            steps = [0]

            def step(instruction):
                steps[0] += 1
                instruction.then_inc(gate_step, 1)
                dve.wait_ge(gate_step, steps[0])

            aggregate(nc, dve, stats, mv, mv_step)
            dve.wait_ge(rstd_step, 3)
            for b in range(B):
                nc.vector.tensor_scalar(x1[:, b, :], x[:, b, :], mv[:, b, 0:1], rstd[:, b:b + 1],
                                        ALU.subtract, ALU.mult).then_inc(x1_ready, 1)
            nc.vector.memset(logits[:, :, E:8], NEG)
            dve.wait_ge(const_w, 80)
            dve.wait_ge(gate_done, G)
            step(nc.vector.tensor_tensor(logits[:, :, 0:E], gate_ps[0:S, 0, 0:B * E].rearrange("p (b e) -> p b e", e=E),
                                         bg[:, None, :].broadcast_to([S, B, E]), ALU.add))
            for b in range(B):
                nc.vector.max(best[:, b, :], logits[:, b, :]).then_inc(gate_step, 1)
            for b in range(B):
                dve.wait_ge(gate_step, b + 2)
                nc.vector.max_index(best_no[:, b, :], best[:, b, :], logits[:, b, :]).then_inc(gate_step, 1)
            steps[0] += 2 * B
            dve.wait_ge(gate_step, steps[0])
            step(nc.vector.tensor_tensor(share[:], best[:], best[:, :, 0:1].broadcast_to([S, B, 8]), ALU.subtract))
            step(nc.vector.tensor_copy(chosen[:].rearrange("p k b -> p b k"), best_no[:, :, 0:2]))
            step(nc.vector.tensor_tensor(
                one_hot[:].rearrange("p k b e r -> p (k b) e r"),
                expert_no[:, None, :, None].broadcast_to([S, 2 * B, E, R]),
                chosen[:].rearrange("p k b -> p (k b)")[:, :, None, None].broadcast_to([S, 2 * B, E, R]), ALU.is_equal))
            nc.vector.tensor_tensor(one_hot[:, 1], one_hot[:, 1], one_hot[:, 0], ALU.subtract).then_inc(one_hot_ready, 1)
            dve.wait_ge(exp_ready, 1)
            nc.vector.tensor_copy(ratio[:], share[:, :, 1]).then_inc(ratio_ready, 1)
            step(nc.vector.tensor_reduce(total[:], share[:], AX.X, ALU.add))
            step(nc.vector.reciprocal(weight[:], total[:]))
            for g in range(G):
                dve.wait_ge(one_hot_done, g + 1)
                dve.wait_ge(low_ready, g + 1)
                at = g * GT
                nc.vector.tensor_tensor(low_first[:, at:at + GT], low[:, at:at + GT], y_ps[0:ER, 0, 0:GT], ALU.mult)
                nc.vector.tensor_tensor(low_change[:, at:at + GT], low[:, at:at + GT], y_ps[0:ER, 1, 0:GT], ALU.mult
                                        ).then_inc(masked_ready, 1)

            def body(g, first, last):
                for f in range(FC):
                    n = g * FC + f
                    since(dve, h_step, n * 3 - 3)
                    since(dve, first_ready, n + 1)
                    since(dve, change_done, n + 1)
                    if isinstance(g, int) and n == 0:
                        dve.wait_ge(ratio_ready, 1 + G)
                    nc.vector.tensor_tensor(z_second[:, f % 2, :], z_first[:, f % 4, :], change_ps[:, f % 2, 0:GT], ALU.add
                                            ).then_inc(h_step, 1)
                    dve.wait_ge(h_step, n * 3 + 1)
                    nc.vector.scalar_tensor_tensor(z_second[:, f % 2, :], z_second[:, f % 2, :], 0.0, ratio_rows[:, bass.ds(g * GT, GT)],
                                                   ALU.max, ALU.mult).then_inc(h_step, 1)
                    dve.wait_ge(h_step, n * 3 + 2)
                    if f == 0:
                        since(dve, y_done, g * GB)
                    nc.vector.scalar_tensor_tensor(h[:, f, :], z_first[:, f % 4, :], 0.0, z_second[:, f % 2, :], ALU.max, ALU.add
                                                   ).then_inc(h_step, 1)
                for j in range(GB):
                    b = g * GB + j
                    dve.wait_ge(y_done, b + 1)
                    if j == 0:
                        since(dve, stored, g * 16)
                    nc.vector.scalar_tensor_tensor(result[:, j, :], y_ps[0:S, j % 2, 0:D], weight[:, bass.ds(b, 1)],
                                                   x[:, b, :], ALU.mult, ALU.add).then_inc(x_step, 1)
            over_steps(dve, body, G)

        @block.scalar
        def _(act):
            for g in range(G):
                act.wait_ge(xT_done, g + 1)
                nc.scalar.activation(x1T[:, :, g * GT:(g + 1) * GT], (z_ps, change_ps)[g % 2][:, :, 0:GT], ACT.Copy
                                     ).then_inc(xT_ready, 1)
                act.wait_ge(gate_done, g + 1)
                nc.scalar.activation(low[:, g * GT:(g + 1) * GT], y_ps[0:ER, g % 2, 0:GT], ACT.Copy).then_inc(low_ready, 1)
            act.wait_ge(gate_step, 2 * B + 2)
            nc.scalar.activation(share[:], share[:], ACT.Exp).then_inc(exp_ready, 1)
            for g in range(G):
                act.wait_ge(ratio_done, g + 1)
                nc.scalar.activation(ratio_rows[:, g * GT:(g + 1) * GT], ratio_ps[:, 0, 0:GT], ACT.Copy
                                     ).then_inc(ratio_ready, 1)

            def body(g, first, last):
                for f in range(FC):
                    n = g * FC + f
                    since(act, first_done, n + 1)
                    since(act, h_step, n * 3 - 9)
                    nc.scalar.activation(z_first[:, f % 4, :], z_ps[:, f % 2, 0:GT], ACT.Copy).then_inc(first_ready, 1)
            over_steps(act, body, G)

        @block.tensor
        def _(pe):
            pe.wait_ge(const_w, 80)
            for g in range(G):
                pe.wait_ge(x1_ready, (g + 1) * GB)
                if g >= 2:
                    pe.wait_ge(xT_ready, g - 1)
                for c in range(KC):
                    for j in range(GB):
                        done = nc.tensor.transpose((z_ps, change_ps)[g % 2][:, c, j * S:(j + 1) * S],
                                                   x1[:, g * GB + j, c * 128:(c + 1) * 128], ident[0:S, 0:S])
                done.then_inc(xT_done, 1)
                pe.wait_ge(xT_ready, g + 1)
                if g >= 2:
                    pe.wait_ge(low_ready, g - 1)
                for j in range(GB):
                    b = g * GB + j
                    for c in range(KC):
                        nc.tensor.matmul(gate_ps[0:S, 0, b * E:(b + 1) * E], x1T[:, c, b * S:(b + 1) * S], wg[:, c, :],
                                         start=(c == 0), stop=(c == KC - 1))
                for c in range(KC):
                    done = nc.tensor.matmul(y_ps[0:ER, g % 2, 0:GT], low_a[:, c, :], x1T[:, c, g * GT:(g + 1) * GT],
                                            start=(c == 0), stop=(c == KC - 1))
                done.then_inc(gate_done, 1)
            pe.wait_ge(one_hot_ready, 1)
            pe.wait_ge(low_ready, G)
            for g in range(G):
                since(pe, masked_ready, g)
                for k in range(2):
                    for j in range(GB):
                        done = nc.tensor.transpose(y_ps[0:ER, k, j * S:(j + 1) * S],
                                                   one_hot[:, k, g * GB + j].rearrange("p e r -> p (e r)"),
                                                   ident[0:S, 0:S])
                done.then_inc(one_hot_done, 1)
                if g == 0:
                    pe.wait_ge(ratio_ready, 1)
                else:
                    pe.wait_ge(ratio_ready, 1 + g)
                for j in range(GB):
                    done = nc.tensor.matmul(ratio_ps[:, 0, j * S:(j + 1) * S],
                                            ratio[:, g * GB + j:g * GB + j + 1].broadcast_to([S, 128]),
                                            ident[0:S, 0:S], start=True, stop=True)
                done.then_inc(ratio_done, 1)

            def multiply_first(g, f):
                n = g * FC + f
                since(pe, first_ready, n - 1)
                for c in range(KC):
                    nc.tensor.matmul(z_ps[:, f % 2, 0:GT], wi[:, c, f * 128:(f + 1) * 128],
                                     x1T[:, c, bass.ds(g * GT, GT)], start=(c == 0), stop=False)
                nc.tensor.matmul(z_ps[:, f % 2, 0:GT], low_b[:, f * 128:(f + 1) * 128],
                                 low_first[:, bass.ds(g * GT, GT)], start=False, stop=True).then_inc(first_done, 1)

            def multiply_change(g, f):
                n = g * FC + f
                if isinstance(n, int):
                    since(pe, h_step, n * 3 - 5)
                else:
                    wait_apart(pe, h_step, n * 3 - 5, passed)
                nc.tensor.matmul(change_ps[:, f % 2, 0:GT], low_b[:, f * 128:(f + 1) * 128],
                                 low_change[:, bass.ds(g * GT, GT)], start=True, stop=True).then_inc(change_done, 1)

            def body(g, first, last):
                for f in range(FC):
                    multiply_change(g, f)
                    if f + 2 < FC:
                        multiply_first(g, f + 2)
                if not last:
                    multiply_first(g + 1, 0)
                    multiply_first(g + 1, 1)
                for j in range(GB):
                    b = g * GB + j
                    since(pe, x_step, b - 1)
                    for f in range(FC):
                        if j == 0:
                            pe.wait_ge(h_step, (g * FC + f) * 3 + 3)
                        done = nc.tensor.matmul(y_ps[0:S, j % 2, 0:D], h[:, f, j * S:(j + 1) * S], wo[:, f, :],
                                                start=(f == 0), stop=(f == FC - 1))
                    done.then_inc(y_done, 1)

            pe.wait_ge(masked_ready, G)
            pe.wait_ge(weight_w, 32)
            multiply_first(0, 0)
            multiply_first(0, 1)
            over_steps(pe, body, G)


def load_x(nc, x, stats, ident, A):
    with ExitStack() as ctx:
        ph = Phase(nc, ctx, "in")
        loaded, stats_done = ph.sem("loaded"), ph.sem("stats_done")
        block = ctx.enter_context(nc.Block())

        @block.sync
        def _(sp):
            sp.dma_start(x[:], A["x"].rearrange("b s d -> s b d")).then_inc(loaded, 16)
            sp.dma_start(ident[:], A["ident"]).then_inc(loaded, 16)

        @block.vector
        def _(dve):
            dve.wait_ge(loaded, 32)
            for b in range(B):
                nc.vector.bn_stats(stats[:, b, :], x[:, b, :]).then_inc(stats_done, 1)


def program(nc, A, out):
    with ExitStack() as ctx:
        x = ctx.enter_context(nc.sbuf_tensor("x", [S, B, D], F32))
        stats = ctx.enter_context(nc.sbuf_tensor("stats", [S, B, 6], F32))
        ident = ctx.enter_context(nc.sbuf_tensor("ident", [128, 128], F32))
        passed = ctx.enter_context(nc.semaphore("passed"))
        load_x(nc, x, stats, ident, A)
        l0_attention(nc, x, stats, ident, passed, A)
        l0_cross_attention(nc, x, stats, ident, passed, A)
        l0_experts(nc, x, stats, ident, passed, A)
        l1_attention(nc, x, stats, ident, passed, A)
        l1_context_mix(nc, x, stats, ident, passed, A)
        l1_experts(nc, x, stats, ident, passed, A, out)


def constants():
    dim = 128
    pos = np.arange(S, dtype=np.float32)[:, None]
    inv_freq = np.exp(-np.log(np.float32(10000.0)) * (np.arange(0, dim, 2, dtype=np.float32) / np.float32(dim)))
    ang = (pos * inv_freq[None, :]).astype(np.float32)
    pe = np.zeros((S, dim), np.float32)
    pe[:, 0::2], pe[:, 1::2] = np.sin(ang), np.cos(ang)
    causal = np.where(np.tril(np.ones((S, S), bool)), np.float32(0), np.float32(NEG))
    return {"pos_q": pe.T, "pos_k": pe[0:1].T, "causal": causal, "ident": np.eye(128, dtype=np.float32),
            "before": np.triu(np.ones((S, S), np.float32), 1), "expert_no": np.arange(8, dtype=np.float32)[None],
            "heads": np.kron(np.eye(8, dtype=np.float32), np.full((16, 16), 0.25, np.float32)),
            "tile_no": np.arange((B * S + 8 * 127) // 128, dtype=np.float32)[None]}


def by_feature(*vectors):
    return np.stack(vectors).reshape(len(vectors), KC, 128).transpose(2, 0, 1)


def mask_words(mask):
    pad = [(0, 0)] * (mask.ndim - 1) + [(0, 4 * MASK_WORDS - N)]
    return np.pad(mask, pad).view(np.uint32)


def kernel(**inputs):
    from concourse import bacc
    from concourse.bass_utils import run_bass_kernel_spmd

    i = {k: np.asarray(v) for k, v in inputs.items()}
    arrays = {
        "x": i["x"],
        "l0a_wq": i["L0_attn_Wq"].T, "l0a_wk": i["L0_attn_Wk"].T, "l0a_wv": i["L0_attn_Wv"].T,
        "l0a_wo": i["L0_attn_Wo"].T,
        "l0x_wq": i["L0_xattn_Wq"], "l0x_wkv": i["L0_xattn_Wkv"], "l0x_wout": i["L0_xattn_Wout"],
        "l0x_affine": by_feature(i["L0_xattn_g1"], i["L0_xattn_b1"], i["L0_xattn_g2"], i["L0_xattn_b2"]),
        "ctx": i["ctx_1024"], "ctx_mask": mask_words(i["mask_BxS2_bk0"]),
        "l0f_w1": i["L0_ffn_W1"], "l0f_wr": i["L0_ffn_Wr"].T, "l0f_wo": i["L0_ffn_Wo"],
        "l0f_b1": i["L0_ffn_b1"].reshape(1, -1),
        "l0f_rows": np.stack([i["L0_ffn_bo"], i["L0_ffn_gamma"], i["L0_ffn_beta"]])[None],
        "l1a_wq": i["L1_attn_Wq"], "l1a_wk": np.concatenate([i["L1_attn_Wkv"][:, :64]] * 2, 1),
        "l1a_wv": i["L1_attn_Wkv"][:, 64:], "l1a_wo": i["L1_attn_Wo"], "l1a_gamma": by_feature(i["L1_attn_gamma"]),
        "l1x_wq": i["L1_xattn_wq_w"].T, "l1x_wo": i["L1_xattn_wo_w"].T,
        "l1x_wkv": np.concatenate([i["L1_xattn_wk_w"], i["L1_xattn_wv_w"]]).T,
        "l1x_q_bias": by_feature(i["L1_xattn_wq_b"]),
        "l1x_kv_bias": np.concatenate([i["L1_xattn_wk_b"], i["L1_xattn_wv_b"]])[None],
        "l1x_rows": np.stack([i["L1_xattn_wo_b"], i["L1_xattn_ln_g"], i["L1_xattn_ln_b"]])[None],
        "l1f_wi": i["L1_ffn_Wi"].T, "l1f_wo": i["L1_ffn_Wo"].T, "l1f_wg": i["L1_ffn_Wg"].T,
        "l1f_a": i["L1_ffn_A"].reshape(-1, D).T, "l1f_b": i["L1_ffn_B"].transpose(0, 2, 1).reshape(-1, 1024),
        "l1f_bg": i["L1_ffn_bg"][None],
        "ctxT": i["ctx_1024"].transpose(0, 2, 1), "score_mask": mask_words(i["mask_Bx1xSxS2_bf0"][:, 0]),
        **constants(),
    }
    arrays = {k: np.ascontiguousarray(v) for k, v in arrays.items()}
    nc = bacc.Bacc("TRN2", target_bir_lowering=False, num_devices=1)
    A = {k: nc.dram_tensor(f"in_{k}", v.shape, mybir.dt.from_np(v.dtype), kind="ExternalInput").ap()
         for k, v in arrays.items()}
    out = nc.dram_tensor("out", (B, S, D), F32, kind="ExternalOutput").ap()
    program(nc, A, out)
    r = run_bass_kernel_spmd(nc, [{f"in_{k}": v for k, v in arrays.items()}], core_ids=[0])
    return r.results[0]["out"]
```

```python
from contextlib import ExitStack

import numpy as np

import concourse.bass as bass
from concourse import mybir

F32 = mybir.dt.float32
F32R = mybir.dt.float32r
U8 = mybir.dt.uint8
U32 = mybir.dt.uint32
ALU = mybir.AluOpType
ACT = mybir.ActivationFunctionType
AX = mybir.AxisListType

B, S, D, N = 16, 112, 256, 375
KC = D // 128
MASK_WORDS = -(-N // 4)
LOW_ROWS = 80
PAIR = 2 * S
NEG = -3.0e38
LN_EPS = 1e-5
SORTED_TILES = (B * S + 8 * 127) // 128


def since(eng, sem, value):
    if isinstance(value, int) and value <= 0:
        return
    eng.wait_ge(sem, value)


def over_steps(eng, body, count):
    body(0, first=True, last=False)
    if count > 2:
        with eng.Fori(1, count - 1) as i:
            body(i, first=False, last=False)
    body(count - 1, first=False, last=True)


class Phase:

    def __init__(self, nc, ctx, name):
        self.nc, self.ctx, self.name = nc, ctx, name

    def sb(self, name, shape, dt=F32):
        return self.ctx.enter_context(self.nc.sbuf_tensor(f"{self.name}_{name}", shape, dt))

    def banks(self, name, n):
        return self.ctx.enter_context(self.nc.psum_tensor(f"{self.name}_{name}_ps", [128, n, 512], F32))

    def sem(self, name):
        return self.ctx.enter_context(self.nc.semaphore(f"{self.name}_{name}"))


def wait_apart(eng, sem, value, passed):
    since(eng, sem, value)
    eng.sem_inc(passed, 1)


def update_x(nc, dve, x, stats, x_new, x_stats, y, b, x_step):
    nc.vector.tensor_tensor(x_new[:], x[:, b, :], y, ALU.add).then_inc(x_step, 1)
    dve.wait_ge(x_step, b * 4 + 1)
    nc.vector.bn_stats(x_stats[:], x_new[:]).then_inc(x_step, 1)
    nc.vector.tensor_scalar(x[:, b, :], x_new[:], 1.0, None, ALU.mult).then_inc(x_step, 1)
    dve.wait_ge(x_step, b * 4 + 3)
    nc.vector.tensor_scalar(stats[:, b, :], x_stats[:], 1.0, None, ALU.mult).then_inc(x_step, 1)


def aggregate(nc, dve, stats, mv, mv_step):
    for b in range(B):
        nc.vector.bn_aggr(mv[:, b, :], stats[:, b, :]).then_inc(mv_step, 1)


def single_rstd(nc, pool, mv, half, rstd, mv_step, rstd_step):
    nc.gpsimd.memset(half[:], -0.5).then_inc(rstd_step, 1)
    pool.wait_ge(mv_step, B)
    nc.gpsimd.tensor_scalar(rstd[:], mv[:, :, 1], LN_EPS, None, ALU.add).then_inc(rstd_step, 1)
    pool.wait_ge(rstd_step, 2)
    nc.gpsimd.tensor_tensor(rstd[:], rstd[:], half[0:S, :], ALU.pow).then_inc(rstd_step, 1)


def double_rstd(nc, pool, mv, half, rstd, rvar, rstd2, mv_step, rstd_step):
    nc.gpsimd.memset(half[:], -0.5).then_inc(rstd_step, 1)
    pool.wait_ge(mv_step, B)
    nc.gpsimd.tensor_scalar(rvar[:], mv[:, :, 1], LN_EPS, None, ALU.add).then_inc(rstd_step, 1)
    pool.wait_ge(rstd_step, 2)
    nc.gpsimd.tensor_tensor(rstd[:], rvar[:], half[0:S, :], ALU.pow).then_inc(rstd_step, 1)
    pool.wait_ge(rstd_step, 3)
    nc.gpsimd.tensor_tensor(rvar[:], mv[:, :, 1], rstd[:], ALU.mult).then_inc(rstd_step, 1)
    pool.wait_ge(rstd_step, 4)
    nc.gpsimd.tensor_tensor(rvar[:], rvar[:], rstd[:], ALU.mult).then_inc(rstd_step, 1)
    pool.wait_ge(rstd_step, 5)
    nc.gpsimd.tensor_scalar(rvar[:], rvar[:], LN_EPS, None, ALU.add).then_inc(rstd_step, 1)
    pool.wait_ge(rstd_step, 6)
    nc.gpsimd.tensor_tensor(rstd2[:], rvar[:], half[0:S, :], ALU.pow).then_inc(rstd_step, 1)
    pool.wait_ge(rstd_step, 7)
    nc.gpsimd.tensor_tensor(rstd2[:], rstd2[:], rstd[:], ALU.mult).then_inc(rstd_step, 1)


def l0_attention(nc, x, stats, ident, passed, A):
    H, DH = 8, 128
    SCALE = float(DH) ** -0.5
    G = B // 2
    with ExitStack() as ctx:
        ph = Phase(nc, ctx, "l0a")
        wq, wk, wv = ph.sb("wq", [128, KC, H * DH]), ph.sb("wk", [128, KC, DH]), ph.sb("wv", [128, KC, DH])
        wo = ph.sb("wo", [128, H, D])
        pos_q, pos_k = ph.sb("pos_q", [DH, S]), ph.sb("pos_k", [DH, 1])
        causal = ph.sb("causal", [S, S])
        rstd = ph.sb("rstd", [S, B])
        half = ph.sb("half", [S, B])
        xn = ph.sb("xn", [S, 2, D])
        xT = ph.sb("xT", [128, KC, PAIR])
        qT, kT = ph.sb("qT", [DH, H, PAIR]), ph.sb("kT", [DH, PAIR])
        v = ph.sb("v", [S, 2, DH])
        p = ph.sb("p", [S, 2, H, S])
        pn = ph.sb("pn", [S, 2, H, S])
        pT = ph.sb("pT", [S, 2, H, S])
        oT = ph.sb("oT", [DH, 2, H, S])
        top, shift = ph.sb("top", [S, 2, H]), ph.sb("shift", [S, 2, H])
        total, inv = ph.sb("total", [S, 2, H]), ph.sb("inv", [S, 2, H])
        mv = ph.sb("mv", [S, B, 2])
        x_new, x_stats = ph.sb("x_new", [S, D]), ph.sb("x_stats", [S, 6])

        score_ps = [ph.banks("score0", 2), ph.banks("score1", 2)]
        q_ps = ph.banks("q", 2)
        v_ps, xT_ps = ph.banks("v", 1), ph.banks("xT", 1)

        weight_w = ph.sem("weight_w")
        mv_step, rstd_step = ph.sem("mv_step"), ph.sem("rstd_step")
        xn_ready, xT_done, xT_ready = ph.sem("xn_ready"), ph.sem("xT_done"), ph.sem("xT_ready")
        q_done, q_ready, k_ready = ph.sem("q_done"), ph.sem("q_ready"), ph.sem("k_ready")
        v_done, v_ready = ph.sem("v_done"), ph.sem("v_ready")
        score_done, softmax_step, exp_ready = ph.sem("score_done"), ph.sem("softmax_step"), ph.sem("exp_ready")
        pn_ready, pT_done, pT_ready = ph.sem("pn_ready"), ph.sem("pT_done"), ph.sem("pT_ready")
        o_done, o_ready, y_done, x_step = ph.sem("o_done"), ph.sem("o_ready"), ph.sem("y_done"), ph.sem("x_step")

        block = ctx.enter_context(nc.Block())

        @block.sync
        def _(sp):
            sp.dma_start(wq[:], A["l0a_wq"].rearrange("(c p) n -> p c n", p=128)).then_inc(weight_w, 16)
            sp.dma_start(wk[:], A["l0a_wk"].rearrange("(c p) n -> p c n", p=128)).then_inc(weight_w, 16)
            sp.dma_start(wv[:], A["l0a_wv"].rearrange("(c p) n -> p c n", p=128)).then_inc(weight_w, 16)
            sp.dma_start(wo[:], A["l0a_wo"].rearrange("(h p) n -> p h n", p=128)).then_inc(weight_w, 16)
            sp.dma_start(pos_q[:], A["pos_q"]).then_inc(weight_w, 16)
            sp.dma_start(pos_k[:], A["pos_k"]).then_inc(weight_w, 16)
            sp.dma_start(causal[:], A["causal"]).then_inc(weight_w, 16)

        @block.gpsimd
        def _(pool):
            single_rstd(nc, pool, mv, half, rstd, mv_step, rstd_step)

            def body(g, first, last):
                for j in range(2):
                    b = g * 2 + j
                    pool.wait_ge(softmax_step, b * 4 + 4)
                    since(pool, pT_done, b - 1)
                    nc.gpsimd.tensor_tensor(pn[:, j], p[:, j], inv[:, j, :, None].broadcast_to([S, H, S]),
                                            ALU.mult).then_inc(pn_ready, 1)
            over_steps(pool, body, G)

        @block.vector
        def _(dve):
            def norm(g):
                for j in range(2):
                    b = g * 2 + j
                    if j == 0:
                        since(dve, xT_done, g)
                    nc.vector.tensor_scalar(xn[:, j], x[:, b, :], mv[:, b, 0:1], rstd[:, bass.ds(b, 1)],
                                            ALU.subtract, ALU.mult).then_inc(xn_ready, 1)

            def q_add(g, i):
                dve.wait_ge(q_done, g * 5 + i + 1)
                if i == 0:
                    since(dve, score_done, g * 2)
                nc.vector.tensor_tensor(
                    qT[:, 2 * i:2 * i + 2, :].rearrange("p h (j t) -> p (h j) t", j=2),
                    q_ps[:, i % 2, 0:2 * PAIR].rearrange("p (a t) -> p a t", t=S),
                    pos_q[:, None, :].broadcast_to([DH, 4, S]), ALU.add).then_inc(q_ready, 1)

            def softmax(g, j):
                b = g * 2 + j
                dve.wait_ge(score_done, b + 1)
                since(dve, pn_ready, b - 1)
                pj = p[:, j].rearrange("p (a h) s -> p a h s", a=2)
                for a in range(2):
                    last = nc.vector.tensor_tensor(
                        pj[:, a], score_ps[j][0:S, a, 0:4 * S].rearrange("p (h s) -> p h s", h=4),
                        causal[:, None, :].broadcast_to([S, 4, S]), ALU.add)
                last.then_inc(softmax_step, 1)
                dve.wait_ge(softmax_step, b * 4 + 1)
                nc.vector.tensor_reduce(top[:, j], p[:, j], AX.X, ALU.max).then_inc(softmax_step, 1)
                dve.wait_ge(softmax_step, b * 4 + 2)
                nc.vector.tensor_scalar(shift[:, j], top[:, j], -SCALE, None, ALU.mult).then_inc(softmax_step, 1)

            def invert_sums(g, j):
                b = g * 2 + j
                dve.wait_ge(exp_ready, b + 1)
                since(dve, pn_ready, b - 1)
                nc.vector.reciprocal(inv[:, j], total[:, j]).then_inc(softmax_step, 1)

            def update(g, j):
                b = g * 2 + j
                dve.wait_ge(y_done, b + 1)
                update_x(nc, dve, x, stats, x_new, x_stats, score_ps[j][0:S, 0, 0:D], b, x_step)

            aggregate(nc, dve, stats, mv, mv_step)
            dve.wait_ge(rstd_step, 3)
            norm(0)
            dve.wait_ge(weight_w, 112)
            for i in range(H // 2):
                q_add(0, i)

            def body(g, first, last):
                if not last:
                    norm(g + 1)
                softmax(g, 0)
                if not last:
                    q_add(g + 1, 0)
                invert_sums(g, 0)
                softmax(g, 1)
                if not last:
                    q_add(g + 1, 1)
                    q_add(g + 1, 2)
                invert_sums(g, 1)
                if not last:
                    q_add(g + 1, 3)
                update(g, 0)
                update(g, 1)
            over_steps(dve, body, G)

        @block.scalar
        def _(act):
            def copy_xT(g):
                act.wait_ge(xT_done, g + 1)
                since(act, v_done, g)
                nc.scalar.activation(xT[:], xT_ps[:, 0, 0:KC * PAIR].rearrange("p (c t) -> p c t", c=KC),
                                     ACT.Copy).then_inc(xT_ready, 1)

            def add_k(g):
                act.wait_ge(q_done, g * 5 + 5)
                since(act, score_done, g * 2)
                nc.scalar.activation(kT[:], q_ps[:, 0, 0:PAIR], ACT.Identity, bias=pos_k[:, 0:1]).then_inc(k_ready, 1)

            def exp(g, j):
                act.wait_ge(softmax_step, (g * 2 + j) * 4 + 3)
                for h in range(H):
                    done = nc.scalar.activation(p[:, j, h, :], p[:, j, h, :], ACT.Exp, scale=SCALE,
                                                bias=shift[:, j, h:h + 1], accum_out=total[:, j, h:h + 1])
                done.then_inc(exp_ready, 1)

            def body(g, first, last):
                act.wait_ge(v_done, g + 1)
                since(act, o_done, g * 2)
                nc.scalar.activation(v[:], v_ps[0:S, 0, 0:2 * DH].rearrange("p (j d) -> p j d", j=2),
                                     ACT.Copy).then_inc(v_ready, 1)
                if not last:
                    copy_xT(g + 1)
                exp(g, 0)
                exp(g, 1)
                if not last:
                    add_k(g + 1)
                for j in range(2):
                    b = g * 2 + j
                    act.wait_ge(pT_done, b + 1)
                    since(act, o_done, b - 1)
                    nc.scalar.activation(pT[:, j].rearrange("p (a h) s -> p a (h s)", a=2),
                                         score_ps[j][0:S, :, 0:4 * S], ACT.Copy).then_inc(pT_ready, 1)
                for j in range(2):
                    b = g * 2 + j
                    act.wait_ge(o_done, b + 1)
                    since(act, y_done, b - 1)
                    for a in range(2):
                        bank = q_ps[:, a, :] if j == 0 else (v_ps, xT_ps)[a][:, 0, :]
                        done = nc.scalar.activation(oT[:, j].rearrange("p (a h) s -> p a (h s)", a=2)[:, a],
                                                    bank[:, 0:4 * S], ACT.Copy)
                    done.then_inc(o_ready, 1)

            act.wait_ge(weight_w, 112)
            copy_xT(0)
            add_k(0)
            over_steps(act, body, G)

        @block.tensor
        def _(pe):
            def transpose_x(g):
                pe.wait_ge(xn_ready, g * 2 + 2)
                since(pe, o_ready, g * 2 - 2)
                for c in range(KC):
                    for j in range(2):
                        at = c * PAIR + j * S
                        done = nc.tensor.transpose(xT_ps[:, 0, at:at + S], xn[:, j, c * 128:(c + 1) * 128],
                                                   ident[0:S, 0:S])
                done.then_inc(xT_done, 1)

            def project_qk(g):
                pe.wait_ge(xT_ready, g + 1)
                if isinstance(g, int) and g == 0:
                    pe.wait_ge(weight_w, 112)
                for i in range(H // 2 + 1):
                    n = g * 5 + i
                    if i < 2:
                        since(pe, o_ready, g * 2 - 2)
                    else:
                        pe.wait_ge(q_ready, g * 4 + i - 1)
                    for k in range(2 if i < H // 2 else 1):
                        for c in range(KC):
                            w = wq[:, c, (2 * i + k) * DH:(2 * i + k + 1) * DH] if i < H // 2 else wk[:, c, :]
                            done = nc.tensor.matmul(q_ps[:, i % 2, k * PAIR:(k + 1) * PAIR], w, xT[:, c, :],
                                                    start=(c == 0), stop=(c == KC - 1))
                    done.then_inc(q_done, 1)

            def body(g, first, last):
                for j in range(2):
                    if j == 0:
                        pe.wait_ge(q_ready, g * 4 + 4)
                        pe.wait_ge(k_ready, g + 1)
                    b = g * 2 + j
                    since(pe, x_step, b * 4 - 7)
                    for h in range(H):
                        done = nc.tensor.matmul(score_ps[j][0:S, h // 4, (h % 4) * S:(h % 4 + 1) * S],
                                                qT[:, h, j * S:(j + 1) * S], kT[:, j * S:(j + 1) * S],
                                                start=True, stop=True)
                    done.then_inc(score_done, 1)
                since(pe, o_ready, g * 2)
                for j in range(2):
                    for c in range(KC):
                        done = nc.tensor.matmul(v_ps[0:S, 0, j * DH:(j + 1) * DH], xT[:, c, j * S:(j + 1) * S],
                                                wv[:, c, :], start=(c == 0), stop=(c == KC - 1))
                done.then_inc(v_done, 1)
                if not last:
                    transpose_x(g + 1)
                    project_qk(g + 1)
                for j in range(2):
                    b = g * 2 + j
                    pe.wait_ge(pn_ready, b + 1)
                    for h in range(H):
                        done = nc.tensor.transpose(score_ps[j][0:S, h // 4, (h % 4) * S:(h % 4 + 1) * S],
                                                   pn[:, j, h, :], ident[0:S, 0:S])
                    done.then_inc(pT_done, 1)
                for j in range(2):
                    b = g * 2 + j
                    pe.wait_ge(pT_ready, b + 1)
                    if j == 0:
                        pe.wait_ge(v_ready, g + 1)
                        if not last:
                            pe.wait_ge(k_ready, g + 2)
                            pe.wait_ge(q_ready, g * 4 + 8)
                    elif not last:
                        pe.wait_ge(xT_ready, g + 2)
                    for a in range(2):
                        bank = q_ps[:, a, :] if j == 0 else (v_ps, xT_ps)[a][:, 0, :]
                        done = nc.tensor.matmul(bank[:, 0:4 * S], v[:, j, :],
                                                pT[:, j, 4 * a:4 * a + 4, :], start=True, stop=True)
                    done.then_inc(o_done, 1)
                for j in range(2):
                    b = g * 2 + j
                    pe.wait_ge(o_ready, b + 1)
                    for h in range(H):
                        done = nc.tensor.matmul(score_ps[j][0:S, 0, 0:D], oT[:, j, h, :], wo[:, h, :],
                                                start=(h == 0), stop=(h == H - 1))
                    done.then_inc(y_done, 1)

            transpose_x(0)
            project_qk(0)
            over_steps(pe, body, G)


def l0_cross_attention(nc, x, stats, ident, passed, A):
    H, DH = 16, 64
    INNER = H * DH
    NC, CT = 3, N // 3
    KEYS = 488
    KT = KEYS // 4
    SCALE = float(DH) ** -0.5
    with ExitStack() as ctx:
        ph = Phase(nc, ctx, "l0x")
        wq, wkv = ph.sb("wq", [128, KC, INNER]), ph.sb("wkv", [128, KC, 2 * INNER])
        wout = ph.sb("wout", [128, INNER // 128, D])
        affine = ph.sb("affine", [128, 4, KC])
        mv, half = ph.sb("mv", [S, B, 2]), ph.sb("half", [128, B])
        rstd, rvar, rstd2 = ph.sb("rstd", [S, B]), ph.sb("rvar", [S, B]), ph.sb("rstd2", [S, B])
        c_in, c_norm = ph.sb("c_in", [CT, NC, D]), ph.sb("c_norm", [CT, NC, D])
        c_stats, c_mv = ph.sb("c_stats", [CT, NC, 6]), ph.sb("c_mv", [CT, NC, 2])
        c_var, c_rstd = ph.sb("c_var", [CT, NC]), ph.sb("c_rstd", [CT, NC])
        lat, zeros = ph.sb("lat", [S, D]), ph.sb("zeros", [128, D])
        mask_in, bias = ph.sb("mask_in", [S, MASK_WORDS], U32), ph.sb("bias", [S, KEYS])
        wkv_hi, wkv_lo = ph.sb("wkv_hi", [128, KC, 2 * INNER], F32R), ph.sb("wkv_lo", [128, KC, 2 * INNER], F32R)
        kvT = ph.sb("kvT", [128, KC, KEYS])
        kvT_hi, kvT_lo = ph.sb("kvT_hi", [128, KC, KEYS], F32R), ph.sb("kvT_lo", [128, KC, KEYS], F32R)
        q_hi, q_lo = ph.sb("q_hi", [128, 2, H // 2, S], F32R), ph.sb("q_lo", [128, 2, H // 2, S], F32R)
        kT_hi, kT_lo = ph.sb("kT_hi", [128, H // 2, KEYS], F32R), ph.sb("kT_lo", [128, H // 2, KEYS], F32R)
        v = ph.sb("v", [KT, 4, INNER])
        s_sb, p = ph.sb("s", [S, 2, KEYS]), ph.sb("p", [S, 3, KEYS])
        low, total = ph.sb("low", [S, H]), ph.sb("total", [S, H])
        inv, inv_total = ph.sb("inv", [S, 2]), ph.sb("inv_total", [S, 2, S])
        pT = ph.sb("pT", [KT, 2, 4 * S])
        oT = ph.sb("oT", [128, INNER // 128, S])
        x_new, x_stats = ph.sb("x_new", [S, D]), ph.sb("x_stats", [S, 6])

        score_ps, pT_ps, oT_ps = ph.banks("score", 2), ph.banks("pT", 2), ph.banks("oT", 2)
        proj_ps = ph.banks("proj", 2)

        weight_w, const_w, ctx_w, mask_w = ph.sem("weight_w"), ph.sem("const_w"), ph.sem("ctx_w"), ph.sem("mask_w")
        mv_step, rstd_step, zeroed = ph.sem("mv_step"), ph.sem("rstd_step"), ph.sem("zeroed")
        padded = ph.sem("padded")
        c_step, c_rstd_step = ph.sem("c_step"), ph.sem("c_rstd_step")
        norm_ready, bias_ready = ph.sem("norm_ready"), ph.sem("bias_ready")
        proj_done, kvT_ready = ph.sem("proj_done"), ph.sem("kvT_ready")
        v_even_ready, v_odd_ready = ph.sem("v_even_ready"), ph.sem("v_odd_ready")
        score_done, masked_ready, exp_ready = ph.sem("score_done"), ph.sem("masked_ready"), ph.sem("exp_ready")
        pT_done, pT_even_ready, pT_odd_ready = ph.sem("pT_done"), ph.sem("pT_even_ready"), ph.sem("pT_odd_ready")
        pv_done, inv_step = ph.sem("pv_done"), ph.sem("inv_step")
        oT_even_ready, oT_odd_ready = ph.sem("oT_even_ready"), ph.sem("oT_odd_ready")
        act_start, w_lo_ready = ph.sem("act_start"), ph.sem("w_lo_ready")
        hi_ready, lo_ready = ph.sem("hi_ready"), ph.sem("lo_ready")
        y_done, x_step = ph.sem("y_done"), ph.sem("x_step")

        T0, Q0, K0, V0, USES = 0, 2, 4, 12, 20
        SPLIT_Q, SPLIT_K, SPLITS = 2, 4, 12
        PARTS = [(c, slice(n * INNER, (n + 1) * INNER)) for n in range(2) for c in range(KC)]

        def key_bank(i):
            return (proj_ps, score_ps)[i // 2 % 2][:, i % 2, 0:KEYS]

        block = ctx.enter_context(nc.Block())

        @block.sync
        def _(sp):
            sp.dma_start(affine[:], A["l0x_affine"]).then_inc(const_w, 16)
            def load_ctx(b):
                sp.dma_start(c_in[:], A["ctx"][bass.ds(b, 1)].rearrange("b (c p) d -> p (b c) d", p=CT)
                             ).then_inc(ctx_w, 16)
                sp.dma_start(mask_in[:], A["ctx_mask"][bass.ds(b, 1), :].broadcast_to([S, MASK_WORDS])).then_inc(mask_w, 16)

            load_ctx(0)
            sp.dma_start(wq[:], A["l0x_wq"].rearrange("(c p) n -> p c n", p=128)).then_inc(weight_w, 16)
            sp.dma_start(wkv[:], A["l0x_wkv"].rearrange("(c p) n -> p c n", p=128)).then_inc(weight_w, 16)
            sp.dma_start(wout[:], A["l0x_wout"].rearrange("(c p) n -> p c n", p=128)).then_inc(weight_w, 16)
            sp.wait_ge(zeroed, 5)
            sp.dma_start(A["sorted_x"].rearrange("(t p) d -> p t d", p=128),
                         zeros[:, None, :].broadcast_to([128, SORTED_TILES + 1, D])).then_inc(padded, 16)
            with sp.Fori(1, B) as b:
                sp.wait_ge(norm_ready, b * 4)
                sp.wait_ge(bias_ready, b)
                load_ctx(b)
            sp.wait_ge(padded, 16)

        @block.gpsimd
        def _(pool):
            nc.gpsimd.memset(half[:], -0.5).then_inc(zeroed, 1)
            nc.gpsimd.memset(kvT[:, :, N + S:KEYS], 0.0).then_inc(zeroed, 1)
            nc.gpsimd.memset(bias[:, N:N + S], 0.0).then_inc(zeroed, 1)
            nc.gpsimd.memset(bias[:, N + S:KEYS], NEG).then_inc(zeroed, 1)
            nc.gpsimd.memset(zeros[:], 0.0).then_inc(zeroed, 1)

            def context_rstd(b):
                since(pool, norm_ready, b * 4)
                wait_apart(pool, c_step, b * 6 + 6, passed)
                nc.gpsimd.tensor_scalar(c_var[:], c_mv[:, :, 1], LN_EPS, None, ALU.add).then_inc(c_rstd_step, 1)
                pool.wait_ge(c_rstd_step, b * 2 + 1)
                nc.gpsimd.tensor_tensor(c_rstd[:], c_var[:], half[0:CT, 0:NC], ALU.pow).then_inc(c_rstd_step, 1)

            def mask_bias(b):
                since(pool, mask_w, b * 16 + 16)
                wait_apart(pool, masked_ready, b * H, passed)
                nc.gpsimd.tensor_scalar(bias[:, 0:N], mask_in[:].bitcast(U8)[:, 0:N], 1.0, -NEG, ALU.subtract, ALU.mult
                                        ).then_inc(bias_ready, 1)

            pool.wait_ge(zeroed, 5)
            context_rstd(0)
            pool.wait_ge(mv_step, B)
            nc.gpsimd.tensor_scalar(rvar[:], mv[:, :, 1], LN_EPS, None, ALU.add).then_inc(rstd_step, 1)
            pool.wait_ge(rstd_step, 1)
            nc.gpsimd.tensor_tensor(rstd[:], rvar[:], half[0:S, :], ALU.pow).then_inc(rstd_step, 1)
            pool.wait_ge(rstd_step, 2)
            nc.gpsimd.tensor_tensor(rvar[:], mv[:, :, 1], rstd[:], ALU.mult).then_inc(rstd_step, 1)
            pool.wait_ge(rstd_step, 3)
            nc.gpsimd.tensor_tensor(rvar[:], rvar[:], rstd[:], ALU.mult).then_inc(rstd_step, 1)
            pool.wait_ge(rstd_step, 4)
            nc.gpsimd.tensor_scalar(rvar[:], rvar[:], LN_EPS, None, ALU.add).then_inc(rstd_step, 1)
            pool.wait_ge(rstd_step, 5)
            nc.gpsimd.tensor_tensor(rstd2[:], rvar[:], half[0:S, :], ALU.pow).then_inc(rstd_step, 1)
            pool.wait_ge(rstd_step, 6)
            nc.gpsimd.tensor_tensor(rstd2[:], rstd2[:], rstd[:], ALU.mult).then_inc(rstd_step, 1)
            mask_bias(0)
            with pool.Fori(1, B) as b:
                context_rstd(b)
                mask_bias(b)

        @block.vector
        def _(dve):
            def context_stats(b):
                dve.wait_ge(ctx_w, b * 16 + 16)
                for t in range(NC):
                    nc.vector.bn_stats(c_stats[:, t, :], c_in[:, t, :]).then_inc(c_step, 1)
                for t in range(NC):
                    wait_apart(dve, c_step, b * 6 + t + 1, passed)
                    nc.vector.bn_aggr(c_mv[:, t, :], c_stats[:, t, :]).then_inc(c_step, 1)

            def normalise(b):
                since(dve, proj_done, b * USES - USES + 2)
                dve.wait_ge(c_rstd_step, b * 2 + 2)
                for t in range(NC):
                    nc.vector.tensor_scalar(c_norm[:, t, :], c_in[:, t, :], c_mv[:, t, 0:1], c_rstd[:, t:t + 1],
                                            ALU.subtract, ALU.mult).then_inc(norm_ready, 1)
                nc.vector.tensor_scalar(lat[:], x[:, b, :], mv[:, b, 0:1], rstd2[:, bass.ds(b, 1)],
                                        ALU.subtract, ALU.mult).then_inc(norm_ready, 1)

            def transposed_inputs(b):
                for c in range(KC):
                    dve.wait_ge(proj_done, b * USES + T0 + c + 1)
                    for (lo, hi, a) in ((0, N, 0), (N, N + S, 2)):
                        done = nc.vector.tensor_scalar(kvT[:, c, lo:hi], proj_ps[:, c, lo:hi], affine[:, a, c:c + 1],
                                                       affine[:, a + 1, c:c + 1], ALU.mult, ALU.add)
                    done.then_inc(kvT_ready, 1)

            def split_inputs(b):
                for c in range(KC):
                    dve.wait_ge(hi_ready, b * SPLITS + c + 1)
                    nc.vector.tensor_tensor(kvT_lo[:, c, :], kvT[:, c, :], kvT_hi[:, c, :].bitcast(F32), ALU.subtract
                                            ).then_inc(lo_ready, 1)

            def split_queries_and_keys(b):
                for i in range(2):
                    dve.wait_ge(hi_ready, b * SPLITS + SPLIT_Q + i + 1)
                    for a in range(2):
                        half_of = slice(a * DH, (a + 1) * DH)
                        done = nc.vector.tensor_tensor(
                            q_lo[half_of, a, 4 * i:4 * i + 4, :].rearrange("p h s -> p (h s)"),
                            proj_ps[half_of, i, 0:4 * S],
                            q_hi[half_of, a, 4 * i:4 * i + 4, :].rearrange("p h s -> p (h s)").bitcast(F32), ALU.subtract)
                    done.then_inc(lo_ready, 1)
                for i in range(8):
                    dve.wait_ge(hi_ready, b * SPLITS + SPLIT_K + i + 1)
                    nc.vector.tensor_tensor(kT_lo[:, i, :], key_bank(i), kT_hi[:, i, :].bitcast(F32), ALU.subtract
                                            ).then_inc(lo_ready, 1)

            def values(b):
                for i in range(1, 8, 2):
                    dve.wait_ge(proj_done, b * USES + V0 + i + 1)
                    nc.vector.tensor_copy(v[:, i // 2, 512:1024], proj_ps[0:KT, 1, :]).then_inc(v_odd_ready, 1)

            def mask_score(b, h):
                if h == 0:
                    dve.wait_ge(bias_ready, b + 1)
                since(dve, exp_ready, b * H + h - 1)
                wait_apart(dve, score_done, b * H + h + 1, passed)
                nc.vector.tensor_tensor_reduce(s_sb[:, h % 2, :], score_ps[0:S, h % 2, 0:KEYS], bias[:], -SCALE, 3.4e38,
                                               ALU.add, ALU.min, low[:, h:h + 1]).then_inc(masked_ready, 1)

            def copy_pT(b, h):
                if h % 2 == 1:
                    since(dve, pv_done, b * H + h - 1)
                    dve.wait_ge(pT_done, b * H + h + 1)
                    nc.vector.tensor_copy(pT[:, 1, :], pT_ps[0:KT, 1, 0:4 * S]).then_inc(pT_odd_ready, 1)

            def invert_total(b, h):
                since(dve, pT_done, b * H + h - 1)
                dve.wait_ge(exp_ready, b * H + h + 1)
                nc.vector.reciprocal(inv[:, h % 2:h % 2 + 1], total[:, h:h + 1]).then_inc(inv_step, 1)
                dve.wait_ge(inv_step, (b * H + h) * 2 + 1)
                nc.vector.tensor_scalar(inv_total[:, h % 2, :], ident[0:S, 0:S], inv[:, h % 2:h % 2 + 1], None, ALU.mult
                                        ).then_inc(inv_step, 1)

            def copy_oT(b):
                dve.wait_ge(pv_done, b * H + H)
                since(dve, y_done, b)
                nc.vector.tensor_copy(oT[:, 4:8, :].rearrange("p h s -> p (h s)"), oT_ps[:, 1, 0:4 * S]
                                      ).then_inc(oT_odd_ready, 1)

            def update(b):
                dve.wait_ge(y_done, b + 1)
                update_x(nc, dve, x, stats, x_new, x_stats, proj_ps[0:S, 1, 0:D], b, x_step)

            aggregate(nc, dve, stats, mv, mv_step)
            context_stats(0)
            dve.wait_ge(rstd_step, 7)
            dve.wait_ge(const_w, 16)
            normalise(0)
            for n, (c, part) in enumerate(PARTS):
                dve.wait_ge(act_start, n + 3)
                nc.vector.tensor_tensor(wkv_lo[:, c, part], wkv[:, c, part],
                                        wkv_hi[:, c, part].bitcast(F32), ALU.subtract).then_inc(w_lo_ready, 1)

            def body(b, first, last):
                if not first:
                    invert_total(b - 1, H - 1)
                transposed_inputs(b)
                if not first:
                    copy_pT(b - 1, H - 1)
                split_inputs(b)
                if not first:
                    copy_oT(b - 1)
                split_queries_and_keys(b)
                values(b)
                for h in range(H):
                    mask_score(b, h)
                    if h >= 1:
                        invert_total(b, h - 1)
                    if h >= 2:
                        copy_pT(b, h - 2)
                    if h == 2 and not first:
                        update(b - 1)
                    if h == 4 and not last:
                        context_stats(b + 1)
                    if h == 8 and not last:
                        normalise(b + 1)
            over_steps(dve, body, B)
            invert_total(B - 1, H - 1)
            copy_pT(B - 1, H - 1)
            copy_oT(B - 1)
            update(B - 1)

        @block.scalar
        def _(act):
            def round_inputs(b):
                for c in range(KC):
                    act.wait_ge(kvT_ready, b * KC + c + 1)
                    nc.scalar.activation(kvT_hi[:, c, :], kvT[:, c, :], ACT.Copy).then_inc(hi_ready, 1)

            def round_queries_and_keys(b):
                if isinstance(b, int) and b == 0:
                    act.wait_ge(act_start, 2)
                for i in range(2):
                    act.wait_ge(proj_done, b * USES + Q0 + i + 1)
                    for a in range(2):
                        half_of = slice(a * DH, (a + 1) * DH)
                        done = nc.scalar.activation(
                            q_hi[half_of, a, 4 * i:4 * i + 4, :].rearrange("p h s -> p (h s)"),
                            proj_ps[half_of, i, 0:4 * S], ACT.Copy)
                    done.then_inc(hi_ready, 1)
                for i in range(8):
                    act.wait_ge(proj_done, b * USES + K0 + i + 1)
                    nc.scalar.activation(kT_hi[:, i, :], key_bank(i), ACT.Copy).then_inc(hi_ready, 1)

            def values(b):
                for i in range(0, 8, 2):
                    act.wait_ge(proj_done, b * USES + V0 + i + 1)
                    nc.scalar.activation(v[:, i // 2, 0:512], proj_ps[0:KT, 0, :], ACT.Copy).then_inc(v_even_ready, 1)

            def exp(b, h):
                act.wait_ge(masked_ready, b * H + h + 1)
                if h >= 3:
                    act.wait_ge(pT_done, b * H + h - 2)
                nc.scalar.activation(p[:, h % 3, :], s_sb[:, h % 2, :], ACT.Exp, scale=-1.0, bias=low[:, h:h + 1],
                                     accum_out=total[:, h:h + 1]).then_inc(exp_ready, 1)

            def copy_pT(b, h):
                if h % 2 == 0:
                    since(act, pv_done, b * H + h - 1)
                    act.wait_ge(pT_done, b * H + h + 1)
                    nc.scalar.activation(pT[:, 0, :], pT_ps[0:KT, 0, 0:4 * S], ACT.Copy).then_inc(pT_even_ready, 1)

            def copy_oT(b):
                act.wait_ge(pv_done, b * H + H)
                since(act, y_done, b)
                nc.scalar.activation(oT[:, 0:4, :].rearrange("p h s -> p (h s)"), oT_ps[:, 0, 0:4 * S], ACT.Copy
                                     ).then_inc(oT_even_ready, 1)

            act.wait_ge(zeroed, 5)
            for q in (q_hi, q_lo):
                nc.scalar.activation(q[:].rearrange("p a h s -> p (a h) s"), ident[:, None, 0:S].broadcast_to([128, H, S]),
                                     ACT.Copy, scale=0.0).then_inc(act_start, 1)
            act.wait_ge(weight_w, 48)
            for n, (c, part) in enumerate(PARTS):
                nc.scalar.activation(wkv_hi[:, c, part], wkv[:, c, part], ACT.Copy).then_inc(act_start, 1)

            def body(b, first, last):
                if not first:
                    copy_pT(b - 1, H - 2)
                round_inputs(b)
                if not first:
                    copy_oT(b - 1)
                round_queries_and_keys(b)
                values(b)
                if not first:
                    act.wait_ge(inv_step, b * H * 2)
                for h in range(H):
                    exp(b, h)
                    if h >= 2:
                        copy_pT(b, h - 2)
            over_steps(act, body, B)
            copy_pT(B - 1, H - 2)
            copy_oT(B - 1)

        @block.tensor
        def _(pe):
            def exact_product(out, a_hi, a_lo, b_hi, b_lo, first, last):
                nc.tensor.matmul(out, a_hi, b_hi, start=first, stop=False)
                nc.tensor.matmul(out, a_hi, b_lo, start=False, stop=False)
                return nc.tensor.matmul(out, a_lo, b_hi, start=False, stop=last)

            def transpose_inputs(b):
                pe.wait_ge(norm_ready, b * 4 + 4)
                for c in range(KC):
                    since(pe, (v_even_ready, v_odd_ready)[c], b * 4)
                    for t in range(NC):
                        nc.tensor.transpose(proj_ps[:, c, t * CT:(t + 1) * CT], c_norm[:, t, c * 128:(c + 1) * 128],
                                            ident[0:CT, 0:CT])
                    nc.tensor.transpose(proj_ps[:, c, N:N + S], lat[:, c * 128:(c + 1) * 128], ident[0:S, 0:S]
                                        ).then_inc(proj_done, 1)

            def project_q_and_k(b):
                pe.wait_ge(kvT_ready, b * KC + KC)
                for i in range(2):
                    for k in range(4):
                        at = (4 * i + k) * 128
                        for c in range(KC):
                            done = nc.tensor.matmul(proj_ps[:, i, k * S:(k + 1) * S], wq[:, c, at:at + 128],
                                                    kvT[:, c, N:N + S], start=(c == 0), stop=(c == KC - 1))
                    done.then_inc(proj_done, 1)
                for i in range(8):
                    if i < 2:
                        pe.wait_ge(lo_ready, b * SPLITS + SPLIT_Q + i + 1)
                    elif i < 4:
                        since(pe, masked_ready, b * H)
                    else:
                        pe.wait_ge(lo_ready, b * SPLITS + SPLIT_K + i - 3)
                    at = slice(i * 128, (i + 1) * 128)
                    for c in range(KC):
                        done = exact_product(key_bank(i), wkv_hi[:, c, at], wkv_lo[:, c, at],
                                             kvT_hi[:, c, :], kvT_lo[:, c, :], c == 0, c == KC - 1)
                    done.then_inc(proj_done, 1)

            def project_v(b):
                for i in range(8):
                    if i < 2:
                        pe.wait_ge(lo_ready, b * SPLITS + SPLIT_K + 4 + i + 1)
                    else:
                        pe.wait_ge((v_even_ready, v_odd_ready)[i % 2], b * 4 + i // 2)
                    keys = slice((i // 2) * KT, (i // 2 + 1) * KT)
                    at = slice(INNER + (i % 2) * 512, INNER + (i % 2) * 512 + 512)
                    for c in range(KC):
                        done = exact_product(proj_ps[0:KT, i % 2, :], kvT_hi[:, c, keys], kvT_lo[:, c, keys],
                                             wkv_hi[:, c, at], wkv_lo[:, c, at], c == 0, c == KC - 1)
                    done.then_inc(proj_done, 1)

            def score(b, h):
                if h == 0:
                    pe.wait_ge(lo_ready, b * SPLITS + SPLITS)
                since(pe, masked_ready, b * H + h - 1)
                exact_product(score_ps[0:S, h % 2, 0:KEYS], q_hi[:, h % 2, h // 2, :], q_lo[:, h % 2, h // 2, :],
                              kT_hi[:, h // 2, :], kT_lo[:, h // 2, :], True, True).then_inc(score_done, 1)

            def transpose_p(b, h):
                since(pe, (pT_even_ready, pT_odd_ready)[h % 2], b * (H // 2) + h // 2)
                pe.wait_ge(inv_step, (b * H + h) * 2 + 2)
                for t in range(4):
                    done = nc.tensor.matmul(pT_ps[0:KT, h % 2, t * S:(t + 1) * S], p[:, h % 3, t * KT:(t + 1) * KT],
                                            inv_total[:, h % 2, :], start=True, stop=True)
                done.then_inc(pT_done, 1)

            def weigh_values(b, h):
                if h == 0:
                    pe.wait_ge(v_even_ready, b * 4 + 4)
                    pe.wait_ge(v_odd_ready, b * 4 + 4)
                    since(pe, oT_even_ready, b)
                    since(pe, oT_odd_ready, b)
                pe.wait_ge((pT_even_ready, pT_odd_ready)[h % 2], b * (H // 2) + h // 2 + 1)
                i, at = h // 2, (h % 2) * DH
                for t in range(4):
                    done = nc.tensor.matmul(oT_ps[at:at + DH, i // 4, (i % 4) * S:(i % 4 + 1) * S],
                                            v[:, t, h * DH:(h + 1) * DH], pT[:, h % 2, t * S:(t + 1) * S],
                                            start=(t == 0), stop=(t == 3))
                done.then_inc(pv_done, 1)

            def finish_heads(b):
                transpose_p(b, H - 2)
                weigh_values(b, H - 3)
                transpose_p(b, H - 1)
                weigh_values(b, H - 2)
                weigh_values(b, H - 1)

            def project_out(b, emptied):
                since(pe, v_odd_ready, emptied)
                pe.wait_ge(oT_even_ready, b + 1)
                pe.wait_ge(oT_odd_ready, b + 1)
                for c in range(INNER // 128):
                    done = nc.tensor.matmul(proj_ps[0:S, 1, 0:D], oT[:, c, :], wout[:, c, :],
                                            start=(c == 0), stop=(c == INNER // 128 - 1))
                done.then_inc(y_done, 1)

            def body(b, first, last):
                transpose_inputs(b)
                if first:
                    pe.wait_ge(weight_w, 48)
                    pe.wait_ge(w_lo_ready, len(PARTS))
                if not first:
                    finish_heads(b - 1)
                project_q_and_k(b)
                project_v(b)
                for h in range(H):
                    score(b, h)
                    if h == 1 and not first:
                        project_out(b - 1, b * 4 + 4)
                    if h >= 2:
                        transpose_p(b, h - 2)
                    if h >= 3:
                        weigh_values(b, h - 3)
                if not first:
                    pe.wait_ge(x_step, b * 4 - 3)
            over_steps(pe, body, B)
            finish_heads(B - 1)
            project_out(B - 1, B * 4)


def l0_experts(nc, x, stats, ident, passed, A):
    E, F = 8, 1024
    FC = F // 128
    GB = 4
    TILES = SORTED_TILES
    with ExitStack() as ctx:
        ph = Phase(nc, ctx, "l0f")
        w1 = ph.sb("w1", [128, KC, E * F])
        wo, wr = ph.sb("wo", [128, FC, D]), ph.sb("wr", [128, KC, E])
        rows = ph.sb("rows", [128, 3, D])
        before, ones = ph.sb("before", [S, S]), ph.sb("ones", [S, S])
        expert_no, tile_no = ph.sb("expert_no", [S, E]), ph.sb("tile_no", [1, TILES])
        mv, half, rstd = ph.sb("mv", [S, B, 2]), ph.sb("half", [S, B]), ph.sb("rstd", [S, B])
        x1 = ph.sb("x1", [S, B, D])
        x1T = ph.sb("x1T", [128, 2, 2, KC, S])
        logits, best, best_no = ph.sb("logits", [S, B, E]), ph.sb("best", [S, B, 8]), ph.sb("best_no", [S, B, 8], U32)
        expert = ph.sb("expert", [S, B])
        one_hot, rank = ph.sb("one_hot", [S, B, E]), ph.sb("rank", [S, B, E])
        sums = ph.sb("sums", [S, 2, B, E])
        tiles, tiles_i = ph.sb("tiles", [S, 4, E]), ph.sb("tiles_i", [S, E], mybir.dt.int32)
        slot, slot_i = ph.sb("slot", [S, B]), ph.sb("slot_i", [S, B], U32)
        after = ph.sb("after", [1, TILES, E])
        tile_expert, tile_expert_i = ph.sb("tile_expert", [1, TILES]), ph.sb("tile_expert_i", [1, TILES], mybir.dt.int32)
        xs, xsT = ph.sb("xs", [128, D]), ph.sb("xsT", [128, KC, 128])
        b1 = ph.sb("b1", [128, F])
        pre, h, hT = ph.sb("pre", [128, F]), ph.sb("h", [128, F]), ph.sb("hT", [128, FC, 128])
        ys = ph.sb("ys", [128, D])
        y = ph.sb("y", [S, B, D])
        y_stats, y_mv = ph.sb("y_stats", [S, B, 6]), ph.sb("y_mv", [S, B, 2])
        y_rstd = ph.sb("y_rstd", [S, B])
        sorted_x = A["sorted_x"]
        sorted_y = nc.dram_tensor("sorted_y", (TILES * 128, D), F32, kind="Internal").ap()

        route_ps, xT_ps = ph.banks("route", 1), ph.banks("xT", 1)
        pre_ps, hT_ps, y_ps = ph.banks("pre", 2), ph.banks("hT", 2), ph.banks("y", 1)

        weight_w, const_w = ph.sem("weight_w"), ph.sem("const_w")
        mv_step, rstd_step = ph.sem("mv_step"), ph.sem("rstd_step")
        x1_ready, xT_done, xT_ready = ph.sem("x1_ready"), ph.sem("xT_done"), ph.sem("xT_ready")
        router_done, route_step = ph.sem("router_done"), ph.sem("route_step")
        rank_done = ph.sem("rank_done")
        scattered, xs_w, b1_w = ph.sem("scattered"), ph.sem("xs_w"), ph.sem("b1_w")
        xsT_done, xsT_ready, pre_done = ph.sem("xsT_done"), ph.sem("xsT_ready"), ph.sem("pre_done")
        pre_ready, hT_done = ph.sem("pre_ready"), ph.sem("hT_done")
        hT_even_ready, hT_odd_ready = ph.sem("hT_even_ready"), ph.sem("hT_odd_ready")
        gelu_ready, y_done, ys_ready, ys_w = ph.sem("gelu_ready"), ph.sem("y_done"), ph.sem("ys_ready"), ph.sem("ys_w")
        gathered = [ph.sem("gathered0"), ph.sem("gathered1"), ph.sem("gathered2"), ph.sem("gathered3")]
        y_step, y_rstd_ready, x_step = ph.sem("y_step"), ph.sem("y_rstd_ready"), ph.sem("x_step")

        slot_ready, beta_added = ph.sem("slot_ready"), ph.sem("beta_added")
        block = ctx.enter_context(nc.Block())

        @block.sync
        def _(sp):
            sp.dma_start(wr[:], A["l0f_wr"].rearrange("(c p) n -> p c n", p=128)).then_inc(const_w, 16)
            sp.dma_start(before[:], A["before"]).then_inc(const_w, 16)
            sp.dma_start(expert_no[:], A["expert_no"].broadcast_to([S, E])).then_inc(const_w, 16)
            sp.dma_start(tile_no[:], A["tile_no"]).then_inc(const_w, 16)
            sp.dma_start(rows[:], A["l0f_rows"].broadcast_to([128, 3, D])).then_inc(const_w, 16)
            for c in range(KC):
                sp.dma_start(w1[:, c, :].rearrange("p (e n) -> p e n", e=E),
                             A["l0f_w1"][:, c * 128:(c + 1) * 128, :].rearrange("e p n -> p e n")).then_inc(weight_w, 16)
            sp.dma_start(wo[:], A["l0f_wo"].rearrange("(c p) n -> p c n", p=128)).then_inc(weight_w, 16)

            def load_b1(i):
                e = sp.value_load(tile_expert_i[0:1, bass.ds(i, 1)], min_val=0, max_val=(E - 1) * F)
                sp.dma_start(b1[:], A["l0f_b1"][:, bass.ds(e, F)].broadcast_to([128, F])).then_inc(b1_w, 16)

            def load_tile(i):
                sp.dma_start(xs[:], sorted_x[bass.ds(i * 128, 128), :]).then_inc(xs_w, 16)

            def store_tile(i):
                sp.wait_ge(ys_ready, i + 1)
                sp.dma_start(sorted_y[bass.ds(i * 128, 128), :], ys[:]).then_inc(ys_w, 16)

            sp.wait_ge(scattered, 16 * B)
            load_tile(0)
            sp.wait_ge(xsT_done, 1)
            load_tile(1)
            sp.wait_ge(slot_ready, 2)
            load_b1(0)
            with sp.Fori(0, TILES - 1) as i:
                sp.wait_ge(xsT_done, i + 2)
                load_tile(i + 2)
                sp.wait_ge(pre_ready, i + 1)
                load_b1(i + 1)
                store_tile(i)
            store_tile(TILES - 1)

        @block.gpsimd
        def _(pool):
            single_rstd(nc, pool, mv, half, rstd, mv_step, rstd_step)
            nc.gpsimd.memset(ones[:], 1.0).then_inc(rstd_step, 1)
            pool.wait_ge(x1_ready, B)
            pool.wait_ge(slot_ready, 1)
            for b in range(B):
                nc.gpsimd.indirect_dma_start(sorted_x, bass.IndirectOffsetOnAxis(slot_i[:, b:b + 1], 0), x1[:, b, :],
                                             None).then_inc(scattered, 16)
            for b in range(B):
                nc.gpsimd.tensor_tensor(x[:, b, :], x[:, b, :], rows[0:S, 2, :], ALU.add).then_inc(beta_added, 1)

            def gather(q):
                for b in range(q * GB, (q + 1) * GB):
                    nc.gpsimd.indirect_dma_start(y[:, b, :], None, sorted_y,
                                                 bass.IndirectOffsetOnAxis(slot_i[:, b:b + 1], 0)
                                                 ).then_inc(gathered[q], 16)

            def invert_deviation(q):
                pool.wait_ge(y_step, (q + 1) * 3 * GB)
                group = slice(q * GB, (q + 1) * GB)
                nc.gpsimd.tensor_scalar(y_rstd[:, group], y_mv[:, group, 1], 1e-12, None, ALU.add
                                        ).then_inc(y_rstd_ready, 1)
                pool.wait_ge(y_rstd_ready, 2 * q + 1)
                nc.gpsimd.tensor_tensor(y_rstd[:, group], y_rstd[:, group], half[:, group], ALU.pow
                                        ).then_inc(y_rstd_ready, 1)

            pool.wait_ge(ys_w, 16 * TILES)
            gather(0)
            for q in range(1, B // GB):
                gather(q)
                invert_deviation(q - 1)
            invert_deviation(B // GB - 1)

        @block.vector
        def _(dve):
            steps = [0]

            def step(instruction):
                steps[0] += 1
                instruction.then_inc(route_step, 1)
                dve.wait_ge(route_step, steps[0])

            aggregate(nc, dve, stats, mv, mv_step)
            dve.wait_ge(rstd_step, 3)
            for b in range(B):
                nc.vector.tensor_scalar(x1[:, b, :], x[:, b, :], mv[:, b, 0:1], rstd[:, b:b + 1],
                                        ALU.subtract, ALU.mult).then_inc(x1_ready, 1)
            dve.wait_ge(router_done, B // 2)
            step(nc.vector.tensor_copy(logits[:].rearrange("p b e -> p (b e)"), route_ps[0:S, 0, 0:B * E]))
            for b in range(B):
                nc.vector.max(best[:, b, :], logits[:, b, :]).then_inc(route_step, 1)
            for b in range(B):
                dve.wait_ge(route_step, b + 2)
                nc.vector.max_index(best_no[:, b, :], best[:, b, :], logits[:, b, :]).then_inc(route_step, 1)
            steps[0] += 2 * B
            dve.wait_ge(route_step, steps[0])
            step(nc.vector.tensor_copy(expert[:], best_no[:, :, 0]))
            dve.wait_ge(const_w, 80)
            step(nc.vector.tensor_tensor(one_hot[:], expert_no[:, None, :].broadcast_to([S, B, E]),
                                         expert[:, :, None].broadcast_to([S, B, E]), ALU.is_equal))
            dve.wait_ge(rank_done, 1)
            nc.vector.tensor_copy(rank[:].rearrange("p b e -> p (b e)"), route_ps[0:S, 0, 128:256])
            step(nc.vector.tensor_copy(sums[:, 0].rearrange("p b e -> p (b e)"), route_ps[0:S, 0, 256:384]))
            for n, d in enumerate((1, 2, 4, 8)):
                a, z = sums[:, n % 2], sums[:, (n + 1) % 2]
                nc.vector.tensor_copy(z[:, 0:d, :], a[:, 0:d, :])
                step(nc.vector.tensor_tensor(z[:, d:B, :], a[:, d:B, :], a[:, 0:B - d, :], ALU.add))
            step(nc.vector.tensor_scalar(tiles_i[:], sums[:, 0, B - 1, :], 127.0, None, ALU.add))
            step(nc.vector.tensor_scalar(tiles_i[:], tiles_i[:], 7, None, ALU.arith_shift_right))
            step(nc.vector.tensor_copy(tiles[:, 0, :], tiles_i[:]))
            for n, d in enumerate((1, 2, 4)):
                nc.vector.tensor_copy(tiles[:, n + 1, 0:d], tiles[:, n, 0:d])
                step(nc.vector.tensor_tensor(tiles[:, n + 1, d:E], tiles[:, n, d:E], tiles[:, n, 0:E - d], ALU.add))
            step(nc.vector.tensor_tensor(tiles[:, 0, :], tiles[:, 3, :], tiles[:, 0, :], ALU.subtract))
            step(nc.vector.tensor_scalar(tiles[:, 1, :], tiles[:, 0, :], 128.0, None, ALU.mult))
            step(nc.vector.tensor_tensor(rank[:, 1:B, :], rank[:, 1:B, :], sums[:, 0, 0:B - 1, :], ALU.add))
            step(nc.vector.tensor_tensor(rank[:], rank[:], tiles[:, 1:2, :].broadcast_to([S, B, E]), ALU.add))
            step(nc.vector.tensor_tensor(rank[:], rank[:], one_hot[:], ALU.mult))
            step(nc.vector.tensor_reduce(slot[:], rank[:], AX.X, ALU.add))
            nc.vector.tensor_copy(slot_i[:], slot[:]).then_inc(slot_ready, 1)
            step(nc.vector.tensor_tensor(after[:], tile_no[:, :, None].broadcast_to([1, TILES, E]),
                                         tiles[0:1, 3:4, :].broadcast_to([1, TILES, E]), ALU.is_ge))
            step(nc.vector.tensor_reduce(tile_expert[:], after[:], AX.X, ALU.add))
            step(nc.vector.tensor_scalar(tile_expert[:], tile_expert[:], float(E - 1), float(F), ALU.min, ALU.mult))
            nc.vector.tensor_copy(tile_expert_i[:], tile_expert[:]).then_inc(slot_ready, 1)

            def add_bias(i):
                since(dve, pre_done, i + 1)
                dve.wait_ge(b1_w, i * 16 + 16)
                since(dve, gelu_ready, i)
                nc.vector.tensor_tensor(pre[:], pre_ps[:].rearrange("p a n -> p (a n)"), b1[:], ALU.add
                                        ).then_inc(pre_ready, 1)

            def tile(i, first, last):
                dve.wait_ge(hT_done, i * 2 + 2)
                since(dve, y_done, i)
                nc.vector.tensor_copy(hT[:, 4:8, :].rearrange("p f t -> p (f t)"), hT_ps[:, 1, :]).then_inc(hT_odd_ready, 1)
                if not last:
                    add_bias(i + 1)
                dve.wait_ge(y_done, i + 1)
                since(dve, ys_w, i * 16)
                nc.vector.tensor_tensor(ys[:], y_ps[:, 0, 0:D], rows[:, 0, :], ALU.add).then_inc(ys_ready, 1)
            add_bias(0)
            over_steps(dve, tile, TILES)

            def statistics(q):
                dve.wait_ge(gathered[q], 16 * GB)
                at = q * 3 * GB
                for b in range(q * GB, (q + 1) * GB):
                    nc.vector.tensor_tensor(y[:, b, :], y[:, b, :], x1[:, b, :], ALU.add).then_inc(y_step, 1)
                for n, b in enumerate(range(q * GB, (q + 1) * GB)):
                    dve.wait_ge(y_step, at + n + 1)
                    nc.vector.bn_stats(y_stats[:, b, :], y[:, b, :]).then_inc(y_step, 1)
                for n, b in enumerate(range(q * GB, (q + 1) * GB)):
                    dve.wait_ge(y_step, at + GB + n + 1)
                    nc.vector.bn_aggr(y_mv[:, b, :], y_stats[:, b, :]).then_inc(y_step, 1)

            def update(q):
                dve.wait_ge(y_rstd_ready, 2 * q + 2)
                at = q * 3 * GB
                for b in range(q * GB, (q + 1) * GB):
                    nc.vector.tensor_scalar(y[:, b, :], y[:, b, :], y_mv[:, b, 0:1], y_rstd[:, b:b + 1],
                                            ALU.subtract, ALU.mult).then_inc(x_step, 1)
                for n, b in enumerate(range(q * GB, (q + 1) * GB)):
                    dve.wait_ge(x_step, at + n + 1)
                    nc.vector.tensor_tensor(y[:, b, :], y[:, b, :], rows[0:S, 1, :], ALU.mult).then_inc(x_step, 1)
                for n, b in enumerate(range(q * GB, (q + 1) * GB)):
                    dve.wait_ge(x_step, at + GB + n + 1)
                    nc.vector.tensor_tensor(x[:, b, :], x[:, b, :], y[:, b, :], ALU.add).then_inc(x_step, 1)
                for n, b in enumerate(range(q * GB, (q + 1) * GB)):
                    dve.wait_ge(x_step, at + 2 * GB + n + 1)
                    nc.vector.bn_stats(stats[:, b, :], x[:, b, :])

            dve.wait_ge(beta_added, B)
            statistics(0)
            for q in range(1, B // GB):
                statistics(q)
                update(q - 1)
            update(B // GB - 1)

        @block.scalar
        def _(act):
            for g in range(B // 2):
                act.wait_ge(xT_done, g + 1)
                if g >= 2:
                    act.wait_ge(router_done, g - 1)
                nc.scalar.activation(x1T[:, g % 2].rearrange("p j c t -> p (j c t)"),
                                     (xT_ps, y_ps)[g % 2][:, 0, 0:2 * KC * S], ACT.Copy).then_inc(xT_ready, 1)

            def tile_input(i):
                since(act, pre_done, i)
                act.wait_ge(xsT_done, i + 1)
                nc.scalar.activation(xsT[:].rearrange("p c t -> p (c t)"), xT_ps[:, 0, 0:KC * 128], ACT.Copy
                                     ).then_inc(xsT_ready, 1)

            def activate(i):
                act.wait_ge(pre_ready, i + 1)
                since(act, hT_done, i * 2)
                nc.scalar.activation(h[:], pre[:], ACT.Gelu).then_inc(gelu_ready, 1)

            def tile(i, first, last):
                act.wait_ge(hT_done, i * 2 + 1)
                since(act, y_done, i)
                nc.scalar.activation(hT[:, 0:4, :].rearrange("p f t -> p (f t)"), hT_ps[:, 0, :], ACT.Copy
                                     ).then_inc(hT_even_ready, 1)
                if not last:
                    tile_input(i + 2)
                    activate(i + 1)

            tile_input(0)
            activate(0)
            tile_input(1)
            over_steps(act, tile, TILES)

        @block.tensor
        def _(pe):
            pe.wait_ge(const_w, 80)
            for g in range(B // 2 + 1):
                if g < B // 2:
                    pe.wait_ge(x1_ready, 2 * g + 2)
                    if g >= 2:
                        pe.wait_ge(xT_ready, g - 1)
                    bank = (xT_ps, y_ps)[g % 2]
                    for j in range(2):
                        for c in range(KC):
                            at = (j * KC + c) * S
                            done = nc.tensor.transpose(bank[:, 0, at:at + S],
                                                       x1[:, 2 * g + j, c * 128:(c + 1) * 128], ident[0:S, 0:S])
                    done.then_inc(xT_done, 1)
                if g >= 1:
                    pe.wait_ge(xT_ready, g)
                    for j in range(2):
                        b = 2 * (g - 1) + j
                        for c in range(KC):
                            done = nc.tensor.matmul(route_ps[0:S, 0, b * E:(b + 1) * E], x1T[:, (g - 1) % 2, j, c, :],
                                                    wr[:, c, :], start=(c == 0), stop=(c == KC - 1))
                    done.then_inc(router_done, 1)
            pe.wait_ge(route_step, 2 * B + 3)
            pe.wait_ge(rstd_step, 4)
            for n, m in enumerate((before, ones)):
                done = nc.tensor.matmul(route_ps[0:S, 0, (n + 1) * 128:(n + 2) * 128], m[:],
                                        one_hot[:].rearrange("p b e -> p (b e)"), start=True, stop=True)
            done.then_inc(rank_done, 1)

            def transpose_tile(i):
                since(pe, xs_w, i * 16 + 16)
                since(pe, xsT_ready, i)
                for c in range(KC):
                    done = nc.tensor.transpose(xT_ps[:, 0, c * 128:(c + 1) * 128], xs[:, c * 128:(c + 1) * 128], ident[:])
                done.then_inc(xsT_done, 1)

            def multiply(i):
                e = pe.value_load(tile_expert_i[0:1, bass.ds(i, 1)], min_val=0, max_val=(E - 1) * F)
                pe.wait_ge(xsT_ready, i + 1)
                since(pe, pre_ready, i)
                for a in range(2):
                    for c in range(KC):
                        done = nc.tensor.matmul(pre_ps[:, a, :], xsT[:, c, :], w1[:, c, bass.ds(e + a * 512, 512)],
                                                start=(c == 0), stop=(c == KC - 1))
                done.then_inc(pre_done, 1)

            def tile(i, first, last):
                pe.wait_ge(gelu_ready, i + 1)
                since(pe, hT_even_ready, i)
                since(pe, hT_odd_ready, i)
                for f in range(FC):
                    done = nc.tensor.transpose(hT_ps[:, f // 4, (f % 4) * 128:(f % 4 + 1) * 128],
                                               h[:, f * 128:(f + 1) * 128], ident[:])
                    if f % 4 == 3:
                        done.then_inc(hT_done, 1)
                if not last:
                    multiply(i + 1)
                    transpose_tile(i + 2)
                pe.wait_ge(hT_even_ready, i + 1)
                pe.wait_ge(hT_odd_ready, i + 1)
                since(pe, ys_ready, i)
                for f in range(FC):
                    done = nc.tensor.matmul(y_ps[:, 0, 0:D], hT[:, f, :], wo[:, f, :],
                                            start=(f == 0), stop=(f == FC - 1))
                done.then_inc(y_done, 1)

            transpose_tile(0)
            pe.wait_ge(slot_ready, 2)
            pe.wait_ge(weight_w, 16 * (KC + 1))
            multiply(0)
            transpose_tile(1)
            over_steps(pe, tile, TILES)


def l1_attention(nc, x, stats, ident, passed, A):
    H, DH = 16, 64
    HP = H // 2
    SCALE = float(DH) ** -0.5
    G = B // 2
    QB = 4
    Q, QT = B // QB, QB * S
    with ExitStack() as ctx:
        ph = Phase(nc, ctx, "l1a")
        wo = ph.sb("wo", [128, HP, D])
        gamma, causal = ph.sb("gamma", [128, 1, KC]), ph.sb("causal", [S, S])
        mv, half = ph.sb("mv", [S, B, 2]), ph.sb("half", [S, B])
        rstd, rvar, rstd2 = ph.sb("rstd", [S, B]), ph.sb("rvar", [S, B]), ph.sb("rstd2", [S, B])
        all_qT, qT = ph.sb("all_qT", [128, HP, B * S]), ph.sb("qT", [128, HP, PAIR])
        kT = ph.sb("kT", [128, B, 2, S])
        all_v, v = ph.sb("all_v", [S, B, DH]), ph.sb("v", [S, 2, DH])
        pT, oT = ph.sb("pT", [S, H, S]), ph.sb("oT", [128, 2, HP, S])
        top, shift = ph.sb("top", [S, 2, H]), ph.sb("shift", [S, 2, H])
        total, inv = ph.sb("total", [S, 2, H]), ph.sb("inv", [S, 2, H])
        x_new, x_stats = ph.sb("x_new", [S, D]), ph.sb("x_stats", [S, 6])

        score_ps = ph.banks("score", 4)
        o_ps, y_ps = ph.banks("o", 2), ph.banks("y", 2)

        weight_w, mv_step, rstd_step = ph.sem("weight_w"), ph.sem("mv_step"), ph.sem("rstd_step")
        norm_ready, inT_done, proj_done = ph.sem("norm_ready"), ph.sem("inT_done"), ph.sem("proj_done")
        act_step, dve_step = ph.sem("act_step"), ph.sem("dve_step")
        qv_ready = ph.sem("qv_ready")
        score_done, softmax_step, exp_ready = ph.sem("score_done"), ph.sem("softmax_step"), ph.sem("exp_ready")
        pn_ready, pT_done, pT_ready = ph.sem("pn_ready"), ph.sem("pT_done"), ph.sem("pT_ready")
        o_done, o_ready, y_done, x_step = ph.sem("o_done"), ph.sem("o_ready"), ph.sem("y_done"), ph.sem("x_step")

        WQ_HI = 1

        def in_step(q, k):
            return 2 + k if q == 0 else 8 * q + 1 + k

        def even_step(q, i):
            return 4 + 8 * q + i // 2 + 1

        def kv_step(q):
            return 4 + 8 * q + 8

        WQ_LO = 1

        def lo_step(q):
            return 1 + 5 * q + 1

        def odd_step(q, i):
            return 1 + 5 * q + 1 + i // 2 + 1

        def query_bank(i):
            return (y_ps, o_ps)[i // 2 % 2][:, i % 2, 0:QT]

        with ExitStack() as projections:
            ph_in = Phase(nc, projections, "l1q")
            wv = ph_in.sb("wv", [128, KC, DH])
            wq, wk = ph_in.sb("wq", [128, KC, H * DH]), ph_in.sb("wk", [128, KC, 2 * DH])
            wq_hi, wq_lo = ph_in.sb("wq_hi", [128, KC, H * DH], F32R), ph_in.sb("wq_lo", [128, KC, H * DH], F32R)
            x1, x2 = ph_in.sb("x1", [S, QB, D]), ph_in.sb("x2", [S, QB, D])
            x1T, x2T = ph_in.sb("x1T", [128, 2, KC, QT]), ph_in.sb("x2T", [128, KC, QT])
            x2T_hi, x2T_lo = ph_in.sb("x2T_hi", [128, 2, KC, QT], F32R), ph_in.sb("x2T_lo", [128, 2, KC, QT], F32R)
            block = projections.enter_context(nc.Block())

            @block.sync
            def _(sp):
                sp.dma_start(gamma[:], A["l1a_gamma"]).then_inc(weight_w, 16)
                sp.dma_start(causal[:], A["causal"]).then_inc(weight_w, 16)
                sp.dma_start(wq[:], A["l1a_wq"].rearrange("(c p) n -> p c n", p=128)).then_inc(weight_w, 16)
                sp.dma_start(wk[:], A["l1a_wk"].rearrange("(c p) n -> p c n", p=128)).then_inc(weight_w, 16)
                sp.dma_start(wv[:], A["l1a_wv"].rearrange("(c p) n -> p c n", p=128)).then_inc(weight_w, 16)
                sp.dma_start(wo[:], A["l1a_wo"].rearrange("(c p) n -> p c n", p=128)).then_inc(weight_w, 16)

            @block.gpsimd
            def _(pool):
                double_rstd(nc, pool, mv, half, rstd, rvar, rstd2, mv_step, rstd_step)
                nc.gpsimd.memset(kT[:], 0.0).then_inc(rstd_step, 1)

            @block.vector
            def _(dve):
                def norm(q):
                    if q >= 1:
                        dve.wait_ge(inT_done, q * 2)
                    for j in range(QB):
                        b = q * QB + j
                        nc.vector.tensor_scalar(x2[:, j], x[:, b, :], mv[:, b, 0:1], rstd2[:, b:b + 1],
                                                ALU.subtract, ALU.mult).then_inc(norm_ready, 1)
                    for j in range(QB):
                        b = q * QB + j
                        nc.vector.tensor_scalar(x1[:, j], x[:, b, :], mv[:, b, 0:1], rstd[:, b:b + 1],
                                                ALU.subtract, ALU.mult).then_inc(norm_ready, 1)

                aggregate(nc, dve, stats, mv, mv_step)
                dve.wait_ge(rstd_step, 8)
                norm(0)
                dve.wait_ge(act_step, WQ_HI)
                nc.vector.tensor_tensor(wq_lo[:], wq[:], wq_hi[:].bitcast(F32), ALU.subtract).then_inc(dve_step, 1)
                for q in range(Q):
                    dve.wait_ge(act_step, in_step(q, 1))
                    if q >= 2:
                        dve.wait_ge(proj_done, 9 * (q - 2) + 8)
                    nc.vector.tensor_tensor(x2T_lo[:, q % 2], x2T[:], x2T_hi[:, q % 2].bitcast(F32), ALU.subtract
                                            ).then_inc(dve_step, 1)
                    if q + 1 < Q:
                        norm(q + 1)
                    for i in range(1, HP, 2):
                        dve.wait_ge(proj_done, 9 * q + i + 1)
                        nc.vector.tensor_copy(all_qT[:, i, q * QT:(q + 1) * QT], query_bank(i)).then_inc(dve_step, 1)

            @block.scalar
            def _(act):
                def take_inputs(q):
                    act.wait_ge(inT_done, q * 2 + 1)
                    if q >= 1:
                        act.wait_ge(dve_step, lo_step(q - 1))
                    for c in range(KC):
                        done = nc.scalar.activation(x2T[:, c, :], score_ps[:, c, 0:QT], ACT.Copy, scale=gamma[:, 0, c:c + 1])
                    done.then_inc(act_step, 1)
                    act.wait_ge(act_step, in_step(q, 0))
                    if q >= 2:
                        act.wait_ge(proj_done, 9 * (q - 2) + 8)
                    nc.scalar.activation(x2T_hi[:, q % 2], x2T[:], ACT.Copy).then_inc(act_step, 1)
                    act.wait_ge(inT_done, q * 2 + 2)
                    if q >= 2:
                        act.wait_ge(proj_done, 9 * (q - 2) + 9)
                    nc.scalar.activation(x1T[:, q % 2], score_ps[:, 2:4, 0:QT], ACT.Copy).then_inc(act_step, 1)

                act.wait_ge(weight_w, 96)
                nc.scalar.activation(wq_hi[:], wq[:], ACT.Copy).then_inc(act_step, 1)
                take_inputs(0)
                act.wait_ge(rstd_step, 9)
                for q in range(Q):
                    for i in range(0, HP, 2):
                        act.wait_ge(proj_done, 9 * q + i + 1)
                        nc.scalar.activation(all_qT[:, i, q * QT:(q + 1) * QT], query_bank(i), ACT.Copy
                                             ).then_inc(act_step, 1)
                    if q + 1 < Q:
                        take_inputs(q + 1)
                    act.wait_ge(proj_done, 9 * q + 9)
                    for a in range(2):
                        part = slice(a * DH, (a + 1) * DH)
                        nc.scalar.activation(kT[part, q * QB:(q + 1) * QB, a, :],
                                             o_ps[part, 0, 0:QT].rearrange("p (j t) -> p j t", j=QB), ACT.Copy)
                    nc.scalar.activation(all_v[:, q * QB:(q + 1) * QB, :].rearrange("p j d -> p (j d)"),
                                         o_ps[0:S, 1, 0:QB * DH], ACT.Copy).then_inc(act_step, 1)

            @block.tensor
            def _(pe):
                def transpose_inputs(q, n):
                    pe.wait_ge(norm_ready, q * 2 * QB + (n + 1) * QB)
                    if q >= 1:
                        pe.wait_ge(act_step, in_step(q - 1, 0 if n == 0 else 2))
                    for c in range(KC):
                        for j in range(QB):
                            done = nc.tensor.transpose(score_ps[:, 2 * n + c, j * S:(j + 1) * S],
                                                       (x2, x1)[n][:, j, c * 128:(c + 1) * 128], ident[0:S, 0:S])
                    done.then_inc(inT_done, 1)

                transpose_inputs(0, 0)
                transpose_inputs(0, 1)
                pe.wait_ge(weight_w, 96)
                pe.wait_ge(dve_step, WQ_LO)
                for q in range(Q):
                    pe.wait_ge(dve_step, lo_step(q))
                    for i in range(HP):
                        if i >= 4:
                            pe.wait_ge(*((act_step, even_step(q, i - 4)) if i % 2 == 0 else (dve_step, odd_step(q, i - 4))))
                        elif q >= 1 and i < 2:
                            pe.wait_ge(*((act_step, even_step(q - 1, 4)) if i == 0 else (dve_step, odd_step(q - 1, 5))))
                        elif q >= 1:
                            pe.wait_ge(act_step, kv_step(q - 1))
                        heads = slice(i * 128, (i + 1) * 128)
                        for c in range(KC):
                            hi, lo = x2T_hi[:, q % 2, c, :], x2T_lo[:, q % 2, c, :]
                            nc.tensor.matmul(query_bank(i), wq_hi[:, c, heads], hi, start=(c == 0), stop=False)
                            nc.tensor.matmul(query_bank(i), wq_hi[:, c, heads], lo, start=False, stop=False)
                            done = nc.tensor.matmul(query_bank(i), wq_lo[:, c, heads], hi, start=False, stop=(c == KC - 1))
                        done.then_inc(proj_done, 1)
                        if i == 5 and q + 1 < Q:
                            transpose_inputs(q + 1, 0)
                    if q + 1 < Q:
                        transpose_inputs(q + 1, 1)
                    pe.wait_ge(act_step, even_step(q, 6))
                    pe.wait_ge(dve_step, odd_step(q, 7))
                    pe.wait_ge(act_step, in_step(q, 2))
                    for c in range(KC):
                        nc.tensor.matmul(o_ps[:, 0, 0:QT], wk[:, c, :], x1T[:, q % 2, c, :],
                                         start=(c == 0), stop=(c == KC - 1))
                    for j in range(QB):
                        for c in range(KC):
                            done = nc.tensor.matmul(o_ps[0:S, 1, j * DH:(j + 1) * DH],
                                                    x1T[:, q % 2, c, j * S:(j + 1) * S], wv[:, c, :],
                                                    start=(c == 0), stop=(c == KC - 1))
                    done.then_inc(proj_done, 1)

        p, pn = ph.sb("p", [S, 2, H, S]), ph.sb("pn", [S, 2, H, S])
        with nc.Block() as block:
            @block.gpsimd
            def _(pool):
                def body(g, first, last):
                    for j in range(2):
                        b = g * 2 + j
                        pool.wait_ge(softmax_step, b * 4 + 4)
                        since(pool, pT_done, b * 2 - 2)
                        nc.gpsimd.tensor_tensor(pn[:, j], p[:, j], inv[:, j, :, None].broadcast_to([S, H, S]),
                                                ALU.mult).then_inc(pn_ready, 1)
                over_steps(pool, body, G)

            @block.vector
            def _(dve):
                def softmax(g, j):
                    b = g * 2 + j
                    dve.wait_ge(score_done, b + 1)
                    since(dve, pn_ready, b - 1)
                    nc.vector.tensor_tensor(
                        p[:, j].rearrange("p (a h) s -> p a h s", a=4),
                        score_ps[0:S, :, 0:4 * S].rearrange("p a (h s) -> p a h s", h=4),
                        causal[:, None, None, :].broadcast_to([S, 4, 4, S]), ALU.add).then_inc(softmax_step, 1)
                    dve.wait_ge(softmax_step, b * 4 + 1)
                    nc.vector.tensor_reduce(top[:, j], p[:, j], AX.X, ALU.max).then_inc(softmax_step, 1)
                    dve.wait_ge(softmax_step, b * 4 + 2)
                    nc.vector.tensor_scalar(shift[:, j], top[:, j], -SCALE, None, ALU.mult).then_inc(softmax_step, 1)

                def invert_sums(g, j):
                    b = g * 2 + j
                    dve.wait_ge(exp_ready, b + 1)
                    since(dve, pn_ready, b - 1)
                    nc.vector.reciprocal(inv[:, j], total[:, j]).then_inc(softmax_step, 1)

                def copy_pT(g, j):
                    b = g * 2 + j
                    for k in range(2):
                        dve.wait_ge(pT_done, b * 2 + k + 1)
                        if k == 0:
                            since(dve, o_done, b)
                        nc.vector.tensor_copy(pT[:, 8 * k:8 * k + 8, :].rearrange("p (a h) s -> p a (h s)", a=2),
                                              score_ps[0:S, 2 * k:2 * k + 2, 0:4 * S]).then_inc(pT_ready, 1)

                def update(g, j):
                    b = g * 2 + j
                    dve.wait_ge(y_done, b + 1)
                    update_x(nc, dve, x, stats, x_new, x_stats, y_ps[0:S, j, 0:D], b, x_step)

                softmax(0, 0)
                invert_sums(0, 0)

                def body(g, first, last):
                    softmax(g, 1)
                    copy_pT(g, 0)
                    if not first:
                        update(g - 1, 1)
                    invert_sums(g, 1)
                    if not last:
                        softmax(g + 1, 0)
                    copy_pT(g, 1)
                    update(g, 0)
                    if not last:
                        invert_sums(g + 1, 0)
                over_steps(dve, body, G)
                update(G - 1, 1)

            @block.scalar
            def _(act):
                def exp(g, j):
                    act.wait_ge(softmax_step, (g * 2 + j) * 4 + 3)
                    for h in range(H):
                        done = nc.scalar.activation(p[:, j, h, :], p[:, j, h, :], ACT.Exp, scale=SCALE,
                                                    bias=shift[:, j, h:h + 1], accum_out=total[:, j, h:h + 1])
                    done.then_inc(exp_ready, 1)

                def take_queries(g):
                    since(act, score_done, g * 2)
                    nc.scalar.activation(qT[:], all_qT[:, :, bass.ds(g * PAIR, PAIR)], ACT.Copy).then_inc(qv_ready, 1)

                def take_values(g):
                    since(act, o_done, g * 2)
                    nc.scalar.activation(v[:], all_v[:, bass.ds(g * 2, 2), :], ACT.Copy).then_inc(qv_ready, 1)

                def copy_o(g, j):
                    b = g * 2 + j
                    act.wait_ge(o_done, b + 1)
                    since(act, y_done, b - 1)
                    nc.scalar.activation(oT[:, j].rearrange("p (a h) s -> p a (h s)", a=2), o_ps[:, :, 0:4 * S],
                                         ACT.Copy).then_inc(o_ready, 1)

                take_queries(0)
                exp(0, 0)

                def body(g, first, last):
                    take_values(g)
                    if not last:
                        take_queries(g + 1)
                    exp(g, 1)
                    copy_o(g, 0)
                    if not last:
                        exp(g + 1, 0)
                    copy_o(g, 1)
                over_steps(act, body, G)

            @block.tensor
            def _(pe):
                def score(g, j):
                    b = g * 2 + j
                    pe.wait_ge(qv_ready, g * 2 + 1)
                    since(pe, softmax_step, b * 4 - 3)
                    since(pe, pT_ready, b * 2 - 2)
                    for n in range(HP):
                        done = nc.tensor.matmul(score_ps[0:S, n // 2, (n % 2) * PAIR:(n % 2 + 1) * PAIR],
                                                qT[:, n, j * S:(j + 1) * S],
                                                kT[:, bass.ds(b, 1)].rearrange("p b a s -> p (b a s)"), start=True, stop=True)
                    done.then_inc(score_done, 1)

                def transpose_p(g, j, last):
                    b = g * 2 + j
                    if not (last and j == 1):
                        pe.wait_ge(softmax_step, b * 4 + 5)
                    since(pe, pT_ready, b * 2)
                    pe.wait_ge(pn_ready, b + 1)
                    for n in range(H):
                        done = nc.tensor.transpose(score_ps[0:S, n // 4, (n % 4) * S:(n % 4 + 1) * S], pn[:, j, n, :],
                                                   ident[0:S, 0:S])
                        if n % 8 == 7:
                            done.then_inc(pT_done, 1)

                def weigh_values(g, j):
                    b = g * 2 + j
                    if j == 0:
                        pe.wait_ge(qv_ready, g * 2 + 2)
                    since(pe, o_ready, b)
                    for k in range(2):
                        pe.wait_ge(pT_ready, b * 2 + k + 1)
                        for a in range(2):
                            heads = pT[:, 8 * k:8 * k + 8, :].rearrange("p (h a) s -> p a h s", a=2)
                            done = nc.tensor.matmul(o_ps[a * DH:(a + 1) * DH, k, 0:4 * S], v[:, j, :], heads[:, a],
                                                    start=True, stop=True)
                    done.then_inc(o_done, 1)

                def project_out(g, j):
                    b = g * 2 + j
                    pe.wait_ge(o_ready, b + 1)
                    since(pe, x_step, b * 4 - (7 if j == 0 else 3))
                    for c in range(HP):
                        done = nc.tensor.matmul(y_ps[0:S, j, 0:D], oT[:, j, c, :], wo[:, c, :],
                                                start=(c == 0), stop=(c == HP - 1))
                    done.then_inc(y_done, 1)

                def body(g, first, last):
                    if not first:
                        project_out(g - 1, 1)
                    transpose_p(g, 0, last)
                    weigh_values(g, 0)
                    if not last:
                        score(g + 1, 0)
                    project_out(g, 0)
                    transpose_p(g, 1, last)
                    weigh_values(g, 1)
                    if not last:
                        score(g + 1, 1)

                score(0, 0)
                score(0, 1)
                over_steps(pe, body, G)
                project_out(G - 1, 1)


def l1_context_mix(nc, x, stats, ident, passed, A):
    HD = 16
    CT, NC = N // 3, 3
    with ExitStack() as ctx:
        ph = Phase(nc, ctx, "l1x")
        wq, wkv, wo = ph.sb("wq", [128, KC, D]), ph.sb("wkv", [128, KC, 2 * D]), ph.sb("wo", [128, KC, D])
        q_bias = ph.sb("q_bias", [128, 1, KC])
        kv_bias, rows = ph.sb("kv_bias", [CT, 2 * D]), ph.sb("rows", [S, 3, D])
        heads = ph.sb("heads", [128, 128])
        mv, half, rstd = ph.sb("mv", [S, B, 2]), ph.sb("half", [S, B]), ph.sb("rstd", [S, B])
        ctxT, ctxT_next = ph.sb("ctxT", [128, KC, N]), ph.sb("ctxT_next", [128, KC, N])
        masked = ph.sb("masked", [S, MASK_WORDS], U32)
        flag = ph.sb("flag", [S, 1])
        kv, kTv = ph.sb("kv", [CT, NC, 2 * D]), ph.sb("kTv", [128, KC, 128])
        x1, x1T = ph.sb("x1", [S, D]), ph.sb("x1T", [128, KC, S])
        y_in = ph.sb("y_in", [S, D])
        qT, cT = ph.sb("qT", [128, KC, S]), ph.sb("cT", [128, KC, S])
        y, y_stats, y_mv, y_rstd = ph.sb("y", [S, D]), ph.sb("y_stats", [S, 6]), ph.sb("y_mv", [S, 2]), ph.sb("y_rstd", [S, 1])
        y_var = ph.sb("y_var", [S, 1])
        z = ph.sb("z", [S, D])
        x_new, x_stats = ph.sb("x_new", [S, D]), ph.sb("x_stats", [S, 6])

        kv_ps, kTv_ps, xT_ps = ph.banks("kv", 3), ph.banks("kTv", 1), ph.banks("xT", 1)
        qT_ps, cT_ps, o_ps = ph.banks("qT", 1), ph.banks("cT", 1), ph.banks("o", 1)

        weight_w, ctx_w, mask_w = ph.sem("weight_w"), ph.sem("ctx_w"), ph.sem("mask_w")
        mv_step, rstd_step = ph.sem("mv_step"), ph.sem("rstd_step")
        x1_ready, xT_done, xT_ready = ph.sem("x1_ready"), ph.sem("xT_done"), ph.sem("xT_ready")
        kv_done, kv_ready, kTv_done, kTv_ready = ph.sem("kv_done"), ph.sem("kv_ready"), ph.sem("kTv_done"), ph.sem("kTv_ready")
        q_done, q_ready, c_done, c_ready = ph.sem("q_done"), ph.sem("q_ready"), ph.sem("c_done"), ph.sem("c_ready")
        o_done, flag_step, y_step = ph.sem("o_done"), ph.sem("flag_step"), ph.sem("y_step")
        z_step, x_step, ctx_ready = ph.sem("z_step"), ph.sem("x_step"), ph.sem("ctx_ready")
        y_in_ready = ph.sem("y_in_ready")

        block = ctx.enter_context(nc.Block())

        @block.sync
        def _(sp):
            def load_context(b):
                sp.dma_start(ctxT_next[:], A["ctxT"][bass.ds(b, 1)].rearrange("b (c p) n -> p (b c) n", p=128)
                             ).then_inc(ctx_w, 16)

            sp.dma_start(wkv[:], A["l1x_wkv"].rearrange("(c p) n -> p c n", p=128)).then_inc(weight_w, 16)
            load_context(0)
            sp.dma_start(wq[:], A["l1x_wq"].rearrange("(c p) n -> p c n", p=128)).then_inc(weight_w, 16)
            sp.dma_start(wo[:], A["l1x_wo"].rearrange("(c p) n -> p c n", p=128)).then_inc(weight_w, 16)
            sp.dma_start(q_bias[:], A["l1x_q_bias"]).then_inc(weight_w, 16)
            sp.dma_start(kv_bias[:], A["l1x_kv_bias"].broadcast_to([CT, 2 * D])).then_inc(weight_w, 16)
            sp.dma_start(rows[:], A["l1x_rows"].broadcast_to([S, 3, D])).then_inc(weight_w, 16)
            sp.dma_start(heads[:], A["heads"]).then_inc(weight_w, 16)
            with sp.Fori(1, B) as b:
                sp.wait_ge(ctx_ready, b)
                load_context(b)

        @block.gpsimd
        def _(pool):
            pool.dma_start(masked[:], A["score_mask"][0]).then_inc(mask_w, 16)
            single_rstd(nc, pool, mv, half, rstd, mv_step, rstd_step)

            def body(b, first, last):
                since(pool, x1_ready, b + 1)
                since(pool, y_step, b * 4 - 3)
                nc.gpsimd.tensor_tensor(y_in[:], x1[:], rows[:, 0, :], ALU.add).then_inc(y_in_ready, 1)
                wait_apart(pool, y_step, b * 4 + 3, passed)
                nc.gpsimd.tensor_scalar(y_var[:], y_mv[:, 1:2], LN_EPS, None, ALU.add).then_inc(z_step, 1)
                pool.wait_ge(z_step, b * 4 + 1)
                nc.gpsimd.tensor_tensor(y_rstd[:], y_var[:], half[:, 0:1], ALU.pow).then_inc(z_step, 1)
                pool.wait_ge(y_step, b * 4 + 4)
                since(pool, x_step, b * 4 - 3)
                nc.gpsimd.tensor_tensor(z[:], y[:], rows[:, 1, :], ALU.mult).then_inc(z_step, 1)
                pool.wait_ge(z_step, b * 4 + 3)
                nc.gpsimd.tensor_tensor(z[:], z[:], rows[:, 2, :], ALU.add).then_inc(z_step, 1)
                if not last:
                    since(pool, flag_step, b * 4 + 1)
                    pool.dma_start(masked[:], A["score_mask"][bass.ds(b + 1, 1)].rearrange("b s n -> s (b n)")
                                   ).then_inc(mask_w, 16)
            pool.wait_ge(weight_w, 112)
            over_steps(pool, body, B)

        @block.vector
        def _(dve):
            def add_kv_bias(b):
                for t in range(NC):
                    since(dve, kv_done, b * NC + t + 1)
                    if t == 0:
                        since(dve, kTv_done, b)
                    nc.vector.tensor_tensor(kv[:, t, :], kv_ps[0:CT, t, :], kv_bias[:], ALU.add).then_inc(kv_ready, 1)

            def block_diagonal(b):
                since(dve, kTv_done, b + 1)
                since(dve, c_done, b)
                nc.vector.tensor_tensor(kTv[:], kTv_ps[:, 0, 0:KC * 128].rearrange("p (c n) -> p c n", c=KC),
                                        heads[:, None, :].broadcast_to([128, KC, 128]), ALU.mult).then_inc(kTv_ready, 1)

            def norm(b):
                since(dve, xT_done, b)
                since(dve, y_in_ready, b)
                nc.vector.tensor_scalar(x1[:], x[:, b, :], mv[:, b, 0:1], rstd[:, bass.ds(b, 1)],
                                        ALU.subtract, ALU.mult).then_inc(x1_ready, 1)

            def mask_flag(b):
                since(dve, mask_w, b * 16 + 16)
                nc.vector.tensor_reduce(flag[:], masked[:].bitcast(U8)[:, 0:N], AX.X, ALU.max).then_inc(flag_step, 1)
                dve.wait_ge(flag_step, b * 4 + 1)
                nc.vector.tensor_scalar(flag[:], flag[:], -1.0, 1.0, ALU.mult, ALU.add).then_inc(flag_step, 1)
                dve.wait_ge(flag_step, b * 4 + 2)
                nc.vector.reciprocal(flag[:], flag[:]).then_inc(flag_step, 1)
                dve.wait_ge(flag_step, b * 4 + 3)
                nc.vector.tensor_scalar(flag[:], flag[:], 0.0, None, ALU.mult).then_inc(flag_step, 1)

            def add_output(b):
                dve.wait_ge(o_done, b + 1)
                dve.wait_ge(flag_step, b * 4 + 4)
                dve.wait_ge(y_in_ready, b + 1)
                since(dve, z_step, b * 4 - 1)
                nc.vector.scalar_tensor_tensor(y[:], o_ps[0:S, 0, 0:D], flag[:, 0:1], y_in[:], ALU.add, ALU.add
                                               ).then_inc(y_step, 1)
                dve.wait_ge(y_step, b * 4 + 1)
                nc.vector.bn_stats(y_stats[:], y[:]).then_inc(y_step, 1)
                wait_apart(dve, y_step, b * 4 + 2, passed)
                nc.vector.bn_aggr(y_mv[:], y_stats[:]).then_inc(y_step, 1)

            def normalise(b):
                dve.wait_ge(z_step, b * 4 + 2)
                nc.vector.tensor_scalar(y[:], y[:], y_mv[:, 0:1], y_rstd[:, 0:1], ALU.subtract, ALU.mult
                                        ).then_inc(y_step, 1)

            def update(b):
                dve.wait_ge(z_step, b * 4 + 4)
                update_x(nc, dve, x, stats, x_new, x_stats, z[:], b, x_step)

            aggregate(nc, dve, stats, mv, mv_step)
            dve.wait_ge(rstd_step, 3)
            norm(0)
            dve.wait_ge(weight_w, 112)
            add_kv_bias(0)
            block_diagonal(0)

            def body(b, first, last):
                if not first:
                    update(b - 1)
                if not last:
                    norm(b + 1)
                    add_kv_bias(b + 1)
                mask_flag(b)
                add_output(b)
                if not last:
                    block_diagonal(b + 1)
                normalise(b)
            over_steps(dve, body, B)
            update(B - 1)

        @block.scalar
        def _(act):
            def take_context(b):
                since(act, ctx_w, b * 16 + 16)
                since(act, kv_done, b * NC)
                nc.scalar.activation(ctxT[:], ctxT_next[:], ACT.Copy).then_inc(ctx_ready, 1)

            act.wait_ge(weight_w, 112)
            take_context(0)

            def body(b, first, last):
                act.wait_ge(xT_done, b + 1)
                nc.scalar.activation(x1T[:].rearrange("p c t -> p (c t)"), xT_ps[:, 0, 0:KC * S], ACT.Copy
                                     ).then_inc(xT_ready, 1)
                if not last:
                    take_context(b + 1)
                act.wait_ge(q_done, b + 1)
                for c in range(KC):
                    done = nc.scalar.activation(qT[:, c, :], qT_ps[:, 0, c * S:(c + 1) * S], ACT.Identity,
                                                bias=q_bias[:, 0, c:c + 1])
                done.then_inc(q_ready, 1)
                act.wait_ge(c_done, b + 1)
                nc.scalar.activation(cT[:].rearrange("p c t -> p (c t)"), cT_ps[:, 0, 0:KC * S], ACT.Copy
                                     ).then_inc(c_ready, 1)
            over_steps(act, body, B)

        @block.tensor
        def _(pe):
            def project_kv(b, t):
                if t == 0:
                    since(pe, ctx_ready, b + 1)
                since(pe, kv_ready, b * NC - NC + t + 1)
                for c in range(KC):
                    done = nc.tensor.matmul(kv_ps[0:CT, t, :], ctxT[:, c, t * CT:(t + 1) * CT], wkv[:, c, :],
                                            start=(c == 0), stop=(c == KC - 1))
                done.then_inc(kv_done, 1)

            def multiply_kTv(b):
                since(pe, kTv_ready, b)
                for c in range(KC):
                    for t in range(NC):
                        since(pe, kv_ready, b * NC + t + 1)
                        done = nc.tensor.matmul(kTv_ps[:, 0, c * 128:(c + 1) * 128], kv[:, t, c * 128:(c + 1) * 128],
                                                kv[:, t, D + c * 128:D + (c + 1) * 128],
                                                start=(t == 0), stop=(t == NC - 1))
                done.then_inc(kTv_done, 1)

            pe.wait_ge(weight_w, 112)
            for t in range(NC):
                project_kv(0, t)
            multiply_kTv(0)

            def body(b, first, last):
                since(pe, x1_ready, b + 1)
                since(pe, xT_ready, b)
                for c in range(KC):
                    done = nc.tensor.transpose(xT_ps[:, 0, c * S:(c + 1) * S], x1[:, c * 128:(c + 1) * 128],
                                               ident[0:S, 0:S])
                done.then_inc(xT_done, 1)
                pe.wait_ge(xT_ready, b + 1)
                since(pe, q_ready, b)
                for u in range(KC):
                    for c in range(KC):
                        done = nc.tensor.matmul(qT_ps[:, 0, u * S:(u + 1) * S], wq[:, c, u * 128:(u + 1) * 128],
                                                x1T[:, c, :], start=(c == 0), stop=(c == KC - 1))
                done.then_inc(q_done, 1)
                if not last:
                    project_kv(b + 1, 0)
                pe.wait_ge(q_ready, b + 1)
                pe.wait_ge(kTv_ready, b + 1)
                since(pe, c_ready, b)
                for u in range(KC):
                    done = nc.tensor.matmul(cT_ps[:, 0, u * S:(u + 1) * S], kTv[:, u, :], qT[:, u, :],
                                            start=True, stop=True)
                done.then_inc(c_done, 1)
                if not last:
                    project_kv(b + 1, 1)
                    project_kv(b + 1, 2)
                pe.wait_ge(c_ready, b + 1)
                since(pe, y_step, b * 4 - 3)
                for u in range(KC):
                    done = nc.tensor.matmul(o_ps[0:S, 0, 0:D], cT[:, u, :], wo[:, u, :],
                                            start=(u == 0), stop=(u == KC - 1))
                done.then_inc(o_done, 1)
                if not last:
                    multiply_kTv(b + 1)
            over_steps(pe, body, B)


def l1_experts(nc, x, stats, ident, passed, A, out):
    E, R, F = 4, 4, 1024
    ER, FC = LOW_ROWS, F // 128
    B_LO, LOW_LO = slice(32, 32 + E * R), slice(64, 64 + E * R)
    GB = 4
    G, GT = B // GB, GB * S
    with ExitStack() as ctx:
        ph = Phase(nc, ctx, "l1f")
        wi, wo = ph.sb("wi", [128, KC, F]), ph.sb("wo", [128, FC, D])
        wg, low_a, low_b = ph.sb("wg", [128, KC, E]), ph.sb("low_a", [128, KC, ER]), ph.sb("low_b", [ER, F])
        bg, row_expert = ph.sb("bg", [S, E]), ph.sb("row_expert", [S, ER])
        low_b_r = ph.sb("low_b_r", [ER, F], F32R)
        mv, half, rstd = ph.sb("mv", [S, B, 2]), ph.sb("half", [S, B]), ph.sb("rstd", [S, B])
        x1, x1T = ph.sb("x1", [S, B, D]), ph.sb("x1T", [128, KC, B * S])
        logits, best, best_no = ph.sb("logits", [S, B, 8]), ph.sb("best", [S, B, 8]), ph.sb("best_no", [S, B, 8], U32)
        share, total = ph.sb("share", [S, B, 8]), ph.sb("total", [S, B])
        weight, ratio = ph.sb("weight", [S, B]), ph.sb("ratio", [S, B])
        chosen = ph.sb("chosen", [S, 2, B])
        one_hot = ph.sb("one_hot", [S, 2, B, ER])
        low = ph.sb("low", [ER, B * S])
        low_masked = ph.sb("low_masked", [ER, 2, GT])
        low_first, low_change = ph.sb("low_first", [ER, B * S], F32R), ph.sb("low_change", [ER, B * S], F32R)
        ratio_rows = ph.sb("ratio_rows", [128, B * S])
        z_first, z_second = ph.sb("z_first", [128, 4, GT]), ph.sb("z_second", [128, 2, GT])
        h = ph.sb("h", [128, FC, GT])

        result = ph.sb("result", [S, GB, D])

        z_ps, change_ps, y_ps = ph.banks("z", 2), ph.banks("change", 2), ph.banks("y", 2)
        gate_ps, ratio_ps = ph.banks("gate", 1), ph.banks("ratio", 1)

        weight_w, const_w, stored = ph.sem("weight_w"), ph.sem("const_w"), ph.sem("stored")
        mv_step, rstd_step = ph.sem("mv_step"), ph.sem("rstd_step")
        x1_ready, xT_done, xT_ready = ph.sem("x1_ready"), ph.sem("xT_done"), ph.sem("xT_ready")
        gate_done, low_ready, gate_step, exp_ready = ph.sem("gate_done"), ph.sem("low_ready"), ph.sem("gate_step"), ph.sem("exp_ready")
        one_hot_done = ph.sem("one_hot_done")
        ratio_done, ratio_ready, masked_ready = ph.sem("ratio_done"), ph.sem("ratio_ready"), ph.sem("masked_ready")
        first_done, first_ready, change_done = ph.sem("first_done"), ph.sem("first_ready"), ph.sem("change_done")
        low_hi_ready, low_lo_ready = ph.sem("low_hi_ready"), ph.sem("low_lo_ready")
        b_step = ph.sem("b_step")
        h_step, y_done, x_step = ph.sem("h_step"), ph.sem("y_done"), ph.sem("x_step")

        block = ctx.enter_context(nc.Block())

        @block.sync
        def _(sp):
            sp.dma_start(wg[:], A["l1f_wg"].rearrange("(c p) n -> p c n", p=128)).then_inc(const_w, 16)
            sp.dma_start(low_a[:], A["l1f_a"].rearrange("(c p) n -> p c n", p=128)).then_inc(const_w, 16)
            sp.dma_start(low_b[:], A["l1f_b"]).then_inc(const_w, 16)
            sp.dma_start(bg[:], A["l1f_bg"].broadcast_to([S, E])).then_inc(const_w, 16)
            sp.dma_start(row_expert[:], A["row_expert"].broadcast_to([S, ER])).then_inc(const_w, 16)
            sp.dma_start(wi[:], A["l1f_wi"].rearrange("(c p) n -> p c n", p=128)).then_inc(weight_w, 16)
            sp.dma_start(wo[:], A["l1f_wo"].rearrange("(c p) n -> p c n", p=128)).then_inc(weight_w, 16)
            with sp.Fori(0, G) as g:
                sp.wait_ge(x_step, g * GB + GB)
                sp.dma_start(out[bass.ds(g * GB, GB)].rearrange("b s d -> s b d"), result[:]).then_inc(stored, 16)
            sp.wait_ge(stored, 16 * G)

        @block.gpsimd
        def _(pool):
            single_rstd(nc, pool, mv, half, rstd, mv_step, rstd_step)

        @block.vector
        def _(dve):
            steps = [0]

            def step(instruction):
                steps[0] += 1
                instruction.then_inc(gate_step, 1)
                dve.wait_ge(gate_step, steps[0])

            aggregate(nc, dve, stats, mv, mv_step)
            dve.wait_ge(b_step, 1)
            nc.vector.tensor_tensor(low_b_r[B_LO, :], low_b[B_LO, :], low_b_r[B_LO, :].bitcast(F32), ALU.subtract
                                    ).then_inc(b_step, 1)
            dve.wait_ge(rstd_step, 3)
            for b in range(B):
                nc.vector.tensor_scalar(x1[:, b, :], x[:, b, :], mv[:, b, 0:1], rstd[:, b:b + 1],
                                        ALU.subtract, ALU.mult).then_inc(x1_ready, 1)
            nc.vector.memset(logits[:, :, E:8], NEG)
            dve.wait_ge(const_w, 80)
            dve.wait_ge(gate_done, G)
            step(nc.vector.tensor_tensor(logits[:, :, 0:E], gate_ps[0:S, 0, 0:B * E].rearrange("p (b e) -> p b e", e=E),
                                         bg[:, None, :].broadcast_to([S, B, E]), ALU.add))
            for b in range(B):
                nc.vector.max(best[:, b, :], logits[:, b, :]).then_inc(gate_step, 1)
            for b in range(B):
                dve.wait_ge(gate_step, b + 2)
                nc.vector.max_index(best_no[:, b, :], best[:, b, :], logits[:, b, :]).then_inc(gate_step, 1)
            steps[0] += 2 * B
            dve.wait_ge(gate_step, steps[0])
            step(nc.vector.tensor_tensor(share[:], best[:], best[:, :, 0:1].broadcast_to([S, B, 8]), ALU.subtract))
            step(nc.vector.tensor_copy(chosen[:].rearrange("p k b -> p b k"), best_no[:, :, 0:2]))
            step(nc.vector.tensor_tensor(
                one_hot[:].rearrange("p k b e -> p (k b) e"), row_expert[:, None, :].broadcast_to([S, 2 * B, ER]),
                chosen[:].rearrange("p k b -> p (k b)")[:, :, None].broadcast_to([S, 2 * B, ER]), ALU.is_equal))
            step(nc.vector.tensor_tensor(one_hot[:, 1], one_hot[:, 1], one_hot[:, 0], ALU.subtract))
            dve.wait_ge(exp_ready, 1)
            nc.vector.tensor_copy(ratio[:], share[:, :, 1]).then_inc(ratio_ready, 1)
            step(nc.vector.tensor_reduce(total[:], share[:], AX.X, ALU.add))
            step(nc.vector.reciprocal(weight[:], total[:]))
            for g in range(G):
                dve.wait_ge(one_hot_done, g + 1)
                dve.wait_ge(low_ready, g + 1)
                group = slice(g * GT, (g + 1) * GT)
                if g >= 1:
                    dve.wait_ge(low_lo_ready, 2 * g)
                for k in range(2):
                    nc.vector.tensor_tensor(low_masked[:, k, :], low[:, group], y_ps[0:ER, k, 0:GT], ALU.mult
                                            ).then_inc(masked_ready, 1)
                for k, split in enumerate((low_first, low_change)):
                    dve.wait_ge(low_hi_ready, 2 * g + k + 1)
                    nc.vector.tensor_tensor(split[LOW_LO, group], low_masked[LOW_LO, k, :],
                                            split[LOW_LO, group].bitcast(F32), ALU.subtract).then_inc(low_lo_ready, 1)

            def body(g, first, last):
                for f in range(FC):
                    n = g * FC + f
                    since(dve, h_step, n * 3 - 3)
                    since(dve, first_ready, n + 1)
                    since(dve, change_done, n + 1)
                    if isinstance(g, int) and n == 0:
                        dve.wait_ge(ratio_ready, 1 + G)
                    nc.vector.tensor_tensor(z_second[:, f % 2, :], z_first[:, f % 4, :], change_ps[:, f % 2, 0:GT], ALU.add
                                            ).then_inc(h_step, 1)
                    dve.wait_ge(h_step, n * 3 + 1)
                    nc.vector.scalar_tensor_tensor(z_second[:, f % 2, :], z_second[:, f % 2, :], 0.0, ratio_rows[:, bass.ds(g * GT, GT)],
                                                   ALU.max, ALU.mult).then_inc(h_step, 1)
                    dve.wait_ge(h_step, n * 3 + 2)
                    if f == 0:
                        since(dve, y_done, g * GB)
                    nc.vector.scalar_tensor_tensor(h[:, f, :], z_first[:, f % 4, :], 0.0, z_second[:, f % 2, :], ALU.max, ALU.add
                                                   ).then_inc(h_step, 1)
                for j in range(GB):
                    b = g * GB + j
                    dve.wait_ge(y_done, b + 1)
                    if j == 0:
                        since(dve, stored, g * 16)
                    nc.vector.scalar_tensor_tensor(result[:, j, :], y_ps[0:S, j % 2, 0:D], weight[:, bass.ds(b, 1)],
                                                   x[:, b, :], ALU.mult, ALU.add).then_inc(x_step, 1)
            over_steps(dve, body, G)

        @block.scalar
        def _(act):
            act.wait_ge(const_w, 80)
            nc.scalar.activation(low_b_r[:], low_b[:], ACT.Copy).then_inc(b_step, 1)
            for g in range(G):
                act.wait_ge(xT_done, g + 1)
                nc.scalar.activation(x1T[:, :, g * GT:(g + 1) * GT], (z_ps, change_ps)[g % 2][:, :, 0:GT], ACT.Copy
                                     ).then_inc(xT_ready, 1)
                act.wait_ge(gate_done, g + 1)
                nc.scalar.activation(low[:, g * GT:(g + 1) * GT], y_ps[0:ER, g % 2, 0:GT], ACT.Copy).then_inc(low_ready, 1)
            act.wait_ge(gate_step, 2 * B + 2)
            nc.scalar.activation(share[:], share[:], ACT.Exp).then_inc(exp_ready, 1)
            for g in range(G):
                for k, split in enumerate((low_first, low_change)):
                    act.wait_ge(masked_ready, 2 * g + k + 1)
                    nc.scalar.activation(split[:, g * GT:(g + 1) * GT], low_masked[:, k, :], ACT.Copy
                                         ).then_inc(low_hi_ready, 1)
                act.wait_ge(ratio_done, g + 1)
                nc.scalar.activation(ratio_rows[:, g * GT:(g + 1) * GT], ratio_ps[:, 0, 0:GT], ACT.Copy
                                     ).then_inc(ratio_ready, 1)

            def body(g, first, last):
                for f in range(FC):
                    n = g * FC + f
                    since(act, first_done, n + 1)
                    since(act, h_step, n * 3 - 9)
                    nc.scalar.activation(z_first[:, f % 4, :], z_ps[:, f % 2, 0:GT], ACT.Copy).then_inc(first_ready, 1)
            over_steps(act, body, G)

        @block.tensor
        def _(pe):
            for g in range(G):
                pe.wait_ge(x1_ready, (g + 1) * GB)
                if g >= 2:
                    pe.wait_ge(xT_ready, g - 1)
                for c in range(KC):
                    for j in range(GB):
                        done = nc.tensor.transpose((z_ps, change_ps)[g % 2][:, c, j * S:(j + 1) * S],
                                                   x1[:, g * GB + j, c * 128:(c + 1) * 128], ident[0:S, 0:S])
                done.then_inc(xT_done, 1)
                if g == 0:
                    pe.wait_ge(const_w, 80)
                pe.wait_ge(xT_ready, g + 1)
                if g >= 2:
                    pe.wait_ge(low_ready, g - 1)
                for j in range(GB):
                    b = g * GB + j
                    for c in range(KC):
                        nc.tensor.matmul(gate_ps[0:S, 0, b * E:(b + 1) * E], x1T[:, c, b * S:(b + 1) * S], wg[:, c, :],
                                         start=(c == 0), stop=(c == KC - 1))
                for c in range(KC):
                    done = nc.tensor.matmul(y_ps[0:ER, g % 2, 0:GT], low_a[:, c, :], x1T[:, c, g * GT:(g + 1) * GT],
                                            start=(c == 0), stop=(c == KC - 1))
                done.then_inc(gate_done, 1)
            pe.wait_ge(gate_step, 2 * B + 5)
            pe.wait_ge(low_ready, G)
            for g in range(G):
                since(pe, masked_ready, 2 * g)
                for k in range(2):
                    for j in range(GB):
                        done = nc.tensor.transpose(y_ps[0:ER, k, j * S:(j + 1) * S],
                                                   one_hot[:, k, g * GB + j],
                                                   ident[0:S, 0:S])
                done.then_inc(one_hot_done, 1)
                if g == 0:
                    pe.wait_ge(ratio_ready, 1)
                else:
                    pe.wait_ge(ratio_ready, 1 + g)
                for j in range(GB):
                    done = nc.tensor.matmul(ratio_ps[:, 0, j * S:(j + 1) * S],
                                            ratio[:, g * GB + j:g * GB + j + 1].broadcast_to([S, 128]),
                                            ident[0:S, 0:S], start=True, stop=True)
                done.then_inc(ratio_done, 1)

            def multiply_first(g, f):
                n = g * FC + f
                since(pe, first_ready, n - 1)
                for c in range(KC):
                    nc.tensor.matmul(z_ps[:, f % 2, 0:GT], wi[:, c, f * 128:(f + 1) * 128],
                                     x1T[:, c, bass.ds(g * GT, GT)], start=(c == 0), stop=False)
                nc.tensor.matmul(z_ps[:, f % 2, 0:GT], low_b_r[:, f * 128:(f + 1) * 128],
                                 low_first[:, bass.ds(g * GT, GT)], start=False, stop=True).then_inc(first_done, 1)

            def multiply_change(g, f):
                n = g * FC + f
                if isinstance(n, int):
                    since(pe, h_step, n * 3 - 5)
                else:
                    wait_apart(pe, h_step, n * 3 - 5, passed)
                nc.tensor.matmul(change_ps[:, f % 2, 0:GT], low_b_r[:, f * 128:(f + 1) * 128],
                                 low_change[:, bass.ds(g * GT, GT)], start=True, stop=True).then_inc(change_done, 1)

            def body(g, first, last):
                for f in range(FC):
                    multiply_change(g, f)
                    if f + 2 < FC:
                        multiply_first(g, f + 2)
                if not last:
                    multiply_first(g + 1, 0)
                    multiply_first(g + 1, 1)
                for j in range(GB):
                    b = g * GB + j
                    since(pe, x_step, b - 1)
                    for f in range(FC):
                        if j == 0:
                            pe.wait_ge(h_step, (g * FC + f) * 3 + 3)
                        done = nc.tensor.matmul(y_ps[0:S, j % 2, 0:D], h[:, f, j * S:(j + 1) * S], wo[:, f, :],
                                                start=(f == 0), stop=(f == FC - 1))
                    done.then_inc(y_done, 1)

            pe.wait_ge(low_lo_ready, 2 * G)
            pe.wait_ge(b_step, 2)
            pe.wait_ge(weight_w, 32)
            multiply_first(0, 0)
            multiply_first(0, 1)
            over_steps(pe, body, G)


def load_x(nc, x, stats, ident, A):
    with ExitStack() as ctx:
        ph = Phase(nc, ctx, "in")
        loaded, stats_done = ph.sem("loaded"), ph.sem("stats_done")
        block = ctx.enter_context(nc.Block())

        @block.sync
        def _(sp):
            sp.dma_start(x[:], A["x"].rearrange("b s d -> s b d")).then_inc(loaded, 16)
            sp.dma_start(ident[:], A["ident"]).then_inc(loaded, 16)

        @block.vector
        def _(dve):
            dve.wait_ge(loaded, 32)
            for b in range(B):
                nc.vector.bn_stats(stats[:, b, :], x[:, b, :]).then_inc(stats_done, 1)


def program(nc, A, out):
    with ExitStack() as ctx:
        x = ctx.enter_context(nc.sbuf_tensor("x", [S, B, D], F32))
        A["sorted_x"] = nc.dram_tensor("sorted_x", ((SORTED_TILES + 1) * 128, D), F32, kind="Internal").ap()
        stats = ctx.enter_context(nc.sbuf_tensor("stats", [S, B, 6], F32))
        ident = ctx.enter_context(nc.sbuf_tensor("ident", [128, 128], F32))
        passed = ctx.enter_context(nc.semaphore("passed"))
        load_x(nc, x, stats, ident, A)
        l0_attention(nc, x, stats, ident, passed, A)
        l0_cross_attention(nc, x, stats, ident, passed, A)
        l0_experts(nc, x, stats, ident, passed, A)
        l1_attention(nc, x, stats, ident, passed, A)
        l1_context_mix(nc, x, stats, ident, passed, A)
        l1_experts(nc, x, stats, ident, passed, A, out)


def constants():
    dim = 128
    pos = np.arange(S, dtype=np.float32)[:, None]
    inv_freq = np.exp(-np.log(np.float32(10000.0)) * (np.arange(0, dim, 2, dtype=np.float32) / np.float32(dim)))
    ang = (pos * inv_freq[None, :]).astype(np.float32)
    pe = np.zeros((S, dim), np.float32)
    pe[:, 0::2], pe[:, 1::2] = np.sin(ang), np.cos(ang)
    causal = np.where(np.tril(np.ones((S, S), bool)), np.float32(0), np.float32(NEG))
    return {"pos_q": pe.T, "pos_k": pe[0:1].T, "causal": causal, "ident": np.eye(128, dtype=np.float32),
            "before": np.triu(np.ones((S, S), np.float32), 1), "expert_no": np.arange(8, dtype=np.float32)[None],
            "heads": np.kron(np.eye(8, dtype=np.float32), np.full((16, 16), 0.25, np.float32)),
            "row_expert": low_rows(np.repeat(np.arange(4, dtype=np.float32), 4)[:, None] + 1).T - 1,
            "tile_no": np.arange(SORTED_TILES, dtype=np.float32)[None]}


def by_feature(*vectors):
    return np.stack(vectors).reshape(len(vectors), KC, 128).transpose(2, 0, 1)


def low_rows(a):
    rows = np.zeros((LOW_ROWS, *a.shape[1:]), a.dtype)
    for at in (0, 32, 64):
        rows[at:at + 16] = a
    return rows


def mask_words(mask):
    pad = [(0, 0)] * (mask.ndim - 1) + [(0, 4 * MASK_WORDS - N)]
    return np.pad(mask, pad).view(np.uint32)


def kernel(**inputs):
    from concourse import bacc
    from concourse.bass_utils import run_bass_kernel_spmd

    i = {k: np.asarray(v) for k, v in inputs.items()}
    arrays = {
        "x": i["x"],
        "l0a_wq": i["L0_attn_Wq"].T, "l0a_wk": i["L0_attn_Wk"].T, "l0a_wv": i["L0_attn_Wv"].T,
        "l0a_wo": i["L0_attn_Wo"].T,
        "l0x_wq": i["L0_xattn_Wq"], "l0x_wkv": i["L0_xattn_Wkv"], "l0x_wout": i["L0_xattn_Wout"],
        "l0x_affine": by_feature(i["L0_xattn_g1"], i["L0_xattn_b1"], i["L0_xattn_g2"], i["L0_xattn_b2"]),
        "ctx": i["ctx_1024"], "ctx_mask": mask_words(i["mask_BxS2_bk0"]),
        "l0f_w1": i["L0_ffn_W1"], "l0f_wr": i["L0_ffn_Wr"].T, "l0f_wo": i["L0_ffn_Wo"],
        "l0f_b1": i["L0_ffn_b1"].reshape(1, -1),
        "l0f_rows": np.stack([i["L0_ffn_bo"], i["L0_ffn_gamma"], i["L0_ffn_beta"]])[None],
        "l1a_wq": i["L1_attn_Wq"], "l1a_wk": np.concatenate([i["L1_attn_Wkv"][:, :64]] * 2, 1),
        "l1a_wv": i["L1_attn_Wkv"][:, 64:], "l1a_wo": i["L1_attn_Wo"], "l1a_gamma": by_feature(i["L1_attn_gamma"]),
        "l1x_wq": i["L1_xattn_wq_w"].T, "l1x_wo": i["L1_xattn_wo_w"].T,
        "l1x_wkv": np.concatenate([i["L1_xattn_wk_w"], i["L1_xattn_wv_w"]]).T,
        "l1x_q_bias": by_feature(i["L1_xattn_wq_b"]),
        "l1x_kv_bias": np.concatenate([i["L1_xattn_wk_b"], i["L1_xattn_wv_b"]])[None],
        "l1x_rows": np.stack([i["L1_xattn_wo_b"], i["L1_xattn_ln_g"], i["L1_xattn_ln_b"]])[None],
        "l1f_wi": i["L1_ffn_Wi"].T, "l1f_wo": i["L1_ffn_Wo"].T, "l1f_wg": i["L1_ffn_Wg"].T,
        "l1f_a": low_rows(i["L1_ffn_A"].reshape(16, D)).T,
        "l1f_b": low_rows(i["L1_ffn_B"].transpose(0, 2, 1).reshape(16, 1024)),
        "l1f_bg": i["L1_ffn_bg"][None],
        "ctxT": i["ctx_1024"].transpose(0, 2, 1), "score_mask": mask_words(i["mask_Bx1xSxS2_bf0"][:, 0]),
        **constants(),
    }
    arrays = {k: np.ascontiguousarray(v) for k, v in arrays.items()}
    nc = bacc.Bacc("TRN2", target_bir_lowering=False, num_devices=1)
    A = {k: nc.dram_tensor(f"in_{k}", v.shape, mybir.dt.from_np(v.dtype), kind="ExternalInput").ap()
         for k, v in arrays.items()}
    out = nc.dram_tensor("out", (B, S, D), F32, kind="ExternalOutput").ap()
    program(nc, A, out)
    r = run_bass_kernel_spmd(nc, [{f"in_{k}": v for k, v in arrays.items()}], core_ids=[0])
    return r.results[0]["out"]
```

```python
from contextlib import ExitStack

import numpy as np

import concourse.bass as bass
from concourse import mybir

F32 = mybir.dt.float32
F32R = mybir.dt.float32r
U8 = mybir.dt.uint8
U32 = mybir.dt.uint32
ALU = mybir.AluOpType
ACT = mybir.ActivationFunctionType
AX = mybir.AxisListType

B, S, D, N = 16, 112, 256, 375
KC = D // 128
MASK_WORDS = -(-N // 4)
LOW_ROWS = 80
PAIR = 2 * S
NEG = -3.0e38
LN_EPS = 1e-5
SORTED_TILES = (B * S + 8 * 127) // 128


def since(eng, sem, value):
    if isinstance(value, int) and value <= 0:
        return
    eng.wait_ge(sem, value)


def over_steps(eng, body, count):
    body(0, first=True, last=False)
    if count > 2:
        with eng.Fori(1, count - 1) as i:
            body(i, first=False, last=False)
    body(count - 1, first=False, last=True)


class Phase:

    def __init__(self, nc, ctx, name):
        self.nc, self.ctx, self.name = nc, ctx, name

    def sb(self, name, shape, dt=F32):
        return self.ctx.enter_context(self.nc.sbuf_tensor(f"{self.name}_{name}", shape, dt))

    def banks(self, name, n):
        return self.ctx.enter_context(self.nc.psum_tensor(f"{self.name}_{name}_ps", [128, n, 512], F32))

    def sem(self, name):
        return self.ctx.enter_context(self.nc.semaphore(f"{self.name}_{name}"))


def wait_apart(eng, sem, value, passed):
    since(eng, sem, value)
    eng.sem_inc(passed, 1)


def update_x(nc, dve, x, stats, x_new, x_stats, y, b, x_step):
    nc.vector.tensor_tensor(x_new[:], x[:, b, :], y, ALU.add).then_inc(x_step, 1)
    dve.wait_ge(x_step, b * 4 + 1)
    nc.vector.bn_stats(x_stats[:], x_new[:]).then_inc(x_step, 1)
    nc.vector.tensor_scalar(x[:, b, :], x_new[:], 1.0, None, ALU.mult).then_inc(x_step, 1)
    dve.wait_ge(x_step, b * 4 + 3)
    nc.vector.tensor_scalar(stats[:, b, :], x_stats[:], 1.0, None, ALU.mult).then_inc(x_step, 1)


def aggregate(nc, dve, stats, mv, mv_step):
    for b in range(B):
        nc.vector.bn_aggr(mv[:, b, :], stats[:, b, :]).then_inc(mv_step, 1)


def single_rstd(nc, pool, mv, half, rstd, mv_step, rstd_step):
    nc.gpsimd.memset(half[:], -0.5).then_inc(rstd_step, 1)
    pool.wait_ge(mv_step, B)
    nc.gpsimd.tensor_scalar(rstd[:], mv[:, :, 1], LN_EPS, None, ALU.add).then_inc(rstd_step, 1)
    pool.wait_ge(rstd_step, 2)
    nc.gpsimd.tensor_tensor(rstd[:], rstd[:], half[0:S, :], ALU.pow).then_inc(rstd_step, 1)


def double_rstd(nc, pool, mv, half, rvar, rstd2, mv_step, rstd_step, before):
    pool.wait_ge(mv_step, B)
    nc.gpsimd.tensor_scalar(rvar[:], mv[:, :, 1], LN_EPS, LN_EPS, ALU.add, ALU.mult).then_inc(rstd_step, 1)
    pool.wait_ge(rstd_step, before + 1)
    nc.gpsimd.tensor_tensor(rvar[:], rvar[:], mv[:, :, 1], ALU.add).then_inc(rstd_step, 1)
    pool.wait_ge(rstd_step, before + 2)
    nc.gpsimd.tensor_tensor(rstd2[:], rvar[:], half[0:S, :], ALU.pow).then_inc(rstd_step, 1)


def l0_attention(nc, x, stats, ident, passed, A):
    H, DH = 8, 128
    SCALE = float(DH) ** -0.5
    G = B // 2
    QB = 4
    Q, QT = B // QB, QB * S
    with ExitStack() as ctx:
        ph = Phase(nc, ctx, "l0a")
        wo = ph.sb("wo", [128, H, D])
        pos_q, pos_k = ph.sb("pos_q", [DH, S]), ph.sb("pos_k", [DH, 1])
        causal = ph.sb("causal", [S, S])
        mv, half, rstd = ph.sb("mv", [S, B, 2]), ph.sb("half", [S, B]), ph.sb("rstd", [S, B])
        all_qT, qT = ph.sb("all_qT", [DH, H, B * S]), ph.sb("qT", [DH, H, PAIR])
        kT = ph.sb("kT", [DH, B * S])
        all_v, v = ph.sb("all_v", [S, B, DH]), ph.sb("v", [S, 2, DH])
        pT, oT = ph.sb("pT", [S, H, S]), ph.sb("oT", [DH, 2, H, S])
        top, shift = ph.sb("top", [S, 2, H]), ph.sb("shift", [S, 2, H])
        total, inv = ph.sb("total", [S, 2, H]), ph.sb("inv", [S, 2, H])
        x_new, x_stats = ph.sb("x_new", [S, D]), ph.sb("x_stats", [S, 6])

        score_ps = ph.banks("score", 4)
        o_ps, y_ps = ph.banks("o", 2), ph.banks("y", 2)

        weight_w, mv_step, rstd_step = ph.sem("weight_w"), ph.sem("mv_step"), ph.sem("rstd_step")
        norm_ready, inT_done, proj_done = ph.sem("norm_ready"), ph.sem("inT_done"), ph.sem("proj_done")
        act_step, dve_step = ph.sem("act_step"), ph.sem("dve_step")
        qv_ready, x_w, stats_done = ph.sem("qv_ready"), ph.sem("x_w"), ph.sem("stats_done")
        score_done, softmax_step, exp_ready = ph.sem("score_done"), ph.sem("softmax_step"), ph.sem("exp_ready")
        pn_ready, pT_done, pT_ready = ph.sem("pn_ready"), ph.sem("pT_done"), ph.sem("pT_ready")
        o_done, o_ready, y_done, x_step = ph.sem("o_done"), ph.sem("o_ready"), ph.sem("y_done"), ph.sem("x_step")

        WQ_HI = 1

        def in_step(q, k):
            return 2 + k if q == 0 else 3 * q + 1 + k

        def kv_step(q):
            return 3 * q + 6

        WQ_LO = 1

        def lo_step(q):
            return 2 + 9 * q

        def query_step(q, i):
            return 2 + 9 * q + i + 1

        def query_bank(i):
            return (y_ps, o_ps)[i // 2 % 2][:, i % 2, 0:QT]

        with ExitStack() as projections:
            ph_in = Phase(nc, projections, "l0q")
            wq, wk, wv = (ph_in.sb("wq", [128, KC, H * DH]), ph_in.sb("wk", [128, KC, DH]),
                          ph_in.sb("wv", [128, KC, DH]))
            wq_hi, wq_lo = ph_in.sb("wq_hi", [128, KC, H * DH], F32R), ph_in.sb("wq_lo", [128, KC, H * DH], F32R)
            xn, xT = ph_in.sb("xn", [S, QB, D]), ph_in.sb("xT", [128, 2, KC, QT])
            xT_hi, xT_lo = ph_in.sb("xT_hi", [128, 2, KC, QT], F32R), ph_in.sb("xT_lo", [128, 2, KC, QT], F32R)
            block = projections.enter_context(nc.Block())

            @block.sync
            def _(sp):
                sp.dma_start(x[:], A["x"].rearrange("b s d -> s b d")).then_inc(x_w, 16)
                sp.dma_start(ident[:], A["ident"]).then_inc(x_w, 16)
                sp.dma_start(wq[:], A["l0a_wq"].rearrange("(c p) n -> p c n", p=128)).then_inc(weight_w, 16)
                sp.dma_start(wk[:], A["l0a_wk"].rearrange("(c p) n -> p c n", p=128)).then_inc(weight_w, 16)
                sp.dma_start(wv[:], A["l0a_wv"].rearrange("(c p) n -> p c n", p=128)).then_inc(weight_w, 16)
                sp.dma_start(pos_q[:], A["pos_q"]).then_inc(weight_w, 16)
                sp.dma_start(pos_k[:], A["pos_k"]).then_inc(weight_w, 16)
                sp.dma_start(causal[:], A["causal"]).then_inc(weight_w, 16)
                sp.dma_start(wo[:], A["l0a_wo"].rearrange("(h p) n -> p h n", p=128)).then_inc(weight_w, 16)

            @block.gpsimd
            def _(pool):
                single_rstd(nc, pool, mv, half, rstd, mv_step, rstd_step)

            @block.vector
            def _(dve):
                def norm(q):
                    since(dve, inT_done, q)
                    for j in range(QB):
                        b = q * QB + j
                        nc.vector.tensor_scalar(xn[:, j], x[:, b, :], mv[:, b, 0:1], rstd[:, b:b + 1],
                                                ALU.subtract, ALU.mult).then_inc(norm_ready, 1)

                dve.wait_ge(x_w, 32)
                for b in range(B):
                    nc.vector.bn_stats(stats[:, b, :], x[:, b, :]).then_inc(stats_done, 1)
                dve.wait_ge(stats_done, B)
                aggregate(nc, dve, stats, mv, mv_step)
                dve.wait_ge(rstd_step, 3)
                norm(0)
                dve.wait_ge(act_step, WQ_HI)
                nc.vector.tensor_tensor(wq_lo[:], wq[:], wq_hi[:].bitcast(F32), ALU.subtract).then_inc(dve_step, 1)
                for q in range(Q):
                    dve.wait_ge(act_step, in_step(q, 1))
                    if q >= 2:
                        dve.wait_ge(proj_done, 9 * (q - 2) + 8)
                    nc.vector.tensor_tensor(xT_lo[:, q % 2], xT[:, q % 2], xT_hi[:, q % 2].bitcast(F32), ALU.subtract
                                            ).then_inc(dve_step, 1)
                    if q + 1 < Q:
                        norm(q + 1)
                    for i in range(H):
                        dve.wait_ge(proj_done, 9 * q + i + 1)
                        nc.vector.tensor_tensor(
                            all_qT[:, i, q * QT:(q + 1) * QT].rearrange("p (j t) -> p j t", j=QB),
                            query_bank(i).rearrange("p (j t) -> p j t", j=QB),
                            pos_q[:, None, :].broadcast_to([DH, QB, S]), ALU.add).then_inc(dve_step, 1)

            @block.scalar
            def _(act):
                def take_inputs(q):
                    act.wait_ge(inT_done, q + 1)
                    if q >= 2:
                        act.wait_ge(proj_done, 9 * (q - 2) + 9)
                    nc.scalar.activation(xT[:, q % 2], score_ps[:, 2 * (q % 2):2 * (q % 2) + 2, 0:QT], ACT.Copy
                                         ).then_inc(act_step, 1)
                    act.wait_ge(act_step, in_step(q, 0))
                    nc.scalar.activation(xT_hi[:, q % 2], xT[:, q % 2], ACT.Copy).then_inc(act_step, 1)

                act.wait_ge(weight_w, 112)
                nc.scalar.activation(wq_hi[:], wq[:], ACT.Copy).then_inc(act_step, 1)
                take_inputs(0)
                for q in range(Q):
                    if q + 1 < Q:
                        take_inputs(q + 1)
                    act.wait_ge(proj_done, 9 * q + 9)
                    nc.scalar.activation(kT[:, q * QT:(q + 1) * QT], o_ps[:, 0, 0:QT], ACT.Identity, bias=pos_k[:, 0:1])
                    nc.scalar.activation(all_v[:, q * QB:(q + 1) * QB, :].rearrange("p j d -> p (j d)"),
                                         o_ps[0:S, 1, :], ACT.Copy).then_inc(act_step, 1)

            @block.tensor
            def _(pe):
                def transpose_inputs(q):
                    pe.wait_ge(norm_ready, (q + 1) * QB)
                    if q >= 2:
                        pe.wait_ge(act_step, in_step(q - 2, 0))
                    for c in range(KC):
                        for j in range(QB):
                            done = nc.tensor.transpose(score_ps[:, 2 * (q % 2) + c, j * S:(j + 1) * S],
                                                       xn[:, j, c * 128:(c + 1) * 128], ident[0:S, 0:S])
                    done.then_inc(inT_done, 1)

                transpose_inputs(0)
                pe.wait_ge(weight_w, 112)
                pe.wait_ge(dve_step, WQ_LO)
                for q in range(Q):
                    pe.wait_ge(dve_step, lo_step(q))
                    for i in range(H):
                        if i >= 4:
                            pe.wait_ge(dve_step, query_step(q, i - 4))
                        elif q >= 1 and i < 2:
                            pe.wait_ge(dve_step, query_step(q - 1, i + 4))
                        elif q >= 1:
                            pe.wait_ge(act_step, kv_step(q - 1))
                        head = slice(i * DH, (i + 1) * DH)
                        for c in range(KC):
                            hi, lo = xT_hi[:, q % 2, c, :], xT_lo[:, q % 2, c, :]
                            nc.tensor.matmul(query_bank(i), wq_hi[:, c, head], hi, start=(c == 0), stop=False)
                            nc.tensor.matmul(query_bank(i), wq_hi[:, c, head], lo, start=False, stop=False)
                            done = nc.tensor.matmul(query_bank(i), wq_lo[:, c, head], hi, start=False, stop=(c == KC - 1))
                        done.then_inc(proj_done, 1)
                    if q + 1 < Q:
                        transpose_inputs(q + 1)
                    pe.wait_ge(dve_step, query_step(q, 7))
                    for c in range(KC):
                        nc.tensor.matmul(o_ps[:, 0, 0:QT], wk[:, c, :], xT[:, q % 2, c, :],
                                         start=(c == 0), stop=(c == KC - 1))
                    for j in range(QB):
                        for c in range(KC):
                            done = nc.tensor.matmul(o_ps[0:S, 1, j * DH:(j + 1) * DH],
                                                    xT[:, q % 2, c, j * S:(j + 1) * S], wv[:, c, :],
                                                    start=(c == 0), stop=(c == KC - 1))
                    done.then_inc(proj_done, 1)

        p, pn = ph.sb("p", [S, 2, H, S]), ph.sb("pn", [S, 2, H, S])
        with nc.Block() as block:
            @block.gpsimd
            def _(pool):
                def body(g, first, last):
                    for j in range(2):
                        b = g * 2 + j
                        pool.wait_ge(softmax_step, b * 4 + 4)
                        since(pool, pT_done, b * 2 - 2)
                        nc.gpsimd.tensor_tensor(pn[:, j], p[:, j], inv[:, j, :, None].broadcast_to([S, H, S]),
                                                ALU.mult).then_inc(pn_ready, 1)
                over_steps(pool, body, G)

            @block.vector
            def _(dve):
                def softmax(g, j):
                    b = g * 2 + j
                    dve.wait_ge(score_done, b + 1)
                    since(dve, pn_ready, b - 1)
                    nc.vector.tensor_tensor(
                        p[:, j].rearrange("p (a h) s -> p a h s", a=2),
                        score_ps[0:S, 2 * j:2 * j + 2, 0:4 * S].rearrange("p a (h s) -> p a h s", h=4),
                        causal[:, None, None, :].broadcast_to([S, 2, 4, S]), ALU.add).then_inc(softmax_step, 1)
                    dve.wait_ge(softmax_step, b * 4 + 1)
                    nc.vector.tensor_reduce(top[:, j], p[:, j], AX.X, ALU.max).then_inc(softmax_step, 1)
                    dve.wait_ge(softmax_step, b * 4 + 2)
                    nc.vector.tensor_scalar(shift[:, j], top[:, j], -SCALE, None, ALU.mult).then_inc(softmax_step, 1)

                def invert_sums(g, j):
                    b = g * 2 + j
                    dve.wait_ge(exp_ready, b + 1)
                    since(dve, pn_ready, b - 1)
                    nc.vector.reciprocal(inv[:, j], total[:, j]).then_inc(softmax_step, 1)

                def copy_pT(g, j):
                    b = g * 2 + j
                    for a in range(2):
                        dve.wait_ge(pT_done, b * 2 + a + 1)
                        if a == 0:
                            since(dve, o_done, b)
                        nc.vector.tensor_copy(pT[:, 4 * a:4 * a + 4, :].rearrange("p h s -> p (h s)"),
                                              score_ps[0:S, 2 * j + a, 0:4 * S]).then_inc(pT_ready, 1)

                def update(g, j):
                    b = g * 2 + j
                    dve.wait_ge(y_done, b + 1)
                    update_x(nc, dve, x, stats, x_new, x_stats, y_ps[0:S, j, 0:D], b, x_step)

                softmax(0, 0)
                invert_sums(0, 0)

                def body(g, first, last):
                    softmax(g, 1)
                    copy_pT(g, 0)
                    if not first:
                        update(g - 1, 1)
                    invert_sums(g, 1)
                    if not last:
                        softmax(g + 1, 0)
                    copy_pT(g, 1)
                    update(g, 0)
                    if not last:
                        invert_sums(g + 1, 0)
                over_steps(dve, body, G)
                update(G - 1, 1)

            @block.scalar
            def _(act):
                def exp(g, j):
                    act.wait_ge(softmax_step, (g * 2 + j) * 4 + 3)
                    for h in range(H):
                        done = nc.scalar.activation(p[:, j, h, :], p[:, j, h, :], ACT.Exp, scale=SCALE,
                                                    bias=shift[:, j, h:h + 1], accum_out=total[:, j, h:h + 1])
                    done.then_inc(exp_ready, 1)

                def take_queries(g):
                    since(act, score_done, g * 2)
                    nc.scalar.activation(qT[:], all_qT[:, :, bass.ds(g * PAIR, PAIR)], ACT.Copy).then_inc(qv_ready, 1)

                def take_values(g):
                    since(act, o_done, g * 2)
                    nc.scalar.activation(v[:], all_v[:, bass.ds(g * 2, 2), :], ACT.Copy).then_inc(qv_ready, 1)

                def copy_o(g, j):
                    b = g * 2 + j
                    act.wait_ge(o_done, b + 1)
                    since(act, y_done, b - 1)
                    nc.scalar.activation(oT[:, j].rearrange("p (a h) s -> p a (h s)", a=2), o_ps[:, :, 0:4 * S],
                                         ACT.Copy).then_inc(o_ready, 1)

                take_queries(0)
                exp(0, 0)

                def body(g, first, last):
                    take_values(g)
                    if not last:
                        take_queries(g + 1)
                    exp(g, 1)
                    copy_o(g, 0)
                    if not last:
                        exp(g + 1, 0)
                    copy_o(g, 1)
                over_steps(act, body, G)

            @block.tensor
            def _(pe):
                def score(g, j):
                    b = g * 2 + j
                    pe.wait_ge(qv_ready, g * 2 + 1)
                    since(pe, pT_ready, b * 2 - 2)
                    for h in range(H):
                        done = nc.tensor.matmul(score_ps[0:S, 2 * j + h // 4, (h % 4) * S:(h % 4 + 1) * S],
                                                qT[:, h, j * S:(j + 1) * S], kT[:, bass.ds(b * S, S)],
                                                start=True, stop=True)
                    done.then_inc(score_done, 1)

                def transpose_p(g, j):
                    b = g * 2 + j
                    pe.wait_ge(pn_ready, b + 1)
                    for h in range(H):
                        done = nc.tensor.transpose(score_ps[0:S, 2 * j + h // 4, (h % 4) * S:(h % 4 + 1) * S],
                                                   pn[:, j, h, :], ident[0:S, 0:S])
                        if h % 4 == 3:
                            done.then_inc(pT_done, 1)

                def weigh_values(g, j):
                    b = g * 2 + j
                    if j == 0:
                        pe.wait_ge(qv_ready, g * 2 + 2)
                    since(pe, o_ready, b)
                    for a in range(2):
                        pe.wait_ge(pT_ready, b * 2 + a + 1)
                        done = nc.tensor.matmul(o_ps[:, a, 0:4 * S], v[:, j, :], pT[:, 4 * a:4 * a + 4, :],
                                                start=True, stop=True)
                    done.then_inc(o_done, 1)

                def project_out(g, j):
                    b = g * 2 + j
                    pe.wait_ge(o_ready, b + 1)
                    since(pe, x_step, b * 4 - (7 if j == 0 else 3))
                    for c in range(H):
                        done = nc.tensor.matmul(y_ps[0:S, j, 0:D], oT[:, j, c, :], wo[:, c, :],
                                                start=(c == 0), stop=(c == H - 1))
                    done.then_inc(y_done, 1)

                def body(g, first, last):
                    if not first:
                        project_out(g - 1, 1)
                    transpose_p(g, 0)
                    weigh_values(g, 0)
                    if not last:
                        score(g + 1, 0)
                    project_out(g, 0)
                    transpose_p(g, 1)
                    weigh_values(g, 1)
                    if not last:
                        score(g + 1, 1)

                score(0, 0)
                score(0, 1)
                over_steps(pe, body, G)
                project_out(G - 1, 1)


def l0_cross_attention(nc, x, stats, ident, passed, A):
    H, DH = 16, 64
    INNER = H * DH
    NC, CT = 3, N // 3
    KEYS = 488
    KT = KEYS // 4
    SCALE = float(DH) ** -0.5
    with ExitStack() as ctx:
        ph = Phase(nc, ctx, "l0x")
        wq, wkv = ph.sb("wq", [128, KC, INNER]), ph.sb("wkv", [128, KC, 2 * INNER])
        wout = ph.sb("wout", [128, INNER // 128, D])
        affine = ph.sb("affine", [128, 4, KC])
        mv, half = ph.sb("mv", [S, B, 2]), ph.sb("half", [128, B])
        rvar, rstd2 = ph.sb("rvar", [S, B]), ph.sb("rstd2", [S, B])
        c_in, c_norm = ph.sb("c_in", [CT, NC, D]), ph.sb("c_norm", [CT, NC, D])
        c_stats, c_mv = ph.sb("c_stats", [CT, NC, 6]), ph.sb("c_mv", [CT, NC, 2])
        c_var, c_rstd = ph.sb("c_var", [CT, NC]), ph.sb("c_rstd", [CT, NC])
        lat, zeros = ph.sb("lat", [S, D]), ph.sb("zeros", [128, D])
        mask_in, bias = ph.sb("mask_in", [S, MASK_WORDS], U32), ph.sb("bias", [S, KEYS])
        wkv_hi, wkv_lo = ph.sb("wkv_hi", [128, KC, 2 * INNER], F32R), ph.sb("wkv_lo", [128, KC, 2 * INNER], F32R)
        kvT = ph.sb("kvT", [128, KC, KEYS])
        kvT_hi, kvT_lo = ph.sb("kvT_hi", [128, KC, KEYS], F32R), ph.sb("kvT_lo", [128, KC, KEYS], F32R)
        q_hi, q_lo = ph.sb("q_hi", [128, 2, H // 2, S], F32R), ph.sb("q_lo", [128, 2, H // 2, S], F32R)
        kT_hi, kT_lo = ph.sb("kT_hi", [128, H // 2, KEYS], F32R), ph.sb("kT_lo", [128, H // 2, KEYS], F32R)
        v = ph.sb("v", [KT, 4, INNER])
        s_sb, p = ph.sb("s", [S, 2, KEYS]), ph.sb("p", [S, 3, KEYS])
        low, total = ph.sb("low", [S, H]), ph.sb("total", [S, H])
        inv, inv_total = ph.sb("inv", [S, 2]), ph.sb("inv_total", [S, 2, S])
        pT = ph.sb("pT", [KT, 2, 4 * S])
        oT = ph.sb("oT", [128, INNER // 128, S])
        x_new, x_stats = ph.sb("x_new", [S, D]), ph.sb("x_stats", [S, 6])

        score_ps, pT_ps, oT_ps = ph.banks("score", 2), ph.banks("pT", 2), ph.banks("oT", 2)
        proj_ps = ph.banks("proj", 2)

        weight_w, const_w, ctx_w, mask_w = ph.sem("weight_w"), ph.sem("const_w"), ph.sem("ctx_w"), ph.sem("mask_w")
        mv_step, rstd_step, zeroed = ph.sem("mv_step"), ph.sem("rstd_step"), ph.sem("zeroed")
        padded = ph.sem("padded")
        c_step, c_rstd_step = ph.sem("c_step"), ph.sem("c_rstd_step")
        norm_ready, bias_ready = ph.sem("norm_ready"), ph.sem("bias_ready")
        proj_done, kvT_ready = ph.sem("proj_done"), ph.sem("kvT_ready")
        v_even_ready, v_odd_ready = ph.sem("v_even_ready"), ph.sem("v_odd_ready")
        score_done, masked_ready, exp_ready = ph.sem("score_done"), ph.sem("masked_ready"), ph.sem("exp_ready")
        pT_done, pT_even_ready, pT_odd_ready = ph.sem("pT_done"), ph.sem("pT_even_ready"), ph.sem("pT_odd_ready")
        pv_done, inv_step = ph.sem("pv_done"), ph.sem("inv_step")
        oT_even_ready, oT_odd_ready = ph.sem("oT_even_ready"), ph.sem("oT_odd_ready")
        act_start, w_lo_ready = ph.sem("act_start"), ph.sem("w_lo_ready")
        hi_ready, lo_ready = ph.sem("hi_ready"), ph.sem("lo_ready")
        y_done, x_step = ph.sem("y_done"), ph.sem("x_step")

        T0, Q0, K0, V0, USES = 0, 2, 4, 12, 20
        SPLIT_Q, SPLIT_K, SPLITS = 2, 4, 12
        PARTS = [(c, slice(n * INNER, (n + 1) * INNER)) for n in range(2) for c in range(KC)]

        def key_bank(i):
            return (proj_ps, score_ps)[i // 2 % 2][:, i % 2, 0:KEYS]

        block = ctx.enter_context(nc.Block())

        @block.sync
        def _(sp):
            sp.dma_start(affine[:], A["l0x_affine"]).then_inc(const_w, 16)
            def load_ctx(b):
                sp.dma_start(c_in[:], A["ctx"][bass.ds(b, 1)].rearrange("b (c p) d -> p (b c) d", p=CT)
                             ).then_inc(ctx_w, 16)
                sp.dma_start(mask_in[:], A["ctx_mask"][bass.ds(b, 1), :].broadcast_to([S, MASK_WORDS])).then_inc(mask_w, 16)

            load_ctx(0)
            sp.dma_start(wq[:], A["l0x_wq"].rearrange("(c p) n -> p c n", p=128)).then_inc(weight_w, 16)
            all_wkv = A["l0x_wkv"].rearrange("(c p) n -> p c n", p=128)
            sp.dma_start(wkv[:, :, 0:INNER], all_wkv[:, :, 0:INNER]).then_inc(weight_w, 16)
            sp.wait_ge(weight_w, 32)
            sp.dma_start(wkv[:, :, INNER:], all_wkv[:, :, INNER:]).then_inc(weight_w, 16)
            sp.dma_start(wout[:], A["l0x_wout"].rearrange("(c p) n -> p c n", p=128)).then_inc(weight_w, 16)
            sp.wait_ge(zeroed, 5)
            sp.dma_start(A["sorted_x"].rearrange("(t p) d -> p t d", p=128),
                         zeros[:, None, :].broadcast_to([128, SORTED_TILES + 1, D])).then_inc(padded, 16)
            with sp.Fori(1, B) as b:
                sp.wait_ge(norm_ready, b * 4)
                sp.wait_ge(bias_ready, b)
                load_ctx(b)
            sp.wait_ge(padded, 16)

        @block.gpsimd
        def _(pool):
            nc.gpsimd.memset(half[:], -0.5).then_inc(zeroed, 1)
            nc.gpsimd.memset(kvT[:, :, N + S:KEYS], 0.0).then_inc(zeroed, 1)
            nc.gpsimd.memset(bias[:, N:N + S], 0.0).then_inc(zeroed, 1)
            nc.gpsimd.memset(bias[:, N + S:KEYS], NEG).then_inc(zeroed, 1)
            nc.gpsimd.memset(zeros[:], 0.0).then_inc(zeroed, 1)

            def context_rstd(b):
                since(pool, norm_ready, b * 4)
                wait_apart(pool, c_step, b * 6 + 6, passed)
                nc.gpsimd.tensor_scalar(c_var[:], c_mv[:, :, 1], LN_EPS, None, ALU.add).then_inc(c_rstd_step, 1)
                pool.wait_ge(c_rstd_step, b * 2 + 1)
                nc.gpsimd.tensor_tensor(c_rstd[:], c_var[:], half[0:CT, 0:NC], ALU.pow).then_inc(c_rstd_step, 1)

            def mask_bias(b):
                since(pool, mask_w, b * 16 + 16)
                wait_apart(pool, masked_ready, b * H, passed)
                nc.gpsimd.tensor_scalar(bias[:, 0:N], mask_in[:].bitcast(U8)[:, 0:N], 1.0, -NEG, ALU.subtract, ALU.mult
                                        ).then_inc(bias_ready, 1)

            pool.wait_ge(zeroed, 5)
            double_rstd(nc, pool, mv, half, rvar, rstd2, mv_step, rstd_step, 0)
            context_rstd(0)
            mask_bias(0)
            with pool.Fori(1, B) as b:
                context_rstd(b)
                mask_bias(b)

        @block.vector
        def _(dve):
            def context_stats(b):
                dve.wait_ge(ctx_w, b * 16 + 16)
                for t in range(NC):
                    nc.vector.bn_stats(c_stats[:, t, :], c_in[:, t, :]).then_inc(c_step, 1)
                for t in range(NC):
                    wait_apart(dve, c_step, b * 6 + t + 1, passed)
                    nc.vector.bn_aggr(c_mv[:, t, :], c_stats[:, t, :]).then_inc(c_step, 1)

            def normalise(b):
                since(dve, proj_done, b * USES - USES + 2)
                dve.wait_ge(c_rstd_step, b * 2 + 2)
                for t in range(NC):
                    nc.vector.tensor_scalar(c_norm[:, t, :], c_in[:, t, :], c_mv[:, t, 0:1], c_rstd[:, t:t + 1],
                                            ALU.subtract, ALU.mult).then_inc(norm_ready, 1)
                nc.vector.tensor_scalar(lat[:], x[:, b, :], mv[:, b, 0:1], rstd2[:, bass.ds(b, 1)],
                                        ALU.subtract, ALU.mult).then_inc(norm_ready, 1)

            def transposed_inputs(b):
                for c in range(KC):
                    dve.wait_ge(proj_done, b * USES + T0 + c + 1)
                    for (lo, hi, a) in ((0, N, 0), (N, N + S, 2)):
                        done = nc.vector.tensor_scalar(kvT[:, c, lo:hi], proj_ps[:, c, lo:hi], affine[:, a, c:c + 1],
                                                       affine[:, a + 1, c:c + 1], ALU.mult, ALU.add)
                    done.then_inc(kvT_ready, 1)

            def split_inputs(b):
                for c in range(KC):
                    dve.wait_ge(hi_ready, b * SPLITS + c + 1)
                    nc.vector.tensor_tensor(kvT_lo[:, c, :], kvT[:, c, :], kvT_hi[:, c, :].bitcast(F32), ALU.subtract
                                            ).then_inc(lo_ready, 1)

            def split_weights(begin, end):
                for n in range(begin, end):
                    c, part = PARTS[n]
                    dve.wait_ge(act_start, n + 3)
                    nc.vector.tensor_tensor(wkv_lo[:, c, part], wkv[:, c, part],
                                            wkv_hi[:, c, part].bitcast(F32), ALU.subtract).then_inc(w_lo_ready, 1)

            def split_queries_and_keys(b, first):
                for i in range(2):
                    dve.wait_ge(hi_ready, b * SPLITS + SPLIT_Q + i + 1)
                    for a in range(2):
                        half_of = slice(a * DH, (a + 1) * DH)
                        done = nc.vector.tensor_tensor(
                            q_lo[half_of, a, 4 * i:4 * i + 4, :].rearrange("p h s -> p (h s)"),
                            proj_ps[half_of, i, 0:4 * S],
                            q_hi[half_of, a, 4 * i:4 * i + 4, :].rearrange("p h s -> p (h s)").bitcast(F32), ALU.subtract)
                    done.then_inc(lo_ready, 1)
                if first:
                    split_weights(KC, len(PARTS))
                for i in range(8):
                    dve.wait_ge(hi_ready, b * SPLITS + SPLIT_K + i + 1)
                    nc.vector.tensor_tensor(kT_lo[:, i, :], key_bank(i), kT_hi[:, i, :].bitcast(F32), ALU.subtract
                                            ).then_inc(lo_ready, 1)

            def values(b):
                for i in range(1, 8, 2):
                    dve.wait_ge(proj_done, b * USES + V0 + i + 1)
                    nc.vector.tensor_copy(v[:, i // 2, 512:1024], proj_ps[0:KT, 1, :]).then_inc(v_odd_ready, 1)

            def mask_score(b, h):
                if h == 0:
                    dve.wait_ge(bias_ready, b + 1)
                since(dve, exp_ready, b * H + h - 1)
                wait_apart(dve, score_done, b * H + h + 1, passed)
                nc.vector.tensor_tensor_reduce(s_sb[:, h % 2, :], score_ps[0:S, h % 2, 0:KEYS], bias[:], -SCALE, 3.4e38,
                                               ALU.add, ALU.min, low[:, h:h + 1]).then_inc(masked_ready, 1)

            def copy_pT(b, h):
                if h % 2 == 1:
                    since(dve, pv_done, b * H + h - 1)
                    dve.wait_ge(pT_done, b * H + h + 1)
                    nc.vector.tensor_copy(pT[:, 1, :], pT_ps[0:KT, 1, 0:4 * S]).then_inc(pT_odd_ready, 1)

            def invert_total(b, h):
                since(dve, pT_done, b * H + h - 1)
                dve.wait_ge(exp_ready, b * H + h + 1)
                nc.vector.reciprocal(inv[:, h % 2:h % 2 + 1], total[:, h:h + 1]).then_inc(inv_step, 1)
                dve.wait_ge(inv_step, (b * H + h) * 2 + 1)
                nc.vector.tensor_scalar(inv_total[:, h % 2, :], ident[0:S, 0:S], inv[:, h % 2:h % 2 + 1], None, ALU.mult
                                        ).then_inc(inv_step, 1)

            def copy_oT(b):
                dve.wait_ge(pv_done, b * H + H)
                since(dve, y_done, b)
                nc.vector.tensor_copy(oT[:, 4:8, :].rearrange("p h s -> p (h s)"), oT_ps[:, 1, 0:4 * S]
                                      ).then_inc(oT_odd_ready, 1)

            def update(b):
                dve.wait_ge(y_done, b + 1)
                update_x(nc, dve, x, stats, x_new, x_stats, proj_ps[0:S, 1, 0:D], b, x_step)

            aggregate(nc, dve, stats, mv, mv_step)
            context_stats(0)
            dve.wait_ge(rstd_step, 3)
            dve.wait_ge(const_w, 16)
            normalise(0)

            def body(b, first, last):
                if not first:
                    invert_total(b - 1, H - 1)
                transposed_inputs(b)
                if first:
                    split_weights(0, KC)
                if not first:
                    copy_pT(b - 1, H - 1)
                split_inputs(b)
                if not first:
                    copy_oT(b - 1)
                split_queries_and_keys(b, first)
                values(b)
                for h in range(H):
                    mask_score(b, h)
                    if h >= 1:
                        invert_total(b, h - 1)
                    if h >= 2:
                        copy_pT(b, h - 2)
                    if h == 2 and not first:
                        update(b - 1)
                    if h == 4 and not last:
                        context_stats(b + 1)
                    if h == 8 and not last:
                        normalise(b + 1)
            over_steps(dve, body, B)
            invert_total(B - 1, H - 1)
            copy_pT(B - 1, H - 1)
            copy_oT(B - 1)
            update(B - 1)

        @block.scalar
        def _(act):
            def round_inputs(b):
                for c in range(KC):
                    act.wait_ge(kvT_ready, b * KC + c + 1)
                    nc.scalar.activation(kvT_hi[:, c, :], kvT[:, c, :], ACT.Copy).then_inc(hi_ready, 1)

            def round_weights(parts, loaded):
                act.wait_ge(weight_w, loaded)
                for c, part in parts:
                    nc.scalar.activation(wkv_hi[:, c, part], wkv[:, c, part], ACT.Copy).then_inc(act_start, 1)

            def round_queries_and_keys(b, first):
                if isinstance(b, int) and b == 0:
                    act.wait_ge(act_start, 2)
                for i in range(2):
                    act.wait_ge(proj_done, b * USES + Q0 + i + 1)
                    for a in range(2):
                        half_of = slice(a * DH, (a + 1) * DH)
                        done = nc.scalar.activation(
                            q_hi[half_of, a, 4 * i:4 * i + 4, :].rearrange("p h s -> p (h s)"),
                            proj_ps[half_of, i, 0:4 * S], ACT.Copy)
                    done.then_inc(hi_ready, 1)
                if first:
                    round_weights(PARTS[KC:], 64)
                for i in range(8):
                    act.wait_ge(proj_done, b * USES + K0 + i + 1)
                    nc.scalar.activation(kT_hi[:, i, :], key_bank(i), ACT.Copy).then_inc(hi_ready, 1)

            def values(b):
                for i in range(0, 8, 2):
                    act.wait_ge(proj_done, b * USES + V0 + i + 1)
                    nc.scalar.activation(v[:, i // 2, 0:512], proj_ps[0:KT, 0, :], ACT.Copy).then_inc(v_even_ready, 1)

            def exp(b, h):
                act.wait_ge(masked_ready, b * H + h + 1)
                if h >= 3:
                    act.wait_ge(pT_done, b * H + h - 2)
                nc.scalar.activation(p[:, h % 3, :], s_sb[:, h % 2, :], ACT.Exp, scale=-1.0, bias=low[:, h:h + 1],
                                     accum_out=total[:, h:h + 1]).then_inc(exp_ready, 1)

            def copy_pT(b, h):
                if h % 2 == 0:
                    since(act, pv_done, b * H + h - 1)
                    act.wait_ge(pT_done, b * H + h + 1)
                    nc.scalar.activation(pT[:, 0, :], pT_ps[0:KT, 0, 0:4 * S], ACT.Copy).then_inc(pT_even_ready, 1)

            def copy_oT(b):
                act.wait_ge(pv_done, b * H + H)
                since(act, y_done, b)
                nc.scalar.activation(oT[:, 0:4, :].rearrange("p h s -> p (h s)"), oT_ps[:, 0, 0:4 * S], ACT.Copy
                                     ).then_inc(oT_even_ready, 1)

            act.wait_ge(zeroed, 5)
            for q in (q_hi, q_lo):
                nc.scalar.activation(q[:].rearrange("p a h s -> p (a h) s"), ident[:, None, 0:S].broadcast_to([128, H, S]),
                                     ACT.Copy, scale=0.0).then_inc(act_start, 1)
            round_weights(PARTS[:KC], 32)

            def body(b, first, last):
                if not first:
                    copy_pT(b - 1, H - 2)
                round_inputs(b)
                if not first:
                    copy_oT(b - 1)
                round_queries_and_keys(b, first)
                values(b)
                if not first:
                    act.wait_ge(inv_step, b * H * 2)
                for h in range(H):
                    exp(b, h)
                    if h >= 2:
                        copy_pT(b, h - 2)
            over_steps(act, body, B)
            copy_pT(B - 1, H - 2)
            copy_oT(B - 1)

        @block.tensor
        def _(pe):
            def exact_product(out, a_hi, a_lo, b_hi, b_lo, first, last):
                nc.tensor.matmul(out, a_hi, b_hi, start=first, stop=False)
                nc.tensor.matmul(out, a_hi, b_lo, start=False, stop=False)
                return nc.tensor.matmul(out, a_lo, b_hi, start=False, stop=last)

            def transpose_inputs(b):
                pe.wait_ge(norm_ready, b * 4 + 4)
                for c in range(KC):
                    since(pe, (v_even_ready, v_odd_ready)[c], b * 4)
                    for t in range(NC):
                        nc.tensor.transpose(proj_ps[:, c, t * CT:(t + 1) * CT], c_norm[:, t, c * 128:(c + 1) * 128],
                                            ident[0:CT, 0:CT])
                    nc.tensor.transpose(proj_ps[:, c, N:N + S], lat[:, c * 128:(c + 1) * 128], ident[0:S, 0:S]
                                        ).then_inc(proj_done, 1)

            def project_q_and_k(b):
                pe.wait_ge(kvT_ready, b * KC + KC)
                for i in range(2):
                    for k in range(4):
                        at = (4 * i + k) * 128
                        for c in range(KC):
                            done = nc.tensor.matmul(proj_ps[:, i, k * S:(k + 1) * S], wq[:, c, at:at + 128],
                                                    kvT[:, c, N:N + S], start=(c == 0), stop=(c == KC - 1))
                    done.then_inc(proj_done, 1)
                for i in range(8):
                    if i < 2:
                        pe.wait_ge(lo_ready, b * SPLITS + SPLIT_Q + i + 1)
                    elif i < 4:
                        since(pe, masked_ready, b * H)
                    else:
                        pe.wait_ge(lo_ready, b * SPLITS + SPLIT_K + i - 3)
                    at = slice(i * 128, (i + 1) * 128)
                    for c in range(KC):
                        done = exact_product(key_bank(i), wkv_hi[:, c, at], wkv_lo[:, c, at],
                                             kvT_hi[:, c, :], kvT_lo[:, c, :], c == 0, c == KC - 1)
                    done.then_inc(proj_done, 1)

            def project_v(b):
                for i in range(8):
                    if i < 2:
                        pe.wait_ge(lo_ready, b * SPLITS + SPLIT_K + 4 + i + 1)
                    else:
                        pe.wait_ge((v_even_ready, v_odd_ready)[i % 2], b * 4 + i // 2)
                    keys = slice((i // 2) * KT, (i // 2 + 1) * KT)
                    at = slice(INNER + (i % 2) * 512, INNER + (i % 2) * 512 + 512)
                    for c in range(KC):
                        done = exact_product(proj_ps[0:KT, i % 2, :], kvT_hi[:, c, keys], kvT_lo[:, c, keys],
                                             wkv_hi[:, c, at], wkv_lo[:, c, at], c == 0, c == KC - 1)
                    done.then_inc(proj_done, 1)

            def score(b, h):
                if h == 0:
                    pe.wait_ge(lo_ready, b * SPLITS + SPLITS)
                since(pe, masked_ready, b * H + h - 1)
                exact_product(score_ps[0:S, h % 2, 0:KEYS], q_hi[:, h % 2, h // 2, :], q_lo[:, h % 2, h // 2, :],
                              kT_hi[:, h // 2, :], kT_lo[:, h // 2, :], True, True).then_inc(score_done, 1)

            def transpose_p(b, h):
                since(pe, (pT_even_ready, pT_odd_ready)[h % 2], b * (H // 2) + h // 2)
                pe.wait_ge(inv_step, (b * H + h) * 2 + 2)
                for t in range(4):
                    done = nc.tensor.matmul(pT_ps[0:KT, h % 2, t * S:(t + 1) * S], p[:, h % 3, t * KT:(t + 1) * KT],
                                            inv_total[:, h % 2, :], start=True, stop=True)
                done.then_inc(pT_done, 1)

            def weigh_values(b, h):
                if h == 0:
                    pe.wait_ge(v_even_ready, b * 4 + 4)
                    pe.wait_ge(v_odd_ready, b * 4 + 4)
                    since(pe, oT_even_ready, b)
                    since(pe, oT_odd_ready, b)
                pe.wait_ge((pT_even_ready, pT_odd_ready)[h % 2], b * (H // 2) + h // 2 + 1)
                i, at = h // 2, (h % 2) * DH
                for t in range(4):
                    done = nc.tensor.matmul(oT_ps[at:at + DH, i // 4, (i % 4) * S:(i % 4 + 1) * S],
                                            v[:, t, h * DH:(h + 1) * DH], pT[:, h % 2, t * S:(t + 1) * S],
                                            start=(t == 0), stop=(t == 3))
                done.then_inc(pv_done, 1)

            def finish_heads(b):
                transpose_p(b, H - 2)
                weigh_values(b, H - 3)
                transpose_p(b, H - 1)
                weigh_values(b, H - 2)
                weigh_values(b, H - 1)

            def project_out(b, emptied):
                since(pe, v_odd_ready, emptied)
                pe.wait_ge(oT_even_ready, b + 1)
                pe.wait_ge(oT_odd_ready, b + 1)
                for c in range(INNER // 128):
                    done = nc.tensor.matmul(proj_ps[0:S, 1, 0:D], oT[:, c, :], wout[:, c, :],
                                            start=(c == 0), stop=(c == INNER // 128 - 1))
                done.then_inc(y_done, 1)

            def body(b, first, last):
                transpose_inputs(b)
                if first:
                    pe.wait_ge(weight_w, 32)
                    pe.wait_ge(w_lo_ready, KC)
                if not first:
                    finish_heads(b - 1)
                project_q_and_k(b)
                if first:
                    pe.wait_ge(weight_w, 64)
                    pe.wait_ge(w_lo_ready, len(PARTS))
                project_v(b)
                for h in range(H):
                    score(b, h)
                    if h == 1 and not first:
                        project_out(b - 1, b * 4 + 4)
                    if h >= 2:
                        transpose_p(b, h - 2)
                    if h >= 3:
                        weigh_values(b, h - 3)
                if not first:
                    pe.wait_ge(x_step, b * 4 - 3)
            over_steps(pe, body, B)
            finish_heads(B - 1)
            project_out(B - 1, B * 4)


def l0_experts(nc, x, stats, ident, passed, A):
    E, F = 8, 1024
    FC = F // 128
    GB = 4
    TILES = SORTED_TILES
    with ExitStack() as ctx:
        ph = Phase(nc, ctx, "l0f")
        w1 = ph.sb("w1", [128, KC, E * F])
        wo, wr = ph.sb("wo", [128, FC, D]), ph.sb("wr", [128, KC, E])
        rows = ph.sb("rows", [128, 3, D])
        before, ones = ph.sb("before", [S, S]), ph.sb("ones", [S, S])
        expert_no, tile_no = ph.sb("expert_no", [S, E]), ph.sb("tile_no", [1, TILES])
        mv, half, rstd = ph.sb("mv", [S, B, 2]), ph.sb("half", [S, B]), ph.sb("rstd", [S, B])
        x1 = ph.sb("x1", [S, B, D])
        x1T = ph.sb("x1T", [128, 2, 2, KC, S])
        logits, best, best_no = ph.sb("logits", [S, B, E]), ph.sb("best", [S, B, 8]), ph.sb("best_no", [S, B, 8], U32)
        expert = ph.sb("expert", [S, B])
        one_hot, rank = ph.sb("one_hot", [S, B, E]), ph.sb("rank", [S, B, E])
        sums = ph.sb("sums", [S, 2, B, E])
        tiles, tiles_i = ph.sb("tiles", [S, 4, E]), ph.sb("tiles_i", [S, E], mybir.dt.int32)
        slot, slot_i = ph.sb("slot", [S, B]), ph.sb("slot_i", [S, B], U32)
        after = ph.sb("after", [1, TILES, E])
        tile_expert, tile_expert_i = ph.sb("tile_expert", [1, TILES]), ph.sb("tile_expert_i", [1, TILES], mybir.dt.int32)
        xs, xsT = ph.sb("xs", [128, D]), ph.sb("xsT", [128, KC, 128])
        b1 = ph.sb("b1", [128, F])
        pre, h, hT = ph.sb("pre", [128, F]), ph.sb("h", [128, F]), ph.sb("hT", [128, FC, 128])
        ys = ph.sb("ys", [128, D])
        y = ph.sb("y", [S, B, D])
        y_stats, y_mv = ph.sb("y_stats", [S, B, 6]), ph.sb("y_mv", [S, B, 2])
        y_rstd = ph.sb("y_rstd", [S, B])
        sorted_x = A["sorted_x"]
        sorted_y = nc.dram_tensor("sorted_y", (TILES * 128, D), F32, kind="Internal").ap()

        route_ps, xT_ps = ph.banks("route", 1), ph.banks("xT", 1)
        pre_ps, hT_ps, y_ps = ph.banks("pre", 2), ph.banks("hT", 2), ph.banks("y", 1)

        weight_w, const_w = ph.sem("weight_w"), ph.sem("const_w")
        mv_step, rstd_step = ph.sem("mv_step"), ph.sem("rstd_step")
        x1_ready, xT_done, xT_ready = ph.sem("x1_ready"), ph.sem("xT_done"), ph.sem("xT_ready")
        router_done, route_step = ph.sem("router_done"), ph.sem("route_step")
        rank_done = ph.sem("rank_done")
        scattered, xs_w, b1_w = ph.sem("scattered"), ph.sem("xs_w"), ph.sem("b1_w")
        xsT_done, xsT_ready, pre_done = ph.sem("xsT_done"), ph.sem("xsT_ready"), ph.sem("pre_done")
        pre_ready, hT_done = ph.sem("pre_ready"), ph.sem("hT_done")
        hT_even_ready, hT_odd_ready = ph.sem("hT_even_ready"), ph.sem("hT_odd_ready")
        gelu_ready, y_done, ys_ready, ys_w = ph.sem("gelu_ready"), ph.sem("y_done"), ph.sem("ys_ready"), ph.sem("ys_w")
        gathered = [ph.sem("gathered0"), ph.sem("gathered1"), ph.sem("gathered2"), ph.sem("gathered3")]
        y_step, y_rstd_ready, x_step = ph.sem("y_step"), ph.sem("y_rstd_ready"), ph.sem("x_step")

        slot_ready, beta_added = ph.sem("slot_ready"), ph.sem("beta_added")
        block = ctx.enter_context(nc.Block())

        @block.sync
        def _(sp):
            sp.dma_start(wr[:], A["l0f_wr"].rearrange("(c p) n -> p c n", p=128)).then_inc(const_w, 16)
            sp.dma_start(before[:], A["before"]).then_inc(const_w, 16)
            sp.dma_start(expert_no[:], A["expert_no"].broadcast_to([S, E])).then_inc(const_w, 16)
            sp.dma_start(tile_no[:], A["tile_no"]).then_inc(const_w, 16)
            sp.dma_start(rows[:], A["l0f_rows"].broadcast_to([128, 3, D])).then_inc(const_w, 16)
            for c in range(KC):
                sp.dma_start(w1[:, c, :].rearrange("p (e n) -> p e n", e=E),
                             A["l0f_w1"][:, c * 128:(c + 1) * 128, :].rearrange("e p n -> p e n")).then_inc(weight_w, 16)
            sp.dma_start(wo[:], A["l0f_wo"].rearrange("(c p) n -> p c n", p=128)).then_inc(weight_w, 16)

            def load_b1(i):
                e = sp.value_load(tile_expert_i[0:1, bass.ds(i, 1)], min_val=0, max_val=(E - 1) * F)
                sp.dma_start(b1[:], A["l0f_b1"][:, bass.ds(e, F)].broadcast_to([128, F])).then_inc(b1_w, 16)

            def load_tile(i):
                sp.dma_start(xs[:], sorted_x[bass.ds(i * 128, 128), :]).then_inc(xs_w, 16)

            def store_tile(i):
                sp.wait_ge(ys_ready, i + 1)
                sp.dma_start(sorted_y[bass.ds(i * 128, 128), :], ys[:]).then_inc(ys_w, 16)

            sp.wait_ge(scattered, 16 * B)
            load_tile(0)
            sp.wait_ge(xsT_done, 1)
            load_tile(1)
            sp.wait_ge(slot_ready, 2)
            load_b1(0)
            with sp.Fori(0, TILES - 1) as i:
                sp.wait_ge(xsT_done, i + 2)
                load_tile(i + 2)
                sp.wait_ge(pre_ready, i + 1)
                load_b1(i + 1)
                store_tile(i)
            store_tile(TILES - 1)

        @block.gpsimd
        def _(pool):
            single_rstd(nc, pool, mv, half, rstd, mv_step, rstd_step)
            nc.gpsimd.memset(ones[:], 1.0).then_inc(rstd_step, 1)
            pool.wait_ge(x1_ready, B)
            pool.wait_ge(slot_ready, 1)
            for b in range(B):
                nc.gpsimd.indirect_dma_start(sorted_x, bass.IndirectOffsetOnAxis(slot_i[:, b:b + 1], 0), x1[:, b, :],
                                             None).then_inc(scattered, 16)
            for b in range(B):
                nc.gpsimd.tensor_tensor(x[:, b, :], x[:, b, :], rows[0:S, 2, :], ALU.add).then_inc(beta_added, 1)

            def gather(q):
                for b in range(q * GB, (q + 1) * GB):
                    nc.gpsimd.indirect_dma_start(y[:, b, :], None, sorted_y,
                                                 bass.IndirectOffsetOnAxis(slot_i[:, b:b + 1], 0)
                                                 ).then_inc(gathered[q], 16)

            def invert_deviation(q):
                pool.wait_ge(y_step, (q + 1) * 3 * GB)
                group = slice(q * GB, (q + 1) * GB)
                nc.gpsimd.tensor_scalar(y_rstd[:, group], y_mv[:, group, 1], 1e-12, None, ALU.add
                                        ).then_inc(y_rstd_ready, 1)
                pool.wait_ge(y_rstd_ready, 2 * q + 1)
                nc.gpsimd.tensor_tensor(y_rstd[:, group], y_rstd[:, group], half[:, group], ALU.pow
                                        ).then_inc(y_rstd_ready, 1)

            pool.wait_ge(ys_w, 16 * TILES)
            gather(0)
            for q in range(1, B // GB):
                gather(q)
                invert_deviation(q - 1)
            invert_deviation(B // GB - 1)

        @block.vector
        def _(dve):
            steps = [0]

            def step(instruction):
                steps[0] += 1
                instruction.then_inc(route_step, 1)
                dve.wait_ge(route_step, steps[0])

            aggregate(nc, dve, stats, mv, mv_step)
            dve.wait_ge(rstd_step, 3)
            for b in range(B):
                nc.vector.tensor_scalar(x1[:, b, :], x[:, b, :], mv[:, b, 0:1], rstd[:, b:b + 1],
                                        ALU.subtract, ALU.mult).then_inc(x1_ready, 1)
            dve.wait_ge(router_done, B // 2)
            step(nc.vector.tensor_copy(logits[:].rearrange("p b e -> p (b e)"), route_ps[0:S, 0, 0:B * E]))
            for b in range(B):
                nc.vector.max(best[:, b, :], logits[:, b, :]).then_inc(route_step, 1)
            for b in range(B):
                dve.wait_ge(route_step, b + 2)
                nc.vector.max_index(best_no[:, b, :], best[:, b, :], logits[:, b, :]).then_inc(route_step, 1)
            steps[0] += 2 * B
            dve.wait_ge(route_step, steps[0])
            step(nc.vector.tensor_copy(expert[:], best_no[:, :, 0]))
            dve.wait_ge(const_w, 80)
            step(nc.vector.tensor_tensor(one_hot[:], expert_no[:, None, :].broadcast_to([S, B, E]),
                                         expert[:, :, None].broadcast_to([S, B, E]), ALU.is_equal))
            dve.wait_ge(rank_done, 1)
            nc.vector.tensor_copy(rank[:].rearrange("p b e -> p (b e)"), route_ps[0:S, 0, 128:256])
            step(nc.vector.tensor_copy(sums[:, 0].rearrange("p b e -> p (b e)"), route_ps[0:S, 0, 256:384]))
            for n, d in enumerate((1, 2, 4, 8)):
                a, z = sums[:, n % 2], sums[:, (n + 1) % 2]
                nc.vector.tensor_copy(z[:, 0:d, :], a[:, 0:d, :])
                step(nc.vector.tensor_tensor(z[:, d:B, :], a[:, d:B, :], a[:, 0:B - d, :], ALU.add))
            step(nc.vector.tensor_scalar(tiles_i[:], sums[:, 0, B - 1, :], 127.0, None, ALU.add))
            step(nc.vector.tensor_scalar(tiles_i[:], tiles_i[:], 7, None, ALU.arith_shift_right))
            step(nc.vector.tensor_copy(tiles[:, 0, :], tiles_i[:]))
            for n, d in enumerate((1, 2, 4)):
                nc.vector.tensor_copy(tiles[:, n + 1, 0:d], tiles[:, n, 0:d])
                step(nc.vector.tensor_tensor(tiles[:, n + 1, d:E], tiles[:, n, d:E], tiles[:, n, 0:E - d], ALU.add))
            step(nc.vector.tensor_tensor(tiles[:, 0, :], tiles[:, 3, :], tiles[:, 0, :], ALU.subtract))
            step(nc.vector.tensor_scalar(tiles[:, 1, :], tiles[:, 0, :], 128.0, None, ALU.mult))
            step(nc.vector.tensor_tensor(rank[:, 1:B, :], rank[:, 1:B, :], sums[:, 0, 0:B - 1, :], ALU.add))
            step(nc.vector.tensor_tensor(rank[:], rank[:], tiles[:, 1:2, :].broadcast_to([S, B, E]), ALU.add))
            step(nc.vector.tensor_tensor(rank[:], rank[:], one_hot[:], ALU.mult))
            step(nc.vector.tensor_reduce(slot[:], rank[:], AX.X, ALU.add))
            nc.vector.tensor_copy(slot_i[:], slot[:]).then_inc(slot_ready, 1)
            step(nc.vector.tensor_tensor(after[:], tile_no[:, :, None].broadcast_to([1, TILES, E]),
                                         tiles[0:1, 3:4, :].broadcast_to([1, TILES, E]), ALU.is_ge))
            step(nc.vector.tensor_reduce(tile_expert[:], after[:], AX.X, ALU.add))
            step(nc.vector.tensor_scalar(tile_expert[:], tile_expert[:], float(E - 1), float(F), ALU.min, ALU.mult))
            nc.vector.tensor_copy(tile_expert_i[:], tile_expert[:]).then_inc(slot_ready, 1)

            def add_bias(i):
                since(dve, pre_done, i + 1)
                dve.wait_ge(b1_w, i * 16 + 16)
                since(dve, gelu_ready, i)
                nc.vector.tensor_tensor(pre[:], pre_ps[:].rearrange("p a n -> p (a n)"), b1[:], ALU.add
                                        ).then_inc(pre_ready, 1)

            def tile(i, first, last):
                dve.wait_ge(hT_done, i * 2 + 2)
                since(dve, y_done, i)
                nc.vector.tensor_copy(hT[:, 4:8, :].rearrange("p f t -> p (f t)"), hT_ps[:, 1, :]).then_inc(hT_odd_ready, 1)
                if not last:
                    add_bias(i + 1)
                dve.wait_ge(y_done, i + 1)
                since(dve, ys_w, i * 16)
                nc.vector.tensor_tensor(ys[:], y_ps[:, 0, 0:D], rows[:, 0, :], ALU.add).then_inc(ys_ready, 1)
            add_bias(0)
            over_steps(dve, tile, TILES)

            def statistics(q):
                dve.wait_ge(gathered[q], 16 * GB)
                at = q * 3 * GB
                for b in range(q * GB, (q + 1) * GB):
                    nc.vector.tensor_tensor(y[:, b, :], y[:, b, :], x1[:, b, :], ALU.add).then_inc(y_step, 1)
                for n, b in enumerate(range(q * GB, (q + 1) * GB)):
                    dve.wait_ge(y_step, at + n + 1)
                    nc.vector.bn_stats(y_stats[:, b, :], y[:, b, :]).then_inc(y_step, 1)
                for n, b in enumerate(range(q * GB, (q + 1) * GB)):
                    dve.wait_ge(y_step, at + GB + n + 1)
                    nc.vector.bn_aggr(y_mv[:, b, :], y_stats[:, b, :]).then_inc(y_step, 1)

            def update(q):
                at = q * 2 * GB
                dve.wait_ge(y_step, (q + 1) * 3 * GB)
                for b in range(q * GB, (q + 1) * GB):
                    nc.vector.scalar_tensor_tensor(y[:, b, :], y[:, b, :], y_mv[:, b, 0:1], rows[0:S, 1, :],
                                                   ALU.subtract, ALU.mult).then_inc(x_step, 1)
                dve.wait_ge(y_rstd_ready, 2 * q + 2)
                for n, b in enumerate(range(q * GB, (q + 1) * GB)):
                    dve.wait_ge(x_step, at + n + 1)
                    nc.vector.scalar_tensor_tensor(x[:, b, :], y[:, b, :], y_rstd[:, b:b + 1], x[:, b, :],
                                                   ALU.mult, ALU.add).then_inc(x_step, 1)
                for n, b in enumerate(range(q * GB, (q + 1) * GB)):
                    dve.wait_ge(x_step, at + GB + n + 1)
                    nc.vector.bn_stats(stats[:, b, :], x[:, b, :])

            dve.wait_ge(beta_added, B)
            statistics(0)
            for q in range(1, B // GB):
                statistics(q)
                update(q - 1)
            update(B // GB - 1)

        @block.scalar
        def _(act):
            for g in range(B // 2):
                act.wait_ge(xT_done, g + 1)
                if g >= 2:
                    act.wait_ge(router_done, g - 1)
                nc.scalar.activation(x1T[:, g % 2].rearrange("p j c t -> p (j c t)"),
                                     (xT_ps, y_ps)[g % 2][:, 0, 0:2 * KC * S], ACT.Copy).then_inc(xT_ready, 1)

            def tile_input(i):
                since(act, pre_done, i)
                act.wait_ge(xsT_done, i + 1)
                nc.scalar.activation(xsT[:].rearrange("p c t -> p (c t)"), xT_ps[:, 0, 0:KC * 128], ACT.Copy
                                     ).then_inc(xsT_ready, 1)

            def activate(i):
                act.wait_ge(pre_ready, i + 1)
                since(act, hT_done, i * 2)
                nc.scalar.activation(h[:], pre[:], ACT.Gelu).then_inc(gelu_ready, 1)

            def tile(i, first, last):
                act.wait_ge(hT_done, i * 2 + 1)
                since(act, y_done, i)
                nc.scalar.activation(hT[:, 0:4, :].rearrange("p f t -> p (f t)"), hT_ps[:, 0, :], ACT.Copy
                                     ).then_inc(hT_even_ready, 1)
                if not last:
                    tile_input(i + 2)
                    activate(i + 1)

            tile_input(0)
            activate(0)
            tile_input(1)
            over_steps(act, tile, TILES)

        @block.tensor
        def _(pe):
            pe.wait_ge(const_w, 80)
            for g in range(B // 2 + 1):
                if g < B // 2:
                    pe.wait_ge(x1_ready, 2 * g + 2)
                    if g >= 2:
                        pe.wait_ge(xT_ready, g - 1)
                    bank = (xT_ps, y_ps)[g % 2]
                    for j in range(2):
                        for c in range(KC):
                            at = (j * KC + c) * S
                            done = nc.tensor.transpose(bank[:, 0, at:at + S],
                                                       x1[:, 2 * g + j, c * 128:(c + 1) * 128], ident[0:S, 0:S])
                    done.then_inc(xT_done, 1)
                if g >= 1:
                    pe.wait_ge(xT_ready, g)
                    for j in range(2):
                        b = 2 * (g - 1) + j
                        for c in range(KC):
                            done = nc.tensor.matmul(route_ps[0:S, 0, b * E:(b + 1) * E], x1T[:, (g - 1) % 2, j, c, :],
                                                    wr[:, c, :], start=(c == 0), stop=(c == KC - 1))
                    done.then_inc(router_done, 1)
            pe.wait_ge(route_step, 2 * B + 3)
            pe.wait_ge(rstd_step, 4)
            for n, m in enumerate((before, ones)):
                done = nc.tensor.matmul(route_ps[0:S, 0, (n + 1) * 128:(n + 2) * 128], m[:],
                                        one_hot[:].rearrange("p b e -> p (b e)"), start=True, stop=True)
            done.then_inc(rank_done, 1)

            def transpose_tile(i):
                since(pe, xs_w, i * 16 + 16)
                since(pe, xsT_ready, i)
                for c in range(KC):
                    done = nc.tensor.transpose(xT_ps[:, 0, c * 128:(c + 1) * 128], xs[:, c * 128:(c + 1) * 128], ident[:])
                done.then_inc(xsT_done, 1)

            def multiply(i):
                e = pe.value_load(tile_expert_i[0:1, bass.ds(i, 1)], min_val=0, max_val=(E - 1) * F)
                pe.wait_ge(xsT_ready, i + 1)
                since(pe, pre_ready, i)
                for a in range(2):
                    for c in range(KC):
                        done = nc.tensor.matmul(pre_ps[:, a, :], xsT[:, c, :], w1[:, c, bass.ds(e + a * 512, 512)],
                                                start=(c == 0), stop=(c == KC - 1))
                done.then_inc(pre_done, 1)

            def tile(i, first, last):
                pe.wait_ge(gelu_ready, i + 1)
                since(pe, hT_even_ready, i)
                since(pe, hT_odd_ready, i)
                for f in range(FC):
                    done = nc.tensor.transpose(hT_ps[:, f // 4, (f % 4) * 128:(f % 4 + 1) * 128],
                                               h[:, f * 128:(f + 1) * 128], ident[:])
                    if f % 4 == 3:
                        done.then_inc(hT_done, 1)
                if not last:
                    multiply(i + 1)
                    transpose_tile(i + 2)
                pe.wait_ge(hT_even_ready, i + 1)
                pe.wait_ge(hT_odd_ready, i + 1)
                since(pe, ys_ready, i)
                for f in range(FC):
                    done = nc.tensor.matmul(y_ps[:, 0, 0:D], hT[:, f, :], wo[:, f, :],
                                            start=(f == 0), stop=(f == FC - 1))
                done.then_inc(y_done, 1)

            transpose_tile(0)
            pe.wait_ge(slot_ready, 2)
            pe.wait_ge(weight_w, 16 * (KC + 1))
            multiply(0)
            transpose_tile(1)
            over_steps(pe, tile, TILES)


def l1_attention(nc, x, stats, ident, passed, A):
    H, DH = 16, 64
    HP = H // 2
    SCALE = float(DH) ** -0.5
    G = B // 2
    QB = 4
    Q, QT = B // QB, QB * S
    with ExitStack() as ctx:
        ph = Phase(nc, ctx, "l1a")
        wo = ph.sb("wo", [128, HP, D])
        gamma, causal = ph.sb("gamma", [128, 1, KC]), ph.sb("causal", [S, S])
        mv, half = ph.sb("mv", [S, B, 2]), ph.sb("half", [S, B])
        rvar, rstd2, rstd = ph.sb("rvar", [S, B]), ph.sb("rstd2", [S, B]), ph.sb("rstd", [S, B])
        all_qT, qT = ph.sb("all_qT", [128, HP, B * S]), ph.sb("qT", [128, HP, PAIR])
        kT = ph.sb("kT", [128, B, 2, S])
        all_v, v = ph.sb("all_v", [S, B, DH]), ph.sb("v", [S, 2, DH])
        pT, oT = ph.sb("pT", [S, H, S]), ph.sb("oT", [128, 2, HP, S])
        top, shift = ph.sb("top", [S, 2, H]), ph.sb("shift", [S, 2, H])
        total, inv = ph.sb("total", [S, 2, H]), ph.sb("inv", [S, 2, H])
        x_new, x_stats = ph.sb("x_new", [S, D]), ph.sb("x_stats", [S, 6])

        score_ps = ph.banks("score", 4)
        o_ps, y_ps = ph.banks("o", 2), ph.banks("y", 2)

        weight_w, mv_step, rstd_step = ph.sem("weight_w"), ph.sem("mv_step"), ph.sem("rstd_step")
        norm_ready, inT_done, proj_done = ph.sem("norm_ready"), ph.sem("inT_done"), ph.sem("proj_done")
        act_step, dve_step = ph.sem("act_step"), ph.sem("dve_step")
        qv_ready = ph.sem("qv_ready")
        score_done, softmax_step, exp_ready = ph.sem("score_done"), ph.sem("softmax_step"), ph.sem("exp_ready")
        pn_ready, pT_done, pT_ready = ph.sem("pn_ready"), ph.sem("pT_done"), ph.sem("pT_ready")
        o_done, o_ready, y_done, x_step = ph.sem("o_done"), ph.sem("o_ready"), ph.sem("y_done"), ph.sem("x_step")

        WQ_HI = 1

        def in_step(q, k):
            return 2 + k if q == 0 else 8 * q + 1 + k

        def even_step(q, i):
            return 4 + 8 * q + i // 2 + 1

        def kv_step(q):
            return 4 + 8 * q + 8

        WQ_LO = 1

        def lo_step(q):
            return 1 + 5 * q + 1

        def odd_step(q, i):
            return 1 + 5 * q + 1 + i // 2 + 1

        def query_bank(i):
            return (y_ps, o_ps)[i // 2 % 2][:, i % 2, 0:QT]

        with ExitStack() as projections:
            ph_in = Phase(nc, projections, "l1q")
            wv = ph_in.sb("wv", [128, KC, DH])
            wq, wk = ph_in.sb("wq", [128, KC, H * DH]), ph_in.sb("wk", [128, KC, 2 * DH])
            wq_hi, wq_lo = ph_in.sb("wq_hi", [128, KC, H * DH], F32R), ph_in.sb("wq_lo", [128, KC, H * DH], F32R)
            x1, x2 = ph_in.sb("x1", [S, QB, D]), ph_in.sb("x2", [S, QB, D])
            x1T, x2T = ph_in.sb("x1T", [128, 2, KC, QT]), ph_in.sb("x2T", [128, KC, QT])
            x2T_hi, x2T_lo = ph_in.sb("x2T_hi", [128, 2, KC, QT], F32R), ph_in.sb("x2T_lo", [128, 2, KC, QT], F32R)
            block = projections.enter_context(nc.Block())

            @block.sync
            def _(sp):
                sp.dma_start(gamma[:], A["l1a_gamma"]).then_inc(weight_w, 16)
                sp.dma_start(causal[:], A["causal"]).then_inc(weight_w, 16)
                sp.dma_start(wq[:], A["l1a_wq"].rearrange("(c p) n -> p c n", p=128)).then_inc(weight_w, 16)
                sp.dma_start(wk[:], A["l1a_wk"].rearrange("(c p) n -> p c n", p=128)).then_inc(weight_w, 16)
                sp.dma_start(wv[:], A["l1a_wv"].rearrange("(c p) n -> p c n", p=128)).then_inc(weight_w, 16)
                sp.dma_start(wo[:], A["l1a_wo"].rearrange("(c p) n -> p c n", p=128)).then_inc(weight_w, 16)

            @block.gpsimd
            def _(pool):
                nc.gpsimd.memset(half[:], -0.5).then_inc(rstd_step, 1)
                double_rstd(nc, pool, mv, half, rvar, rstd2, mv_step, rstd_step, 1)
                nc.gpsimd.tensor_scalar(rstd[:], mv[:, :, 1], LN_EPS, None, ALU.add).then_inc(rstd_step, 1)
                pool.wait_ge(rstd_step, 5)
                nc.gpsimd.tensor_tensor(rstd[:], rstd[:], half[:], ALU.pow).then_inc(rstd_step, 1)
                nc.gpsimd.memset(kT[:], 0.0).then_inc(rstd_step, 1)

            @block.vector
            def _(dve):
                def norm(q):
                    if q >= 1:
                        dve.wait_ge(inT_done, q * 2)
                    for j in range(QB):
                        b = q * QB + j
                        nc.vector.tensor_scalar(x2[:, j], x[:, b, :], mv[:, b, 0:1], rstd2[:, b:b + 1],
                                                ALU.subtract, ALU.mult).then_inc(norm_ready, 1)
                    if q == 0:
                        dve.wait_ge(rstd_step, 6)
                    for j in range(QB):
                        b = q * QB + j
                        nc.vector.tensor_scalar(x1[:, j], x[:, b, :], mv[:, b, 0:1], rstd[:, b:b + 1],
                                                ALU.subtract, ALU.mult).then_inc(norm_ready, 1)

                aggregate(nc, dve, stats, mv, mv_step)
                dve.wait_ge(rstd_step, 4)
                norm(0)
                dve.wait_ge(act_step, WQ_HI)
                nc.vector.tensor_tensor(wq_lo[:], wq[:], wq_hi[:].bitcast(F32), ALU.subtract).then_inc(dve_step, 1)
                for q in range(Q):
                    dve.wait_ge(act_step, in_step(q, 1))
                    if q >= 2:
                        dve.wait_ge(proj_done, 9 * (q - 2) + 8)
                    nc.vector.tensor_tensor(x2T_lo[:, q % 2], x2T[:], x2T_hi[:, q % 2].bitcast(F32), ALU.subtract
                                            ).then_inc(dve_step, 1)
                    if q + 1 < Q:
                        norm(q + 1)
                    for i in range(1, HP, 2):
                        dve.wait_ge(proj_done, 9 * q + i + 1)
                        nc.vector.tensor_copy(all_qT[:, i, q * QT:(q + 1) * QT], query_bank(i)).then_inc(dve_step, 1)

            @block.scalar
            def _(act):
                def take_inputs(q):
                    act.wait_ge(inT_done, q * 2 + 1)
                    if q >= 1:
                        act.wait_ge(dve_step, lo_step(q - 1))
                    for c in range(KC):
                        done = nc.scalar.activation(x2T[:, c, :], score_ps[:, c, 0:QT], ACT.Copy, scale=gamma[:, 0, c:c + 1])
                    done.then_inc(act_step, 1)
                    act.wait_ge(act_step, in_step(q, 0))
                    if q >= 2:
                        act.wait_ge(proj_done, 9 * (q - 2) + 8)
                    nc.scalar.activation(x2T_hi[:, q % 2], x2T[:], ACT.Copy).then_inc(act_step, 1)
                    act.wait_ge(inT_done, q * 2 + 2)
                    if q >= 2:
                        act.wait_ge(proj_done, 9 * (q - 2) + 9)
                    nc.scalar.activation(x1T[:, q % 2], score_ps[:, 2:4, 0:QT], ACT.Copy).then_inc(act_step, 1)

                act.wait_ge(weight_w, 96)
                nc.scalar.activation(wq_hi[:], wq[:], ACT.Copy).then_inc(act_step, 1)
                take_inputs(0)
                act.wait_ge(rstd_step, 7)
                for q in range(Q):
                    for i in range(0, HP, 2):
                        act.wait_ge(proj_done, 9 * q + i + 1)
                        nc.scalar.activation(all_qT[:, i, q * QT:(q + 1) * QT], query_bank(i), ACT.Copy
                                             ).then_inc(act_step, 1)
                    if q + 1 < Q:
                        take_inputs(q + 1)
                    act.wait_ge(proj_done, 9 * q + 9)
                    for a in range(2):
                        part = slice(a * DH, (a + 1) * DH)
                        nc.scalar.activation(kT[part, q * QB:(q + 1) * QB, a, :],
                                             o_ps[part, 0, 0:QT].rearrange("p (j t) -> p j t", j=QB), ACT.Copy)
                    nc.scalar.activation(all_v[:, q * QB:(q + 1) * QB, :].rearrange("p j d -> p (j d)"),
                                         o_ps[0:S, 1, 0:QB * DH], ACT.Copy).then_inc(act_step, 1)

            @block.tensor
            def _(pe):
                def transpose_inputs(q, n):
                    pe.wait_ge(norm_ready, q * 2 * QB + (n + 1) * QB)
                    if q >= 1:
                        pe.wait_ge(act_step, in_step(q - 1, 0 if n == 0 else 2))
                    for c in range(KC):
                        for j in range(QB):
                            done = nc.tensor.transpose(score_ps[:, 2 * n + c, j * S:(j + 1) * S],
                                                       (x2, x1)[n][:, j, c * 128:(c + 1) * 128], ident[0:S, 0:S])
                    done.then_inc(inT_done, 1)

                transpose_inputs(0, 0)
                transpose_inputs(0, 1)
                pe.wait_ge(weight_w, 96)
                pe.wait_ge(dve_step, WQ_LO)
                for q in range(Q):
                    pe.wait_ge(dve_step, lo_step(q))
                    for i in range(HP):
                        if i >= 4:
                            pe.wait_ge(*((act_step, even_step(q, i - 4)) if i % 2 == 0 else (dve_step, odd_step(q, i - 4))))
                        elif q >= 1 and i < 2:
                            pe.wait_ge(*((act_step, even_step(q - 1, 4)) if i == 0 else (dve_step, odd_step(q - 1, 5))))
                        elif q >= 1:
                            pe.wait_ge(act_step, kv_step(q - 1))
                        heads = slice(i * 128, (i + 1) * 128)
                        for c in range(KC):
                            hi, lo = x2T_hi[:, q % 2, c, :], x2T_lo[:, q % 2, c, :]
                            nc.tensor.matmul(query_bank(i), wq_hi[:, c, heads], hi, start=(c == 0), stop=False)
                            nc.tensor.matmul(query_bank(i), wq_hi[:, c, heads], lo, start=False, stop=False)
                            done = nc.tensor.matmul(query_bank(i), wq_lo[:, c, heads], hi, start=False, stop=(c == KC - 1))
                        done.then_inc(proj_done, 1)
                        if i == 5 and q + 1 < Q:
                            transpose_inputs(q + 1, 0)
                    if q + 1 < Q:
                        transpose_inputs(q + 1, 1)
                    pe.wait_ge(act_step, even_step(q, 6))
                    pe.wait_ge(dve_step, odd_step(q, 7))
                    pe.wait_ge(act_step, in_step(q, 2))
                    for c in range(KC):
                        nc.tensor.matmul(o_ps[:, 0, 0:QT], wk[:, c, :], x1T[:, q % 2, c, :],
                                         start=(c == 0), stop=(c == KC - 1))
                    for j in range(QB):
                        for c in range(KC):
                            done = nc.tensor.matmul(o_ps[0:S, 1, j * DH:(j + 1) * DH],
                                                    x1T[:, q % 2, c, j * S:(j + 1) * S], wv[:, c, :],
                                                    start=(c == 0), stop=(c == KC - 1))
                    done.then_inc(proj_done, 1)

        p, pn = ph.sb("p", [S, 2, H, S]), ph.sb("pn", [S, 2, H, S])
        with nc.Block() as block:
            @block.gpsimd
            def _(pool):
                def body(g, first, last):
                    for j in range(2):
                        b = g * 2 + j
                        pool.wait_ge(softmax_step, b * 4 + 4)
                        since(pool, pT_done, b * 2 - 2)
                        nc.gpsimd.tensor_tensor(pn[:, j], p[:, j], inv[:, j, :, None].broadcast_to([S, H, S]),
                                                ALU.mult).then_inc(pn_ready, 1)
                over_steps(pool, body, G)

            @block.vector
            def _(dve):
                def softmax(g, j):
                    b = g * 2 + j
                    dve.wait_ge(score_done, b + 1)
                    since(dve, pn_ready, b - 1)
                    nc.vector.tensor_tensor(
                        p[:, j].rearrange("p (a h) s -> p a h s", a=4),
                        score_ps[0:S, :, 0:4 * S].rearrange("p a (h s) -> p a h s", h=4),
                        causal[:, None, None, :].broadcast_to([S, 4, 4, S]), ALU.add).then_inc(softmax_step, 1)
                    dve.wait_ge(softmax_step, b * 4 + 1)
                    nc.vector.tensor_reduce(top[:, j], p[:, j], AX.X, ALU.max).then_inc(softmax_step, 1)
                    dve.wait_ge(softmax_step, b * 4 + 2)
                    nc.vector.tensor_scalar(shift[:, j], top[:, j], -SCALE, None, ALU.mult).then_inc(softmax_step, 1)

                def invert_sums(g, j):
                    b = g * 2 + j
                    dve.wait_ge(exp_ready, b + 1)
                    since(dve, pn_ready, b - 1)
                    nc.vector.reciprocal(inv[:, j], total[:, j]).then_inc(softmax_step, 1)

                def copy_pT(g, j):
                    b = g * 2 + j
                    for k in range(2):
                        dve.wait_ge(pT_done, b * 2 + k + 1)
                        if k == 0:
                            since(dve, o_done, b)
                        nc.vector.tensor_copy(pT[:, 8 * k:8 * k + 8, :].rearrange("p (a h) s -> p a (h s)", a=2),
                                              score_ps[0:S, 2 * k:2 * k + 2, 0:4 * S]).then_inc(pT_ready, 1)

                def update(g, j):
                    b = g * 2 + j
                    dve.wait_ge(y_done, b + 1)
                    update_x(nc, dve, x, stats, x_new, x_stats, y_ps[0:S, j, 0:D], b, x_step)

                softmax(0, 0)
                invert_sums(0, 0)

                def body(g, first, last):
                    softmax(g, 1)
                    copy_pT(g, 0)
                    if not first:
                        update(g - 1, 1)
                    invert_sums(g, 1)
                    if not last:
                        softmax(g + 1, 0)
                    copy_pT(g, 1)
                    update(g, 0)
                    if not last:
                        invert_sums(g + 1, 0)
                over_steps(dve, body, G)
                update(G - 1, 1)

            @block.scalar
            def _(act):
                def exp(g, j):
                    act.wait_ge(softmax_step, (g * 2 + j) * 4 + 3)
                    for h in range(H):
                        done = nc.scalar.activation(p[:, j, h, :], p[:, j, h, :], ACT.Exp, scale=SCALE,
                                                    bias=shift[:, j, h:h + 1], accum_out=total[:, j, h:h + 1])
                    done.then_inc(exp_ready, 1)

                def take_queries(g):
                    since(act, score_done, g * 2)
                    nc.scalar.activation(qT[:], all_qT[:, :, bass.ds(g * PAIR, PAIR)], ACT.Copy).then_inc(qv_ready, 1)

                def take_values(g):
                    since(act, o_done, g * 2)
                    nc.scalar.activation(v[:], all_v[:, bass.ds(g * 2, 2), :], ACT.Copy).then_inc(qv_ready, 1)

                def copy_o(g, j):
                    b = g * 2 + j
                    act.wait_ge(o_done, b + 1)
                    since(act, y_done, b - 1)
                    nc.scalar.activation(oT[:, j].rearrange("p (a h) s -> p a (h s)", a=2), o_ps[:, :, 0:4 * S],
                                         ACT.Copy).then_inc(o_ready, 1)

                take_queries(0)
                exp(0, 0)

                def body(g, first, last):
                    take_values(g)
                    if not last:
                        take_queries(g + 1)
                    exp(g, 1)
                    copy_o(g, 0)
                    if not last:
                        exp(g + 1, 0)
                    copy_o(g, 1)
                over_steps(act, body, G)

            @block.tensor
            def _(pe):
                def score(g, j):
                    b = g * 2 + j
                    pe.wait_ge(qv_ready, g * 2 + 1)
                    since(pe, softmax_step, b * 4 - 3)
                    since(pe, pT_ready, b * 2 - 2)
                    for n in range(HP):
                        done = nc.tensor.matmul(score_ps[0:S, n // 2, (n % 2) * PAIR:(n % 2 + 1) * PAIR],
                                                qT[:, n, j * S:(j + 1) * S],
                                                kT[:, bass.ds(b, 1)].rearrange("p b a s -> p (b a s)"), start=True, stop=True)
                    done.then_inc(score_done, 1)

                def transpose_p(g, j, last):
                    b = g * 2 + j
                    if not (last and j == 1):
                        pe.wait_ge(softmax_step, b * 4 + 5)
                    since(pe, pT_ready, b * 2)
                    pe.wait_ge(pn_ready, b + 1)
                    for n in range(H):
                        done = nc.tensor.transpose(score_ps[0:S, n // 4, (n % 4) * S:(n % 4 + 1) * S], pn[:, j, n, :],
                                                   ident[0:S, 0:S])
                        if n % 8 == 7:
                            done.then_inc(pT_done, 1)

                def weigh_values(g, j):
                    b = g * 2 + j
                    if j == 0:
                        pe.wait_ge(qv_ready, g * 2 + 2)
                    since(pe, o_ready, b)
                    for k in range(2):
                        pe.wait_ge(pT_ready, b * 2 + k + 1)
                        for a in range(2):
                            heads = pT[:, 8 * k:8 * k + 8, :].rearrange("p (h a) s -> p a h s", a=2)
                            done = nc.tensor.matmul(o_ps[a * DH:(a + 1) * DH, k, 0:4 * S], v[:, j, :], heads[:, a],
                                                    start=True, stop=True)
                    done.then_inc(o_done, 1)

                def project_out(g, j):
                    b = g * 2 + j
                    pe.wait_ge(o_ready, b + 1)
                    since(pe, x_step, b * 4 - (7 if j == 0 else 3))
                    for c in range(HP):
                        done = nc.tensor.matmul(y_ps[0:S, j, 0:D], oT[:, j, c, :], wo[:, c, :],
                                                start=(c == 0), stop=(c == HP - 1))
                    done.then_inc(y_done, 1)

                def body(g, first, last):
                    if not first:
                        project_out(g - 1, 1)
                    transpose_p(g, 0, last)
                    weigh_values(g, 0)
                    if not last:
                        score(g + 1, 0)
                    project_out(g, 0)
                    transpose_p(g, 1, last)
                    weigh_values(g, 1)
                    if not last:
                        score(g + 1, 1)

                score(0, 0)
                score(0, 1)
                over_steps(pe, body, G)
                project_out(G - 1, 1)


def l1_context_mix(nc, x, stats, ident, passed, A):
    HD = 16
    CT, NC = N // 3, 3
    with ExitStack() as ctx:
        ph = Phase(nc, ctx, "l1x")
        wq, wkv, wo = ph.sb("wq", [128, KC, D]), ph.sb("wkv", [128, KC, 2 * D]), ph.sb("wo", [128, KC, D])
        q_bias = ph.sb("q_bias", [128, 1, KC])
        kv_bias, rows = ph.sb("kv_bias", [CT, 2 * D]), ph.sb("rows", [S, 3, D])
        heads = ph.sb("heads", [128, 128])
        mv, half, rstd = ph.sb("mv", [S, B, 2]), ph.sb("half", [S, B]), ph.sb("rstd", [S, B])
        ctxT, ctxT_next = ph.sb("ctxT", [128, KC, N]), ph.sb("ctxT_next", [128, KC, N])
        masked = ph.sb("masked", [S, MASK_WORDS], U32)
        flag = ph.sb("flag", [S, 1])
        kv, kTv = ph.sb("kv", [CT, NC, 2 * D]), ph.sb("kTv", [128, KC, 128])
        x1, x1T = ph.sb("x1", [S, D]), ph.sb("x1T", [128, KC, S])
        y_in = ph.sb("y_in", [S, D])
        qT, cT = ph.sb("qT", [128, KC, S]), ph.sb("cT", [128, KC, S])
        y, y_stats, y_mv, y_rstd = ph.sb("y", [S, D]), ph.sb("y_stats", [S, 6]), ph.sb("y_mv", [S, 2]), ph.sb("y_rstd", [S, 1])
        y_var = ph.sb("y_var", [S, 1])
        z = ph.sb("z", [S, D])
        x_new, x_stats = ph.sb("x_new", [S, D]), ph.sb("x_stats", [S, 6])

        kv_ps, kTv_ps, xT_ps = ph.banks("kv", 3), ph.banks("kTv", 1), ph.banks("xT", 1)
        qT_ps, cT_ps, o_ps = ph.banks("qT", 1), ph.banks("cT", 1), ph.banks("o", 1)

        weight_w, ctx_w, mask_w = ph.sem("weight_w"), ph.sem("ctx_w"), ph.sem("mask_w")
        mv_step, rstd_step = ph.sem("mv_step"), ph.sem("rstd_step")
        x1_ready, xT_done, xT_ready = ph.sem("x1_ready"), ph.sem("xT_done"), ph.sem("xT_ready")
        kv_done, kv_ready, kTv_done, kTv_ready = ph.sem("kv_done"), ph.sem("kv_ready"), ph.sem("kTv_done"), ph.sem("kTv_ready")
        q_done, q_ready, c_done, c_ready = ph.sem("q_done"), ph.sem("q_ready"), ph.sem("c_done"), ph.sem("c_ready")
        o_done, flag_step, y_step = ph.sem("o_done"), ph.sem("flag_step"), ph.sem("y_step")
        z_step, x_step, ctx_ready = ph.sem("z_step"), ph.sem("x_step"), ph.sem("ctx_ready")
        y_in_ready = ph.sem("y_in_ready")

        block = ctx.enter_context(nc.Block())

        @block.sync
        def _(sp):
            def load_context(b):
                sp.dma_start(ctxT_next[:], A["ctxT"][bass.ds(b, 1)].rearrange("b (c p) n -> p (b c) n", p=128)
                             ).then_inc(ctx_w, 16)

            load_context(0)
            sp.dma_start(wkv[:], A["l1x_wkv"].rearrange("(c p) n -> p c n", p=128)).then_inc(weight_w, 16)
            sp.wait_ge(weight_w, 16)
            sp.dma_start(wq[:], A["l1x_wq"].rearrange("(c p) n -> p c n", p=128)).then_inc(weight_w, 16)
            sp.dma_start(wo[:], A["l1x_wo"].rearrange("(c p) n -> p c n", p=128)).then_inc(weight_w, 16)
            sp.dma_start(q_bias[:], A["l1x_q_bias"]).then_inc(weight_w, 16)
            sp.dma_start(kv_bias[:], A["l1x_kv_bias"].broadcast_to([CT, 2 * D])).then_inc(weight_w, 16)
            sp.dma_start(rows[:], A["l1x_rows"].broadcast_to([S, 3, D])).then_inc(weight_w, 16)
            sp.dma_start(heads[:], A["heads"]).then_inc(weight_w, 16)
            with sp.Fori(1, B) as b:
                sp.wait_ge(ctx_ready, b)
                load_context(b)

        @block.gpsimd
        def _(pool):
            pool.dma_start(masked[:], A["score_mask"][0]).then_inc(mask_w, 16)
            single_rstd(nc, pool, mv, half, rstd, mv_step, rstd_step)

            def body(b, first, last):
                since(pool, x1_ready, b + 1)
                since(pool, y_step, b * 4 - 3)
                nc.gpsimd.tensor_tensor(y_in[:], x1[:], rows[:, 0, :], ALU.add).then_inc(y_in_ready, 1)
                wait_apart(pool, y_step, b * 4 + 3, passed)
                nc.gpsimd.tensor_scalar(y_var[:], y_mv[:, 1:2], LN_EPS, None, ALU.add).then_inc(z_step, 1)
                pool.wait_ge(z_step, b * 4 + 1)
                nc.gpsimd.tensor_tensor(y_rstd[:], y_var[:], half[:, 0:1], ALU.pow).then_inc(z_step, 1)
                pool.wait_ge(y_step, b * 4 + 4)
                since(pool, x_step, b * 4 - 3)
                nc.gpsimd.tensor_tensor(z[:], y[:], rows[:, 1, :], ALU.mult).then_inc(z_step, 1)
                pool.wait_ge(z_step, b * 4 + 3)
                nc.gpsimd.tensor_tensor(z[:], z[:], rows[:, 2, :], ALU.add).then_inc(z_step, 1)
                if not last:
                    since(pool, flag_step, b * 4 + 1)
                    pool.dma_start(masked[:], A["score_mask"][bass.ds(b + 1, 1)].rearrange("b s n -> s (b n)")
                                   ).then_inc(mask_w, 16)
            pool.wait_ge(weight_w, 112)
            over_steps(pool, body, B)

        @block.vector
        def _(dve):
            def add_kv_bias(b):
                for t in range(NC):
                    since(dve, kv_done, b * NC + t + 1)
                    if t == 0:
                        since(dve, kTv_done, b)
                    nc.vector.tensor_tensor(kv[:, t, :], kv_ps[0:CT, t, :], kv_bias[:], ALU.add).then_inc(kv_ready, 1)

            def block_diagonal(b):
                since(dve, kTv_done, b + 1)
                since(dve, c_done, b)
                nc.vector.tensor_tensor(kTv[:], kTv_ps[:, 0, 0:KC * 128].rearrange("p (c n) -> p c n", c=KC),
                                        heads[:, None, :].broadcast_to([128, KC, 128]), ALU.mult).then_inc(kTv_ready, 1)

            def norm(b):
                since(dve, xT_done, b)
                since(dve, y_in_ready, b)
                nc.vector.tensor_scalar(x1[:], x[:, b, :], mv[:, b, 0:1], rstd[:, bass.ds(b, 1)],
                                        ALU.subtract, ALU.mult).then_inc(x1_ready, 1)

            def mask_flag(b):
                since(dve, mask_w, b * 16 + 16)
                nc.vector.tensor_reduce(flag[:], masked[:].bitcast(U8)[:, 0:N], AX.X, ALU.max).then_inc(flag_step, 1)
                dve.wait_ge(flag_step, b * 4 + 1)
                nc.vector.tensor_scalar(flag[:], flag[:], -1.0, 1.0, ALU.mult, ALU.add).then_inc(flag_step, 1)
                dve.wait_ge(flag_step, b * 4 + 2)
                nc.vector.reciprocal(flag[:], flag[:]).then_inc(flag_step, 1)
                dve.wait_ge(flag_step, b * 4 + 3)
                nc.vector.tensor_scalar(flag[:], flag[:], 0.0, None, ALU.mult).then_inc(flag_step, 1)

            def add_output(b):
                dve.wait_ge(o_done, b + 1)
                dve.wait_ge(flag_step, b * 4 + 4)
                dve.wait_ge(y_in_ready, b + 1)
                since(dve, z_step, b * 4 - 1)
                nc.vector.scalar_tensor_tensor(y[:], o_ps[0:S, 0, 0:D], flag[:, 0:1], y_in[:], ALU.add, ALU.add
                                               ).then_inc(y_step, 1)
                dve.wait_ge(y_step, b * 4 + 1)
                nc.vector.bn_stats(y_stats[:], y[:]).then_inc(y_step, 1)
                wait_apart(dve, y_step, b * 4 + 2, passed)
                nc.vector.bn_aggr(y_mv[:], y_stats[:]).then_inc(y_step, 1)

            def normalise(b):
                dve.wait_ge(z_step, b * 4 + 2)
                nc.vector.tensor_scalar(y[:], y[:], y_mv[:, 0:1], y_rstd[:, 0:1], ALU.subtract, ALU.mult
                                        ).then_inc(y_step, 1)

            def update(b):
                dve.wait_ge(z_step, b * 4 + 4)
                update_x(nc, dve, x, stats, x_new, x_stats, z[:], b, x_step)

            aggregate(nc, dve, stats, mv, mv_step)
            dve.wait_ge(rstd_step, 3)
            norm(0)
            dve.wait_ge(weight_w, 112)
            add_kv_bias(0)
            block_diagonal(0)

            def body(b, first, last):
                if not first:
                    update(b - 1)
                if not last:
                    norm(b + 1)
                    add_kv_bias(b + 1)
                mask_flag(b)
                add_output(b)
                if not last:
                    block_diagonal(b + 1)
                normalise(b)
            over_steps(dve, body, B)
            update(B - 1)

        @block.scalar
        def _(act):
            def take_context(b):
                since(act, ctx_w, b * 16 + 16)
                since(act, kv_done, b * NC)
                nc.scalar.activation(ctxT[:], ctxT_next[:], ACT.Copy).then_inc(ctx_ready, 1)

            take_context(0)
            act.wait_ge(weight_w, 112)

            def body(b, first, last):
                act.wait_ge(xT_done, b + 1)
                nc.scalar.activation(x1T[:].rearrange("p c t -> p (c t)"), xT_ps[:, 0, 0:KC * S], ACT.Copy
                                     ).then_inc(xT_ready, 1)
                if not last:
                    take_context(b + 1)
                act.wait_ge(q_done, b + 1)
                for c in range(KC):
                    done = nc.scalar.activation(qT[:, c, :], qT_ps[:, 0, c * S:(c + 1) * S], ACT.Identity,
                                                bias=q_bias[:, 0, c:c + 1])
                done.then_inc(q_ready, 1)
                act.wait_ge(c_done, b + 1)
                nc.scalar.activation(cT[:].rearrange("p c t -> p (c t)"), cT_ps[:, 0, 0:KC * S], ACT.Copy
                                     ).then_inc(c_ready, 1)
            over_steps(act, body, B)

        @block.tensor
        def _(pe):
            def project_kv(b, t):
                if t == 0:
                    since(pe, ctx_ready, b + 1)
                since(pe, kv_ready, b * NC - NC + t + 1)
                for c in range(KC):
                    done = nc.tensor.matmul(kv_ps[0:CT, t, :], ctxT[:, c, t * CT:(t + 1) * CT], wkv[:, c, :],
                                            start=(c == 0), stop=(c == KC - 1))
                done.then_inc(kv_done, 1)

            def multiply_kTv(b):
                since(pe, kTv_ready, b)
                for c in range(KC):
                    for t in range(NC):
                        since(pe, kv_ready, b * NC + t + 1)
                        done = nc.tensor.matmul(kTv_ps[:, 0, c * 128:(c + 1) * 128], kv[:, t, c * 128:(c + 1) * 128],
                                                kv[:, t, D + c * 128:D + (c + 1) * 128],
                                                start=(t == 0), stop=(t == NC - 1))
                done.then_inc(kTv_done, 1)

            pe.wait_ge(weight_w, 16)
            for t in range(NC):
                project_kv(0, t)
            pe.wait_ge(weight_w, 112)
            multiply_kTv(0)

            def body(b, first, last):
                since(pe, x1_ready, b + 1)
                since(pe, xT_ready, b)
                for c in range(KC):
                    done = nc.tensor.transpose(xT_ps[:, 0, c * S:(c + 1) * S], x1[:, c * 128:(c + 1) * 128],
                                               ident[0:S, 0:S])
                done.then_inc(xT_done, 1)
                pe.wait_ge(xT_ready, b + 1)
                since(pe, q_ready, b)
                for u in range(KC):
                    for c in range(KC):
                        done = nc.tensor.matmul(qT_ps[:, 0, u * S:(u + 1) * S], wq[:, c, u * 128:(u + 1) * 128],
                                                x1T[:, c, :], start=(c == 0), stop=(c == KC - 1))
                done.then_inc(q_done, 1)
                if not last:
                    project_kv(b + 1, 0)
                pe.wait_ge(q_ready, b + 1)
                pe.wait_ge(kTv_ready, b + 1)
                since(pe, c_ready, b)
                for u in range(KC):
                    done = nc.tensor.matmul(cT_ps[:, 0, u * S:(u + 1) * S], kTv[:, u, :], qT[:, u, :],
                                            start=True, stop=True)
                done.then_inc(c_done, 1)
                if not last:
                    project_kv(b + 1, 1)
                    project_kv(b + 1, 2)
                pe.wait_ge(c_ready, b + 1)
                since(pe, y_step, b * 4 - 3)
                for u in range(KC):
                    done = nc.tensor.matmul(o_ps[0:S, 0, 0:D], cT[:, u, :], wo[:, u, :],
                                            start=(u == 0), stop=(u == KC - 1))
                done.then_inc(o_done, 1)
                if not last:
                    multiply_kTv(b + 1)
            over_steps(pe, body, B)


def l1_experts(nc, x, stats, ident, passed, A, out):
    E, R, F = 4, 4, 1024
    ER, FC = LOW_ROWS, F // 128
    B_LO, LOW_LO = slice(32, 32 + E * R), slice(64, 64 + E * R)
    GB = 4
    G, GT = B // GB, GB * S
    with ExitStack() as ctx:
        ph = Phase(nc, ctx, "l1f")
        wi, wo = ph.sb("wi", [128, KC, F]), ph.sb("wo", [128, FC, D])
        wg, low_a, low_b = ph.sb("wg", [128, KC, E]), ph.sb("low_a", [128, KC, ER]), ph.sb("low_b", [ER, F])
        bg, row_expert = ph.sb("bg", [S, E]), ph.sb("row_expert", [S, ER])
        low_b_r = ph.sb("low_b_r", [ER, F], F32R)
        mv, half, rstd = ph.sb("mv", [S, B, 2]), ph.sb("half", [S, B]), ph.sb("rstd", [S, B])
        x1, x1T = ph.sb("x1", [S, B, D]), ph.sb("x1T", [128, KC, B * S])
        logits, best, best_no = ph.sb("logits", [S, B, 8]), ph.sb("best", [S, B, 8]), ph.sb("best_no", [S, B, 8], U32)
        share, total = ph.sb("share", [S, B, 8]), ph.sb("total", [S, B])
        weight, ratio = ph.sb("weight", [S, B]), ph.sb("ratio", [S, B])
        chosen = ph.sb("chosen", [S, 2, B])
        one_hot = ph.sb("one_hot", [S, 2, B, ER])
        low = ph.sb("low", [ER, B * S])
        low_masked = ph.sb("low_masked", [ER, 2, GT])
        low_first, low_change = ph.sb("low_first", [ER, B * S], F32R), ph.sb("low_change", [ER, B * S], F32R)
        ratio_rows = ph.sb("ratio_rows", [128, B * S])
        z_first, z_second = ph.sb("z_first", [128, 4, GT]), ph.sb("z_second", [128, 2, GT])
        h = ph.sb("h", [128, FC, GT])

        result = ph.sb("result", [S, GB, D])

        z_ps, change_ps, y_ps = ph.banks("z", 2), ph.banks("change", 2), ph.banks("y", 2)
        gate_ps, ratio_ps = ph.banks("gate", 1), ph.banks("ratio", 1)

        weight_w, const_w, stored = ph.sem("weight_w"), ph.sem("const_w"), ph.sem("stored")
        mv_step, rstd_step = ph.sem("mv_step"), ph.sem("rstd_step")
        x1_ready, xT_done, xT_ready = ph.sem("x1_ready"), ph.sem("xT_done"), ph.sem("xT_ready")
        gate_done, low_ready, gate_step, exp_ready = ph.sem("gate_done"), ph.sem("low_ready"), ph.sem("gate_step"), ph.sem("exp_ready")
        one_hot_done = ph.sem("one_hot_done")
        ratio_done, ratio_ready, masked_ready = ph.sem("ratio_done"), ph.sem("ratio_ready"), ph.sem("masked_ready")
        first_done, first_ready, change_done = ph.sem("first_done"), ph.sem("first_ready"), ph.sem("change_done")
        low_hi_ready, low_lo_ready = ph.sem("low_hi_ready"), ph.sem("low_lo_ready")
        b_step = ph.sem("b_step")
        h_step, y_done, x_step = ph.sem("h_step"), ph.sem("y_done"), ph.sem("x_step")

        GROUP_STEPS = 1 + 2 * GB

        def gate_bank(g):
            return (gate_ps, ratio_ps)[g % 2][0:S, 0, 0:GB * E].rearrange("p (b e) -> p b e", e=E)

        block = ctx.enter_context(nc.Block())

        @block.sync
        def _(sp):
            sp.dma_start(wg[:], A["l1f_wg"].rearrange("(c p) n -> p c n", p=128)).then_inc(const_w, 16)
            sp.dma_start(low_a[:], A["l1f_a"].rearrange("(c p) n -> p c n", p=128)).then_inc(const_w, 16)
            sp.dma_start(low_b[:], A["l1f_b"]).then_inc(const_w, 16)
            sp.dma_start(bg[:], A["l1f_bg"].broadcast_to([S, E])).then_inc(const_w, 16)
            sp.dma_start(row_expert[:], A["row_expert"].broadcast_to([S, ER])).then_inc(const_w, 16)
            sp.dma_start(wi[:], A["l1f_wi"].rearrange("(c p) n -> p c n", p=128)).then_inc(weight_w, 16)
            sp.dma_start(wo[:], A["l1f_wo"].rearrange("(c p) n -> p c n", p=128)).then_inc(weight_w, 16)
            with sp.Fori(0, G) as g:
                sp.wait_ge(x_step, g * GB + GB)
                sp.dma_start(out[bass.ds(g * GB, GB)].rearrange("b s d -> s b d"), result[:]).then_inc(stored, 16)
            sp.wait_ge(stored, 16 * G)

        @block.gpsimd
        def _(pool):
            single_rstd(nc, pool, mv, half, rstd, mv_step, rstd_step)

        @block.vector
        def _(dve):
            steps = [0]

            def step(instruction):
                steps[0] += 1
                instruction.then_inc(gate_step, 1)
                dve.wait_ge(gate_step, steps[0])

            aggregate(nc, dve, stats, mv, mv_step)
            dve.wait_ge(rstd_step, 3)
            for b in range(B):
                nc.vector.tensor_scalar(x1[:, b, :], x[:, b, :], mv[:, b, 0:1], rstd[:, b:b + 1],
                                        ALU.subtract, ALU.mult).then_inc(x1_ready, 1)
            dve.wait_ge(b_step, 1)
            nc.vector.tensor_tensor(low_b_r[B_LO, :], low_b[B_LO, :], low_b_r[B_LO, :].bitcast(F32), ALU.subtract
                                    ).then_inc(b_step, 1)
            nc.vector.memset(logits[:, :, E:8], NEG)
            dve.wait_ge(const_w, 80)
            for g in range(G):
                dve.wait_ge(gate_done, g + 1)
                group = slice(g * GB, (g + 1) * GB)
                step(nc.vector.tensor_tensor(logits[:, group, 0:E], gate_bank(g), bg[:, None, :].broadcast_to([S, GB, E]),
                                             ALU.add))
                for b in range(g * GB, (g + 1) * GB):
                    nc.vector.max(best[:, b, :], logits[:, b, :]).then_inc(gate_step, 1)
                for j in range(GB):
                    b = g * GB + j
                    dve.wait_ge(gate_step, steps[0] + j + 1)
                    nc.vector.max_index(best_no[:, b, :], best[:, b, :], logits[:, b, :]).then_inc(gate_step, 1)
                steps[0] += 2 * GB
            dve.wait_ge(gate_step, steps[0])
            step(nc.vector.tensor_tensor(share[:], best[:], best[:, :, 0:1].broadcast_to([S, B, 8]), ALU.subtract))
            step(nc.vector.tensor_copy(chosen[:].rearrange("p k b -> p b k"), best_no[:, :, 0:2]))
            step(nc.vector.tensor_tensor(
                one_hot[:].rearrange("p k b e -> p (k b) e"), row_expert[:, None, :].broadcast_to([S, 2 * B, ER]),
                chosen[:].rearrange("p k b -> p (k b)")[:, :, None].broadcast_to([S, 2 * B, ER]), ALU.is_equal))
            step(nc.vector.tensor_tensor(one_hot[:, 1], one_hot[:, 1], one_hot[:, 0], ALU.subtract))
            dve.wait_ge(exp_ready, 1)
            nc.vector.tensor_copy(ratio[:], share[:, :, 1]).then_inc(ratio_ready, 1)
            step(nc.vector.tensor_reduce(total[:], share[:], AX.X, ALU.add))
            step(nc.vector.reciprocal(weight[:], total[:]))
            for g in range(G):
                dve.wait_ge(one_hot_done, g + 1)
                dve.wait_ge(low_ready, g + 1)
                group = slice(g * GT, (g + 1) * GT)
                if g >= 1:
                    dve.wait_ge(low_lo_ready, 2 * g)
                for k in range(2):
                    nc.vector.tensor_tensor(low_masked[:, k, :], low[:, group], y_ps[0:ER, k, 0:GT], ALU.mult
                                            ).then_inc(masked_ready, 1)
                for k, split in enumerate((low_first, low_change)):
                    dve.wait_ge(low_hi_ready, 2 * g + k + 1)
                    nc.vector.tensor_tensor(split[LOW_LO, group], low_masked[LOW_LO, k, :],
                                            split[LOW_LO, group].bitcast(F32), ALU.subtract).then_inc(low_lo_ready, 1)

            def body(g, first, last):
                for f in range(FC):
                    n = g * FC + f
                    since(dve, h_step, n * 3 - 3)
                    since(dve, first_ready, n + 1)
                    since(dve, change_done, n + 1)
                    if isinstance(g, int) and n == 0:
                        dve.wait_ge(ratio_ready, 1 + G)
                    nc.vector.tensor_tensor(z_second[:, f % 2, :], z_first[:, f % 4, :], change_ps[:, f % 2, 0:GT], ALU.add
                                            ).then_inc(h_step, 1)
                    dve.wait_ge(h_step, n * 3 + 1)
                    nc.vector.scalar_tensor_tensor(z_second[:, f % 2, :], z_second[:, f % 2, :], 0.0, ratio_rows[:, bass.ds(g * GT, GT)],
                                                   ALU.max, ALU.mult).then_inc(h_step, 1)
                    dve.wait_ge(h_step, n * 3 + 2)
                    if f == 0:
                        since(dve, y_done, g * GB)
                    nc.vector.scalar_tensor_tensor(h[:, f, :], z_first[:, f % 4, :], 0.0, z_second[:, f % 2, :], ALU.max, ALU.add
                                                   ).then_inc(h_step, 1)
                for j in range(GB):
                    b = g * GB + j
                    dve.wait_ge(y_done, b + 1)
                    if j == 0:
                        since(dve, stored, g * 16)
                    nc.vector.scalar_tensor_tensor(result[:, j, :], y_ps[0:S, j % 2, 0:D], weight[:, bass.ds(b, 1)],
                                                   x[:, b, :], ALU.mult, ALU.add).then_inc(x_step, 1)
            over_steps(dve, body, G)

        @block.scalar
        def _(act):
            act.wait_ge(const_w, 80)
            nc.scalar.activation(low_b_r[:], low_b[:], ACT.Copy).then_inc(b_step, 1)
            for g in range(G):
                act.wait_ge(xT_done, g + 1)
                nc.scalar.activation(x1T[:, :, g * GT:(g + 1) * GT], (z_ps, change_ps)[g % 2][:, :, 0:GT], ACT.Copy
                                     ).then_inc(xT_ready, 1)
                act.wait_ge(gate_done, g + 1)
                nc.scalar.activation(low[:, g * GT:(g + 1) * GT], y_ps[0:ER, g % 2, 0:GT], ACT.Copy).then_inc(low_ready, 1)
            act.wait_ge(gate_step, G * GROUP_STEPS + 1)
            nc.scalar.activation(share[:], share[:], ACT.Exp).then_inc(exp_ready, 1)
            for g in range(G):
                for k, split in enumerate((low_first, low_change)):
                    act.wait_ge(masked_ready, 2 * g + k + 1)
                    nc.scalar.activation(split[:, g * GT:(g + 1) * GT], low_masked[:, k, :], ACT.Copy
                                         ).then_inc(low_hi_ready, 1)
                act.wait_ge(ratio_done, g + 1)
                nc.scalar.activation(ratio_rows[:, g * GT:(g + 1) * GT], ratio_ps[:, 0, 0:GT], ACT.Copy
                                     ).then_inc(ratio_ready, 1)

            def body(g, first, last):
                for f in range(FC):
                    n = g * FC + f
                    since(act, first_done, n + 1)
                    since(act, h_step, n * 3 - 9)
                    nc.scalar.activation(z_first[:, f % 4, :], z_ps[:, f % 2, 0:GT], ACT.Copy).then_inc(first_ready, 1)
            over_steps(act, body, G)

        @block.tensor
        def _(pe):
            for g in range(G):
                pe.wait_ge(x1_ready, (g + 1) * GB)
                if g >= 2:
                    pe.wait_ge(xT_ready, g - 1)
                for c in range(KC):
                    for j in range(GB):
                        done = nc.tensor.transpose((z_ps, change_ps)[g % 2][:, c, j * S:(j + 1) * S],
                                                   x1[:, g * GB + j, c * 128:(c + 1) * 128], ident[0:S, 0:S])
                done.then_inc(xT_done, 1)
                if g == 0:
                    pe.wait_ge(const_w, 80)
                pe.wait_ge(xT_ready, g + 1)
                if g >= 2:
                    pe.wait_ge(low_ready, g - 1)
                    pe.wait_ge(gate_step, (g - 2) * GROUP_STEPS + 1)
                for j in range(GB):
                    b = g * GB + j
                    for c in range(KC):
                        nc.tensor.matmul(gate_bank(g)[:, j, :], x1T[:, c, b * S:(b + 1) * S], wg[:, c, :],
                                         start=(c == 0), stop=(c == KC - 1))
                for c in range(KC):
                    done = nc.tensor.matmul(y_ps[0:ER, g % 2, 0:GT], low_a[:, c, :], x1T[:, c, g * GT:(g + 1) * GT],
                                            start=(c == 0), stop=(c == KC - 1))
                done.then_inc(gate_done, 1)
            def multiply_wide(g, f):
                for c in range(KC):
                    nc.tensor.matmul(z_ps[:, f % 2, 0:GT], wi[:, c, f * 128:(f + 1) * 128],
                                     x1T[:, c, bass.ds(g * GT, GT)], start=(c == 0), stop=False)

            pe.wait_ge(weight_w, 32)
            multiply_wide(0, 0)
            multiply_wide(0, 1)
            pe.wait_ge(gate_step, G * GROUP_STEPS + 4)
            pe.wait_ge(low_ready, G)
            for g in range(G):
                since(pe, masked_ready, 2 * g)
                for k in range(2):
                    for j in range(GB):
                        done = nc.tensor.transpose(y_ps[0:ER, k, j * S:(j + 1) * S],
                                                   one_hot[:, k, g * GB + j],
                                                   ident[0:S, 0:S])
                done.then_inc(one_hot_done, 1)
                if g == 0:
                    pe.wait_ge(ratio_ready, 1)
                else:
                    pe.wait_ge(ratio_ready, 1 + g)
                for j in range(GB):
                    done = nc.tensor.matmul(ratio_ps[:, 0, j * S:(j + 1) * S],
                                            ratio[:, g * GB + j:g * GB + j + 1].broadcast_to([S, 128]),
                                            ident[0:S, 0:S], start=True, stop=True)
                done.then_inc(ratio_done, 1)

            def multiply_low(g, f):
                nc.tensor.matmul(z_ps[:, f % 2, 0:GT], low_b_r[:, f * 128:(f + 1) * 128],
                                 low_first[:, bass.ds(g * GT, GT)], start=False, stop=True).then_inc(first_done, 1)

            def multiply_first(g, f):
                since(pe, first_ready, g * FC + f - 1)
                multiply_wide(g, f)
                multiply_low(g, f)

            def multiply_change(g, f):
                n = g * FC + f
                if isinstance(n, int):
                    since(pe, h_step, n * 3 - 5)
                else:
                    wait_apart(pe, h_step, n * 3 - 5, passed)
                nc.tensor.matmul(change_ps[:, f % 2, 0:GT], low_b_r[:, f * 128:(f + 1) * 128],
                                 low_change[:, bass.ds(g * GT, GT)], start=True, stop=True).then_inc(change_done, 1)

            def body(g, first, last):
                for f in range(FC):
                    multiply_change(g, f)
                    if f + 2 < FC:
                        multiply_first(g, f + 2)
                if not last:
                    multiply_first(g + 1, 0)
                    multiply_first(g + 1, 1)
                for j in range(GB):
                    b = g * GB + j
                    since(pe, x_step, b - 1)
                    for f in range(FC):
                        if j == 0:
                            pe.wait_ge(h_step, (g * FC + f) * 3 + 3)
                        done = nc.tensor.matmul(y_ps[0:S, j % 2, 0:D], h[:, f, j * S:(j + 1) * S], wo[:, f, :],
                                                start=(f == 0), stop=(f == FC - 1))
                    done.then_inc(y_done, 1)

            pe.wait_ge(low_lo_ready, 2 * G)
            pe.wait_ge(b_step, 2)
            multiply_low(0, 0)
            multiply_low(0, 1)
            over_steps(pe, body, G)


def program(nc, A, out):
    with ExitStack() as ctx:
        x = ctx.enter_context(nc.sbuf_tensor("x", [S, B, D], F32))
        A["sorted_x"] = nc.dram_tensor("sorted_x", ((SORTED_TILES + 1) * 128, D), F32, kind="Internal").ap()
        stats = ctx.enter_context(nc.sbuf_tensor("stats", [S, B, 6], F32))
        ident = ctx.enter_context(nc.sbuf_tensor("ident", [128, 128], F32))
        passed = ctx.enter_context(nc.semaphore("passed"))
        l0_attention(nc, x, stats, ident, passed, A)
        l0_cross_attention(nc, x, stats, ident, passed, A)
        l0_experts(nc, x, stats, ident, passed, A)
        l1_attention(nc, x, stats, ident, passed, A)
        l1_context_mix(nc, x, stats, ident, passed, A)
        l1_experts(nc, x, stats, ident, passed, A, out)


def constants():
    dim = 128
    pos = np.arange(S, dtype=np.float32)[:, None]
    inv_freq = np.exp(-np.log(np.float32(10000.0)) * (np.arange(0, dim, 2, dtype=np.float32) / np.float32(dim)))
    ang = (pos * inv_freq[None, :]).astype(np.float32)
    pe = np.zeros((S, dim), np.float32)
    pe[:, 0::2], pe[:, 1::2] = np.sin(ang), np.cos(ang)
    causal = np.where(np.tril(np.ones((S, S), bool)), np.float32(0), np.float32(NEG))
    return {"pos_q": pe.T, "pos_k": pe[0:1].T, "causal": causal, "ident": np.eye(128, dtype=np.float32),
            "before": np.triu(np.ones((S, S), np.float32), 1), "expert_no": np.arange(8, dtype=np.float32)[None],
            "heads": np.kron(np.eye(8, dtype=np.float32), np.full((16, 16), 0.25, np.float32)),
            "row_expert": low_rows(np.repeat(np.arange(4, dtype=np.float32), 4)[:, None] + 1).T - 1,
            "tile_no": np.arange(SORTED_TILES, dtype=np.float32)[None]}


def by_feature(*vectors):
    return np.stack(vectors).reshape(len(vectors), KC, 128).transpose(2, 0, 1)


def low_rows(a):
    rows = np.zeros((LOW_ROWS, *a.shape[1:]), a.dtype)
    for at in (0, 32, 64):
        rows[at:at + 16] = a
    return rows


def mask_words(mask):
    pad = [(0, 0)] * (mask.ndim - 1) + [(0, 4 * MASK_WORDS - N)]
    return np.pad(mask, pad).view(np.uint32)


def kernel(**inputs):
    from concourse import bacc
    from concourse.bass_utils import run_bass_kernel_spmd

    i = {k: np.asarray(v) for k, v in inputs.items()}
    arrays = {
        "x": i["x"],
        "l0a_wq": i["L0_attn_Wq"].T, "l0a_wk": i["L0_attn_Wk"].T, "l0a_wv": i["L0_attn_Wv"].T,
        "l0a_wo": i["L0_attn_Wo"].T,
        "l0x_wq": i["L0_xattn_Wq"], "l0x_wkv": i["L0_xattn_Wkv"], "l0x_wout": i["L0_xattn_Wout"],
        "l0x_affine": by_feature(i["L0_xattn_g1"], i["L0_xattn_b1"], i["L0_xattn_g2"], i["L0_xattn_b2"]),
        "ctx": i["ctx_1024"], "ctx_mask": mask_words(i["mask_BxS2_bk0"]),
        "l0f_w1": i["L0_ffn_W1"], "l0f_wr": i["L0_ffn_Wr"].T, "l0f_wo": i["L0_ffn_Wo"],
        "l0f_b1": i["L0_ffn_b1"].reshape(1, -1),
        "l0f_rows": np.stack([i["L0_ffn_bo"], i["L0_ffn_gamma"], i["L0_ffn_beta"]])[None],
        "l1a_wq": i["L1_attn_Wq"], "l1a_wk": np.concatenate([i["L1_attn_Wkv"][:, :64]] * 2, 1),
        "l1a_wv": i["L1_attn_Wkv"][:, 64:], "l1a_wo": i["L1_attn_Wo"], "l1a_gamma": by_feature(i["L1_attn_gamma"]),
        "l1x_wq": i["L1_xattn_wq_w"].T, "l1x_wo": i["L1_xattn_wo_w"].T,
        "l1x_wkv": np.concatenate([i["L1_xattn_wk_w"], i["L1_xattn_wv_w"]]).T,
        "l1x_q_bias": by_feature(i["L1_xattn_wq_b"]),
        "l1x_kv_bias": np.concatenate([i["L1_xattn_wk_b"], i["L1_xattn_wv_b"]])[None],
        "l1x_rows": np.stack([i["L1_xattn_wo_b"], i["L1_xattn_ln_g"], i["L1_xattn_ln_b"]])[None],
        "l1f_wi": i["L1_ffn_Wi"].T, "l1f_wo": i["L1_ffn_Wo"].T, "l1f_wg": i["L1_ffn_Wg"].T,
        "l1f_a": low_rows(i["L1_ffn_A"].reshape(16, D)).T,
        "l1f_b": low_rows(i["L1_ffn_B"].transpose(0, 2, 1).reshape(16, 1024)),
        "l1f_bg": i["L1_ffn_bg"][None],
        "ctxT": i["ctx_1024"].transpose(0, 2, 1), "score_mask": mask_words(i["mask_Bx1xSxS2_bf0"][:, 0]),
        **constants(),
    }
    arrays = {k: np.ascontiguousarray(v) for k, v in arrays.items()}
    nc = bacc.Bacc("TRN2", target_bir_lowering=False, num_devices=1)
    A = {k: nc.dram_tensor(f"in_{k}", v.shape, mybir.dt.from_np(v.dtype), kind="ExternalInput").ap()
         for k, v in arrays.items()}
    out = nc.dram_tensor("out", (B, S, D), F32, kind="ExternalOutput").ap()
    program(nc, A, out)
    r = run_bass_kernel_spmd(nc, [{f"in_{k}": v for k, v in arrays.items()}], core_ids=[0])
    return r.results[0]["out"]
```
